# Optimizing a Trainium2 kernel written in Bass

```python
import numpy as np
import jax
import jax.numpy as jnp

def _softmax(x, axis=-1):
    return jax.nn.softmax(x, axis=axis)

def _gelu(x):
    return jax.nn.gelu(x, approximate=True)

def _silu(x):
    return jax.nn.silu(x)

def _sigmoid(x):
    return jax.nn.sigmoid(x)

def _layernorm(x, axis=-1, eps=1e-05):
    m = jnp.mean(x, axis=axis, keepdims=True)
    v = jnp.var(x, axis=axis, keepdims=True)
    return (x - m) / jnp.sqrt(v + eps)

def _scatter_add(tgt, idx, src, axis=0):
    return tgt.at[idx].add(src)

def _segment_sum(src, seg, n):
    return jax.ops.segment_sum(src, seg, n)
kernel_name = 'mk_xattn_ffn_d4_seqx_r8_657b22'

def setup_inputs(seed: int=0):
    np.random.seed(seed)
    _w = jnp.asarray

    def _rec_inputs():
        import jax
        import jax.numpy as jnp
        _rk = jax.random.key(seed)
        x = 0.002226 + 0.9996 * jax.random.normal(jax.random.fold_in(_rk, 1), (4, 512, 128), jnp.float32)
        _lenS = 512 - jax.random.randint(jax.random.fold_in(_rk, 7), (4,), 0, max(1, 512 // 4) + 1, jnp.int32)
        _lenS2 = 77 - jax.random.randint(jax.random.fold_in(_rk, 8), (4,), 0, max(1, 77 // 4) + 1, jnp.int32)
        _ctx_1024P = jax.random.normal(jax.random.fold_in(_rk, 11), (4, 16, 128), jnp.float32)
        _ctx_1024c = jax.random.dirichlet(jax.random.fold_in(_rk, 511), 0.3 * jnp.ones((16,), jnp.float32), (4, 77))
        _ctx_1024t = jnp.einsum('bsk,bkd->bsd', _ctx_1024c, _ctx_1024P)
        _ctx_1024t = _ctx_1024t * jax.lax.rsqrt(jnp.mean(jnp.square(_ctx_1024t)) + 1e-12) * 0.953939
        ctx_1024 = -7.10856e-05 + 0.999911 * (_ctx_1024t + 0.3 * jax.random.normal(jax.random.fold_in(_rk, 611), (4, 77, 128), jnp.float32))
        _validS = jnp.arange(512)[None, :] < _lenS[:, None]
        _validS2 = jnp.arange(77)[None, :] < _lenS2[:, None]
        _causal = jnp.tril(jnp.ones((512, 512), dtype=bool))
        mask_BxS2_bk0 = jnp.logical_not(jnp.broadcast_to(_validS2[:, :], (4, 77)))
        mask_1x1xSxS2_fk1 = jnp.where(jnp.broadcast_to(_validS2[0:1, None, None, :], (1, 1, 512, 77)), 1.0, 0.0).astype(jnp.float32)
        return (x, ctx_1024, mask_BxS2_bk0, mask_1x1xSxS2_fk1)
    x, ctx_1024, mask_BxS2_bk0, mask_1x1xSxS2_fk1 = _rec_inputs()

    def _L0_xattn_setup():
        import jax, jax.numpy as jnp
        import numpy as np
        HEADS = 8
        DIM_HEAD = 64
        SCALE = DIM_HEAD ** (-0.5)
        LN_EPS = 1e-05
        NEG_INF = -1e+30

        def layernorm(x, gamma, beta):
            mu = jnp.mean(x, axis=-1, keepdims=True)
            var = jnp.var(x, axis=-1, keepdims=True)
            return (x - mu) * jax.lax.rsqrt(var + LN_EPS) * gamma + beta
        key = jax.random.key(seed)
        ks = jax.random.split(key, 8)
        b, f, n, d, inner = (8, 1024, 64, 128, HEADS * DIM_HEAD)
        x = jax.random.normal(ks[0], (b, f, d), dtype=jnp.float32)
        latents = jax.random.normal(ks[1], (b, n, d), dtype=jnp.float32)
        key_padding_mask = jax.random.randint(ks[2], (b, f), 0, 2) > 0
        s = 0.02
        return {'x': x, 'latents': latents, 'key_padding_mask': key_padding_mask, 'kv_gate': jnp.float32(-4.0), 'gamma_media': jnp.ones((d,), jnp.float32), 'beta_media': jnp.zeros((d,), jnp.float32), 'gamma_lat': jnp.ones((d,), jnp.float32), 'beta_lat': jnp.zeros((d,), jnp.float32), 'Wq': jax.random.normal(ks[3], (d, inner), jnp.float32) * s, 'Wk': jax.random.normal(ks[4], (d, inner), jnp.float32) * s, 'Wv': jax.random.normal(ks[5], (d, inner), jnp.float32) * s, 'Wout': jax.random.normal(ks[6], (inner, d), jnp.float32) * s}
    _L0_xattn_all = _L0_xattn_setup()
    _L0_xattn_in = {k: v for k, v in _L0_xattn_all.items() if k in ('kv_gate', 'gamma_media', 'beta_media', 'gamma_lat', 'beta_lat', 'Wq', 'Wk', 'Wv', 'Wout')}
    del _L0_xattn_all

    def _L0_ffn_setup():
        import jax, jax.numpy as jnp
        import numpy as np
        TOPK = 2
        CAPACITY_FACTOR = 1.0
        EPS = 1e-06
        B, S, D = (4, 512, 128)
        E = 8
        SUB_H = 256 // E
        key = jax.random.key(seed)
        ks = jax.random.split(key, 7)
        x = jax.random.normal(ks[0], (B, S, D), dtype=jnp.float32)
        w_gate_w = jax.random.normal(ks[1], (D, E), dtype=jnp.float32) * 0.02
        w_gate_b = jnp.zeros((E,), jnp.float32)
        W1 = jax.random.normal(ks[2], (E, D, SUB_H), dtype=jnp.float32) * 0.02
        b1 = jnp.zeros((E, SUB_H), jnp.float32)
        W2 = jax.random.normal(ks[3], (E, SUB_H, D), dtype=jnp.float32) * 0.02
        b2 = jnp.zeros((E, D), jnp.float32)
        return {'x': x, 'w_gate_w': w_gate_w, 'w_gate_b': w_gate_b, 'W1': W1, 'b1': b1, 'W2': W2, 'b2': b2}
    _L0_ffn_all = _L0_ffn_setup()
    _L0_ffn_in = {k: v for k, v in _L0_ffn_all.items() if k in ('w_gate_w', 'w_gate_b', 'W1', 'b1', 'W2', 'b2')}
    del _L0_ffn_all

    def _L1_xattn_setup():
        import jax, jax.numpy as jnp
        import numpy as np
        B, S, D, H = (4, 256, 128, 16)
        HD = D // H

        def _split_heads(x):
            b, s, _ = x.shape
            return x.reshape(b, s, H, HD).transpose(0, 2, 1, 3)
        key = jax.random.key(seed)
        ks = jax.random.split(key, 12)
        scale = 1.0 / np.sqrt(D)
        inp = {'q': jax.random.normal(ks[0], (B, S, D), jnp.float32), 'k': jax.random.normal(ks[1], (B, S, D), jnp.float32), 'v': jax.random.normal(ks[2], (B, S, D), jnp.float32), 'mask': jnp.triu(jnp.ones((S, S), jnp.float32), k=1)[None, None, :, :], 'Wq': jax.random.normal(ks[3], (D, D), jnp.float32) * scale, 'bq': jnp.zeros((D,), jnp.float32), 'Wk': jax.random.normal(ks[4], (D, D), jnp.float32) * scale, 'bk': jnp.zeros((D,), jnp.float32), 'Wv': jax.random.normal(ks[5], (D, D), jnp.float32) * scale, 'bv': jnp.zeros((D,), jnp.float32), 'Wo': jax.random.normal(ks[6], (D, D), jnp.float32) * scale, 'bo': jnp.zeros((D,), jnp.float32)}
        return inp
    _L1_xattn_all = _L1_xattn_setup()
    _L1_xattn_in = {k: v for k, v in _L1_xattn_all.items() if k in ('Wq', 'bq', 'Wk', 'bk', 'Wv', 'bv', 'Wo', 'bo')}
    del _L1_xattn_all

    def _L1_ffn_setup():
        import jax, jax.numpy as jnp
        import numpy as np
        N_EXPERTS = 8
        TOP_K = 2
        D_MODEL = 128
        HIDDEN = 512
        ROUTED_H = 128
        BATCH, SEQ = (2, 512)
        key = jax.random.key(seed)
        ks = jax.random.split(key, 8)
        std = 0.02
        return {'x': jax.random.normal(ks[0], (BATCH, SEQ, D_MODEL), dtype=jnp.float32), 'w12': std * jax.random.normal(ks[1], (N_EXPERTS, 2 * ROUTED_H, D_MODEL), dtype=jnp.float32), 'w3': std * jax.random.normal(ks[2], (N_EXPERTS, D_MODEL, ROUTED_H), dtype=jnp.float32), 'shared_w1': std * jax.random.normal(ks[3], (HIDDEN, D_MODEL), dtype=jnp.float32), 'shared_w2': std * jax.random.normal(ks[4], (HIDDEN, D_MODEL), dtype=jnp.float32), 'shared_w3': std * jax.random.normal(ks[5], (D_MODEL, HIDDEN), dtype=jnp.float32), 'router_w': std * jax.random.normal(ks[6], (N_EXPERTS, D_MODEL), dtype=jnp.float32), 'expert_bias': jnp.zeros((N_EXPERTS,), dtype=jnp.float32)}
    _L1_ffn_all = _L1_ffn_setup()
    _L1_ffn_in = {k: v for k, v in _L1_ffn_all.items() if k in ('w12', 'w3', 'shared_w1', 'shared_w2', 'shared_w3', 'router_w', 'expert_bias')}
    del _L1_ffn_all

    def _L2_xattn_setup():
        import jax, jax.numpy as jnp
        import numpy as np
        D_MODEL = 128
        N_HEADS = 16
        D_HEAD = D_MODEL // N_HEADS
        key = jax.random.key(seed)
        k1, k2, k3, k4, k5, k6 = jax.random.split(key, 6)
        B, Q, T = (4, 128, 512)
        s = 1.0 / np.sqrt(D_MODEL)
        return {'q_in': jax.random.normal(k1, (B, Q, D_MODEL), dtype=jnp.float32), 'kv_in': jax.random.normal(k2, (B, T, D_MODEL), dtype=jnp.float32), 'Wq': jax.random.normal(k3, (D_MODEL, D_MODEL), dtype=jnp.float32) * s, 'Wk': jax.random.normal(k4, (D_MODEL, D_MODEL), dtype=jnp.float32) * s, 'Wv': jax.random.normal(k5, (D_MODEL, D_MODEL), dtype=jnp.float32) * s, 'Wo': jax.random.normal(k6, (D_MODEL, D_MODEL), dtype=jnp.float32) * s}
    _L2_xattn_all = _L2_xattn_setup()
    _L2_xattn_in = {k: v for k, v in _L2_xattn_all.items() if k in ('Wq', 'Wk', 'Wv', 'Wo')}
    del _L2_xattn_all

    def _L2_ffn_setup():
        import jax, jax.numpy as jnp
        import numpy as np
        E = 8
        TOP_K = 2
        ROUTE_SCALE = 1.0
        ALPHA = 1.702
        LIMIT = 7.0
        D = 128
        F = 128
        B, S = (2, 128)

        def swiglu(h):
            g = jnp.minimum(h[..., ::2], LIMIT)
            l = jnp.clip(h[..., 1::2], -LIMIT, LIMIT)
            return g * jax.nn.sigmoid(ALPHA * g) * (l + 1.0)
        if __name__ == '__main__':
            out = reference(**setup_inputs())
            print(out.shape, out.dtype)
        key = jax.random.key(seed)
        ks = jax.random.split(key, 16)
        sd = 1.0 / np.sqrt(D)
        sf = 1.0 / np.sqrt(F)
        return {'x': jax.random.normal(ks[0], (B, S, D), jnp.float32), 'gate_w': jax.random.normal(ks[1], (E, D), jnp.float32) * sd, 'gate_b': jax.random.normal(ks[2], (E,), jnp.float32) * 0.01, 'w1': jax.random.normal(ks[3], (E, 2 * F, D), jnp.float32) * sd, 'b1': jax.random.normal(ks[4], (E, 2 * F), jnp.float32) * 0.01, 'w3': jax.random.normal(ks[5], (E, 2 * F, D), jnp.float32) * sd, 'b3': jax.random.normal(ks[6], (E, 2 * F), jnp.float32) * 0.01, 'w2': jax.random.normal(ks[7], (E, D, F), jnp.float32) * sf, 'b2': jax.random.normal(ks[8], (E, D), jnp.float32) * 0.01, 'sw1': jax.random.normal(ks[9], (2 * F, D), jnp.float32) * sd, 'sb1': jax.random.normal(ks[10], (2 * F,), jnp.float32) * 0.01, 'sw3': jax.random.normal(ks[11], (2 * F, D), jnp.float32) * sd, 'sb3': jax.random.normal(ks[12], (2 * F,), jnp.float32) * 0.01, 'sw2': jax.random.normal(ks[13], (D, F), jnp.float32) * sf, 'sb2': jax.random.normal(ks[14], (D,), jnp.float32) * 0.01}
    _L2_ffn_all = _L2_ffn_setup()
    _L2_ffn_in = {k: v for k, v in _L2_ffn_all.items() if k in ('gate_w', 'gate_b', 'w1', 'b1', 'w3', 'b3', 'w2', 'b2', 'sw1', 'sb1', 'sw3', 'sb3', 'sw2', 'sb2')}
    del _L2_ffn_all

    def _L3_xattn_setup():
        import jax, jax.numpy as jnp
        import numpy as np
        DIM = 128
        NUM_HEADS = 16
        DIM_HEAD = 64
        INNER = NUM_HEADS * DIM_HEAD
        SCALE = DIM_HEAD ** (-0.5)

        def _layernorm(x, gamma, beta, eps=1e-05):
            mu = jnp.mean(x, axis=-1, keepdims=True)
            var = jnp.mean(jnp.square(x - mu), axis=-1, keepdims=True)
            return (x - mu) * jax.lax.rsqrt(var + eps) * gamma + beta
        key = jax.random.key(seed)
        ks = jax.random.split(key, 8)
        B, SQ, SK = (2, 256, 512)
        x = jax.random.normal(ks[0], (B, SQ, DIM), dtype=jnp.float32)
        context = jax.random.normal(ks[1], (B, SK, DIM), dtype=jnp.float32)
        ln_gamma = jnp.ones((DIM,), jnp.float32)
        ln_beta = jnp.zeros((DIM,), jnp.float32)
        w_q = jax.random.normal(ks[2], (DIM, INNER), dtype=jnp.float32) / np.sqrt(DIM)
        w_kv = jax.random.normal(ks[3], (DIM, 2 * INNER), dtype=jnp.float32) / np.sqrt(DIM)
        w_out = jax.random.normal(ks[4], (INNER, DIM), dtype=jnp.float32) / np.sqrt(INNER)
        b_out = jnp.zeros((DIM,), jnp.float32)
        gate = jnp.array([0.5], jnp.float32)
        return {'x': x, 'context': context, 'ln_gamma': ln_gamma, 'ln_beta': ln_beta, 'w_q': w_q, 'w_kv': w_kv, 'w_out': w_out, 'b_out': b_out, 'gate': gate}
    _L3_xattn_all = _L3_xattn_setup()
    _L3_xattn_in = {k: v for k, v in _L3_xattn_all.items() if k in ('ln_gamma', 'ln_beta', 'w_q', 'w_kv', 'w_out', 'b_out', 'gate')}
    del _L3_xattn_all

    def _L3_ffn_setup():
        import jax, jax.numpy as jnp
        import numpy as np
        HIDDEN = 128
        NUM_EXPERTS = 16
        TOP_K = 6
        EPS = 1e-10
        key = jax.random.key(seed)
        k1, k2, k3, k4 = jax.random.split(key, 4)
        tokens = jax.random.normal(k1, (4, 256, HIDDEN), dtype=jnp.float32)
        bound = 1.0 / np.sqrt(HIDDEN)
        router_w = jax.random.uniform(k2, (NUM_EXPERTS, HIDDEN), jnp.float32, -bound, bound)
        router_b = jax.random.uniform(k3, (NUM_EXPERTS,), jnp.float32, -bound, bound)
        expert_w = jax.random.normal(k4, (NUM_EXPERTS, HIDDEN, HIDDEN), dtype=jnp.float32) / np.sqrt(HIDDEN)
        return {'tokens': tokens, 'router_w': router_w, 'router_b': router_b, 'expert_w': expert_w}
    _L3_ffn_all = _L3_ffn_setup()
    _L3_ffn_in = {k: v for k, v in _L3_ffn_all.items() if k in ('router_w', 'router_b', 'expert_w')}
    del _L3_ffn_all
    return {'x': x, 'ctx_1024': ctx_1024, 'mask_BxS2_bk0': mask_BxS2_bk0, 'mask_1x1xSxS2_fk1': mask_1x1xSxS2_fk1, 'L0_xattn_kv_gate': _L0_xattn_in['kv_gate'], 'L0_xattn_gamma_media': _L0_xattn_in['gamma_media'], 'L0_xattn_beta_media': _L0_xattn_in['beta_media'], 'L0_xattn_gamma_lat': _L0_xattn_in['gamma_lat'], 'L0_xattn_beta_lat': _L0_xattn_in['beta_lat'], 'L0_xattn_Wq': _L0_xattn_in['Wq'], 'L0_xattn_Wk': _L0_xattn_in['Wk'], 'L0_xattn_Wv': _L0_xattn_in['Wv'], 'L0_xattn_Wout': _L0_xattn_in['Wout'], 'L0_ffn_w_gate_w': _L0_ffn_in['w_gate_w'], 'L0_ffn_w_gate_b': _L0_ffn_in['w_gate_b'], 'L0_ffn_W1': _L0_ffn_in['W1'], 'L0_ffn_b1': _L0_ffn_in['b1'], 'L0_ffn_W2': _L0_ffn_in['W2'], 'L0_ffn_b2': _L0_ffn_in['b2'], 'L1_xattn_Wq': _L1_xattn_in['Wq'], 'L1_xattn_bq': _L1_xattn_in['bq'], 'L1_xattn_Wk': _L1_xattn_in['Wk'], 'L1_xattn_bk': _L1_xattn_in['bk'], 'L1_xattn_Wv': _L1_xattn_in['Wv'], 'L1_xattn_bv': _L1_xattn_in['bv'], 'L1_xattn_Wo': _L1_xattn_in['Wo'], 'L1_xattn_bo': _L1_xattn_in['bo'], 'L1_ffn_w12': _L1_ffn_in['w12'], 'L1_ffn_w3': _L1_ffn_in['w3'], 'L1_ffn_shared_w1': _L1_ffn_in['shared_w1'], 'L1_ffn_shared_w2': _L1_ffn_in['shared_w2'], 'L1_ffn_shared_w3': _L1_ffn_in['shared_w3'], 'L1_ffn_router_w': _L1_ffn_in['router_w'], 'L1_ffn_expert_bias': _L1_ffn_in['expert_bias'], 'L2_xattn_Wq': _L2_xattn_in['Wq'], 'L2_xattn_Wk': _L2_xattn_in['Wk'], 'L2_xattn_Wv': _L2_xattn_in['Wv'], 'L2_xattn_Wo': _L2_xattn_in['Wo'], 'L2_ffn_gate_w': _L2_ffn_in['gate_w'], 'L2_ffn_gate_b': _L2_ffn_in['gate_b'], 'L2_ffn_w1': _L2_ffn_in['w1'], 'L2_ffn_b1': _L2_ffn_in['b1'], 'L2_ffn_w3': _L2_ffn_in['w3'], 'L2_ffn_b3': _L2_ffn_in['b3'], 'L2_ffn_w2': _L2_ffn_in['w2'], 'L2_ffn_b2': _L2_ffn_in['b2'], 'L2_ffn_sw1': _L2_ffn_in['sw1'], 'L2_ffn_sb1': _L2_ffn_in['sb1'], 'L2_ffn_sw3': _L2_ffn_in['sw3'], 'L2_ffn_sb3': _L2_ffn_in['sb3'], 'L2_ffn_sw2': _L2_ffn_in['sw2'], 'L2_ffn_sb2': _L2_ffn_in['sb2'], 'L3_xattn_ln_gamma': _L3_xattn_in['ln_gamma'], 'L3_xattn_ln_beta': _L3_xattn_in['ln_beta'], 'L3_xattn_w_q': _L3_xattn_in['w_q'], 'L3_xattn_w_kv': _L3_xattn_in['w_kv'], 'L3_xattn_w_out': _L3_xattn_in['w_out'], 'L3_xattn_b_out': _L3_xattn_in['b_out'], 'L3_xattn_gate': _L3_xattn_in['gate'], 'L3_ffn_router_w': _L3_ffn_in['router_w'], 'L3_ffn_router_b': _L3_ffn_in['router_b'], 'L3_ffn_expert_w': _L3_ffn_in['expert_w']}

def reference(x, ctx_1024, mask_BxS2_bk0, mask_1x1xSxS2_fk1, L0_xattn_kv_gate, L0_xattn_gamma_media, L0_xattn_beta_media, L0_xattn_gamma_lat, L0_xattn_beta_lat, L0_xattn_Wq, L0_xattn_Wk, L0_xattn_Wv, L0_xattn_Wout, L0_ffn_w_gate_w, L0_ffn_w_gate_b, L0_ffn_W1, L0_ffn_b1, L0_ffn_W2, L0_ffn_b2, L1_xattn_Wq, L1_xattn_bq, L1_xattn_Wk, L1_xattn_bk, L1_xattn_Wv, L1_xattn_bv, L1_xattn_Wo, L1_xattn_bo, L1_ffn_w12, L1_ffn_w3, L1_ffn_shared_w1, L1_ffn_shared_w2, L1_ffn_shared_w3, L1_ffn_router_w, L1_ffn_expert_bias, L2_xattn_Wq, L2_xattn_Wk, L2_xattn_Wv, L2_xattn_Wo, L2_ffn_gate_w, L2_ffn_gate_b, L2_ffn_w1, L2_ffn_b1, L2_ffn_w3, L2_ffn_b3, L2_ffn_w2, L2_ffn_b2, L2_ffn_sw1, L2_ffn_sb1, L2_ffn_sw3, L2_ffn_sb3, L2_ffn_sw2, L2_ffn_sb2, L3_xattn_ln_gamma, L3_xattn_ln_beta, L3_xattn_w_q, L3_xattn_w_kv, L3_xattn_w_out, L3_xattn_b_out, L3_xattn_gate, L3_ffn_router_w, L3_ffn_router_b, L3_ffn_expert_w):
    import jax
    import jax.numpy as jnp

    def _L0_xattn_ref(x, latents, key_padding_mask, kv_gate, gamma_media, beta_media, gamma_lat, beta_lat, Wq, Wk, Wv, Wout):
        import jax, jax.numpy as jnp
        import numpy as np
        HEADS = 8
        DIM_HEAD = 64
        SCALE = DIM_HEAD ** (-0.5)
        LN_EPS = 1e-05
        NEG_INF = -1e+30

        def layernorm(x, gamma, beta):
            mu = jnp.mean(x, axis=-1, keepdims=True)
            var = jnp.var(x, axis=-1, keepdims=True)
            return (x - mu) * jax.lax.rsqrt(var + LN_EPS) * gamma + beta
        b, f, d = x.shape
        n = latents.shape[1]
        x = layernorm(x, gamma_media, beta_media)
        latents = layernorm(latents, gamma_lat, beta_lat)
        kv = jnp.concatenate((x, latents * kv_gate), axis=1)
        q = (latents @ Wq).reshape(b, n, HEADS, DIM_HEAD)
        k = (kv @ Wk).reshape(b, f + n, HEADS, DIM_HEAD)
        v = (kv @ Wv).reshape(b, f + n, HEADS, DIM_HEAD)
        sim = jnp.einsum('bqhd,bkhd->bhqk', q * SCALE, k)
        sim = sim - jax.lax.stop_gradient(jnp.max(sim, axis=-1, keepdims=True))
        valid_feat = ~key_padding_mask
        valid_full = jnp.concatenate((valid_feat, jnp.ones((b, n), dtype=bool)), axis=1)
        sim = jnp.where(valid_full[:, None, None, :], sim, NEG_INF)
        attn = jax.nn.softmax(sim, axis=-1)
        out = jnp.einsum('bhqk,bkhd->bqhd', attn, v).reshape(b, n, HEADS * DIM_HEAD)
        return out @ Wout

    def _L0_ffn_ref(x, w_gate_w, w_gate_b, W1, b1, W2, b2):
        import jax, jax.numpy as jnp
        import numpy as np
        TOPK = 2
        CAPACITY_FACTOR = 1.0
        EPS = 1e-06
        B, S, D = (4, 512, 128)
        E = 8
        SUB_H = 256 // E
        Bx, Sx, Dx = x.shape
        Ex = w_gate_b.shape[0]
        K = Sx // 2
        capacity = int(CAPACITY_FACTOR * Bx)
        gate_scores = jax.nn.softmax(x @ w_gate_w + w_gate_b, axis=-1)
        _, top_idx = jax.lax.top_k(gate_scores, TOPK)
        mask = jax.nn.one_hot(top_idx, Ex, dtype=gate_scores.dtype).sum(axis=-2)
        masked = gate_scores * mask
        denom = masked.sum(axis=0, keepdims=True) + EPS
        route = masked / denom * capacity
        route_eb = jnp.transpose(route, (2, 0, 1))
        _, seq_ids = jax.lax.top_k(route_eb, K)
        seq_ids = jnp.sort(seq_ids, axis=-1)
        xg = jax.vmap(lambda idx: jnp.take_along_axis(x, idx[..., None], axis=1))(seq_ids)
        h = jnp.einsum('ebkd,edh->ebkh', xg, W1) + b1[:, None, None, :]
        h = jax.nn.gelu(h, approximate=False)
        o = jnp.einsum('ebkh,ehd->ebkd', h, W2) + b2[:, None, None, :]
        flat_ids = (jnp.arange(Bx)[None, :, None] * Sx + seq_ids).reshape(-1)
        outs = jnp.zeros((Bx * Sx, Dx), x.dtype).at[flat_ids].add(o.reshape(-1, Dx))
        return outs.reshape(Bx, Sx, Dx)

    def _L1_xattn_ref(q, k, v, mask, Wq, bq, Wk, bk, Wv, bv, Wo, bo):
        import jax, jax.numpy as jnp
        import numpy as np
        B, S, D, H = (4, 256, 128, 16)
        HD = D // H

        def _split_heads(x):
            b, s, _ = x.shape
            return x.reshape(b, s, H, HD).transpose(0, 2, 1, 3)
        qh = _split_heads(q @ Wq.T + bq)
        kh = _split_heads(k @ Wk.T + bk)
        vh = _split_heads(v @ Wv.T + bv)
        logits = jnp.einsum('bhqd,bhkd->bhqk', qh, kh) / jnp.sqrt(jnp.float32(HD))
        logits = logits + mask * -1000000000.0
        weights = jax.nn.softmax(logits, axis=-1)
        attn = jnp.einsum('bhqk,bhkd->bhqd', weights, vh)
        attn = attn.transpose(0, 2, 1, 3).reshape(q.shape[0], -1, D)
        return attn @ Wo.T + bo

    def _L1_ffn_ref(x, w12, w3, shared_w1, shared_w2, shared_w3, router_w, expert_bias):
        import jax, jax.numpy as jnp
        import numpy as np
        N_EXPERTS = 8
        TOP_K = 2
        D_MODEL = 128
        HIDDEN = 512
        ROUTED_H = 128
        BATCH, SEQ = (2, 512)
        b, s, d = x.shape
        xf = x.reshape(-1, d)
        shared = jax.nn.silu(xf @ shared_w1.T) * (xf @ shared_w2.T) @ shared_w3.T
        scores = jax.nn.sigmoid(xf @ router_w.T)
        _, top_idx = jax.lax.top_k(scores + expert_bias, TOP_K)
        mask = jax.nn.one_hot(top_idx, N_EXPERTS, dtype=xf.dtype).sum(axis=-2)
        gates = scores * mask
        h12 = jnp.einsum('td,ehd->teh', xf, w12)
        h1, h2 = jnp.split(h12, 2, axis=-1)
        h = jax.nn.silu(h1) * h2 * gates[:, :, None]
        routed = jnp.einsum('teh,edh->td', h, w3)
        return (shared + routed).reshape(b, s, d)

    def _L2_xattn_ref(q_in, kv_in, Wq, Wk, Wv, Wo):
        import jax, jax.numpy as jnp
        import numpy as np
        D_MODEL = 128
        N_HEADS = 16
        D_HEAD = D_MODEL // N_HEADS
        B, Q, D = q_in.shape
        T = kv_in.shape[1]
        scale = D_HEAD ** (-0.5)
        q = (q_in @ Wq.T).reshape(B, Q, N_HEADS, D_HEAD)
        k = (kv_in @ Wk.T).reshape(B, T, N_HEADS, D_HEAD)
        v = (kv_in @ Wv.T).reshape(B, T, N_HEADS, D_HEAD)
        w = jnp.einsum('bqhd,bthd->bhqt', q, k) * scale
        w = jax.nn.softmax(w.astype(jnp.float32), axis=-1).astype(q.dtype)
        out = jnp.einsum('bhqt,bthd->bqhd', w, v).reshape(B, Q, D)
        return out @ Wo.T

    def _L2_ffn_ref(x, gate_w, gate_b, w1, b1, w3, b3, w2, b2, sw1, sb1, sw3, sb3, sw2, sb2):
        import jax, jax.numpy as jnp
        import numpy as np
        E = 8
        TOP_K = 2
        ROUTE_SCALE = 1.0
        ALPHA = 1.702
        LIMIT = 7.0
        D = 128
        F = 128
        B, S = (2, 128)

        def swiglu(h):
            g = jnp.minimum(h[..., ::2], LIMIT)
            l = jnp.clip(h[..., 1::2], -LIMIT, LIMIT)
            return g * jax.nn.sigmoid(ALPHA * g) * (l + 1.0)
        if __name__ == '__main__':
            out = reference(**setup_inputs())
            print(out.shape, out.dtype)
        inp_shape = x.shape
        xt = x.reshape(-1, D)
        logits = xt @ gate_w.T
        scores = jax.nn.softmax(logits.astype(jnp.float32), axis=-1)
        biased = scores + gate_b.astype(jnp.float32)
        idx = jax.lax.top_k(biased, TOP_K)[1]
        weights = (jnp.take_along_axis(scores, idx, axis=-1) * ROUTE_SCALE).astype(x.dtype)
        cw = jnp.sum(jax.nn.one_hot(idx, E, dtype=x.dtype) * weights[..., None], axis=1)
        h1 = jnp.einsum('td,efd->etf', xt, w1) + b1[:, None, :]
        h3 = jnp.einsum('td,efd->etf', xt, w3) + b3[:, None, :]
        a = swiglu(h1 * h3)
        y = jnp.einsum('etf,edf->etd', a, w2) + b2[:, None, :]
        routed = jnp.einsum('te,etd->td', cw, y)
        sh = swiglu((xt @ sw1.T + sb1) * (xt @ sw3.T + sb3))
        shared = sh @ sw2.T + sb2
        return (routed + shared).reshape(inp_shape)

    def _L3_xattn_ref(x, context, ln_gamma, ln_beta, w_q, w_kv, w_out, b_out, gate):
        import jax, jax.numpy as jnp
        import numpy as np
        DIM = 128
        NUM_HEADS = 16
        DIM_HEAD = 64
        INNER = NUM_HEADS * DIM_HEAD
        SCALE = DIM_HEAD ** (-0.5)

        def _layernorm(x, gamma, beta, eps=1e-05):
            mu = jnp.mean(x, axis=-1, keepdims=True)
            var = jnp.mean(jnp.square(x - mu), axis=-1, keepdims=True)
            return (x - mu) * jax.lax.rsqrt(var + eps) * gamma + beta
        B, SQ, _ = x.shape
        SK = context.shape[1]
        xn = _layernorm(x, ln_gamma, ln_beta)
        q = (xn @ w_q).reshape(B, SQ, NUM_HEADS, DIM_HEAD)
        kv = context @ w_kv
        k, v = jnp.split(kv, 2, axis=-1)
        k = k.reshape(B, SK, NUM_HEADS, DIM_HEAD)
        v = v.reshape(B, SK, NUM_HEADS, DIM_HEAD)
        scores = jnp.einsum('bqhd,bkhd->bhqk', q * SCALE, k)
        attn = jax.nn.softmax(scores, axis=-1)
        out = jnp.einsum('bhqk,bkhd->bqhd', attn, v).reshape(B, SQ, INNER)
        out = out @ w_out + b_out
        return out * jnp.tanh(gate[0])

    def _L3_ffn_ref(tokens, router_w, router_b, expert_w):
        import jax, jax.numpy as jnp
        import numpy as np
        HIDDEN = 128
        NUM_EXPERTS = 16
        TOP_K = 6
        EPS = 1e-10
        B, S, H = tokens.shape
        E = expert_w.shape[0]
        T = B * S
        logits = jnp.einsum('bsh,eh->bse', tokens, router_w) + router_b
        probs = jax.nn.softmax(logits, axis=-1)
        top_p, top_i = jax.lax.top_k(probs, TOP_K)
        top_p = top_p / (jnp.sum(top_p, axis=-1, keepdims=True) + EPS)
        x = tokens.reshape(T, H)
        flat_i = top_i.reshape(T, TOP_K)
        flat_p = top_p.reshape(T, TOP_K)
        gate = jnp.zeros((T, E), dtype=flat_p.dtype)
        gate = gate.at[jnp.arange(T)[:, None], flat_i].add(flat_p)
        acc = jnp.maximum(jnp.sum(gate, axis=-1), EPS)
        out = jnp.zeros_like(x)
        for e in range(E):
            out = out + x @ expert_w[e] * gate[:, e:e + 1]
        out = (out / acc[:, None]).reshape(B, S, H)
        out = out + EPS * jnp.sum(top_p, axis=-1, keepdims=True)
        return out
    x = x + _L0_xattn_ref(ctx_1024, _layernorm(x, axis=-1), mask_BxS2_bk0, L0_xattn_kv_gate, L0_xattn_gamma_media, L0_xattn_beta_media, L0_xattn_gamma_lat, L0_xattn_beta_lat, L0_xattn_Wq, L0_xattn_Wk, L0_xattn_Wv, L0_xattn_Wout)
    x = x + _L0_ffn_ref(_layernorm(x, axis=-1), L0_ffn_w_gate_w, L0_ffn_w_gate_b, L0_ffn_W1, L0_ffn_b1, L0_ffn_W2, L0_ffn_b2)
    x = x + _L1_xattn_ref(_layernorm(x, axis=-1), ctx_1024, ctx_1024, mask_1x1xSxS2_fk1, L1_xattn_Wq, L1_xattn_bq, L1_xattn_Wk, L1_xattn_bk, L1_xattn_Wv, L1_xattn_bv, L1_xattn_Wo, L1_xattn_bo)
    x = x + _L1_ffn_ref(_layernorm(x, axis=-1), L1_ffn_w12, L1_ffn_w3, L1_ffn_shared_w1, L1_ffn_shared_w2, L1_ffn_shared_w3, L1_ffn_router_w, L1_ffn_expert_bias)
    x = x + _L2_xattn_ref(_layernorm(x, axis=-1), ctx_1024, L2_xattn_Wq, L2_xattn_Wk, L2_xattn_Wv, L2_xattn_Wo)
    x = x + _L2_ffn_ref(_layernorm(x, axis=-1), L2_ffn_gate_w, L2_ffn_gate_b, L2_ffn_w1, L2_ffn_b1, L2_ffn_w3, L2_ffn_b3, L2_ffn_w2, L2_ffn_b2, L2_ffn_sw1, L2_ffn_sb1, L2_ffn_sw3, L2_ffn_sb3, L2_ffn_sw2, L2_ffn_sb2)
    x = x + _L3_xattn_ref(_layernorm(x, axis=-1), ctx_1024, L3_xattn_ln_gamma, L3_xattn_ln_beta, L3_xattn_w_q, L3_xattn_w_kv, L3_xattn_w_out, L3_xattn_b_out, L3_xattn_gate)
    x = x + _L3_ffn_ref(_layernorm(x, axis=-1), L3_ffn_router_w, L3_ffn_router_b, L3_ffn_expert_w)
    return x

_drawn_inputs = setup_inputs


def setup_inputs(seed=0):
    import zlib

    import numpy as np

    out = dict(_drawn_inputs(seed))
    spreads = {'L0_xattn_gamma_media': (1.0, 0.6),
     'L0_xattn_beta_media': (0.0, 0.8),
     'L0_xattn_gamma_lat': (1.0, 0.6),
     'L0_xattn_beta_lat': (0.0, 0.1),
     'L0_ffn_w_gate_b': (0.0, 0.1),
     'L0_ffn_b1': (0.0, 0.293),
     'L0_ffn_b2': (0.0, 0.1),
     'L1_xattn_bq': (0.0, 0.1),
     'L1_xattn_bk': (0.0, 0.8),
     'L1_xattn_bv': (0.0, 0.1),
     'L1_xattn_bo': (0.0, 0.1),
     'L1_ffn_expert_bias': (0.0, 0.619),
     'L3_xattn_ln_gamma': (1.0, 0.6),
     'L3_xattn_ln_beta': (0.0, 0.637),
     'L3_xattn_b_out': (0.0, 0.1)}
    factors = {'L1_ffn_w12': 4.64,
     'L1_ffn_w3': 4.685,
     'L1_ffn_shared_w3': 2.669,
     'L1_ffn_router_w': 6.544,
     'L2_ffn_b1': 7.681,
     'L2_ffn_b3': 8.0,
     'L2_ffn_b2': 8.0,
     'L2_ffn_sb1': 4.843,
     'L2_ffn_sb3': 4.982,
     'L2_ffn_sb2': 5.059}
    for name, (base, spread) in spreads.items():
        noise = np.random.default_rng([zlib.crc32(name.encode()), seed]).standard_normal(out[name].shape)
        drawn = base * np.exp(spread * noise) if base else spread * noise
        out[name] = jnp.asarray(drawn.astype(out[name].dtype))
    for name, factor in factors.items():
        out[name] = (out[name] * factor).astype(out[name].dtype)
    return out
```

```python
from contextlib import ExitStack

import concourse.bass as bass
from concourse import mybir

ALU = mybir.AluOpType
ACT = mybir.ActivationFunctionType
AX = mybir.AxisListType.X
F32 = mybir.dt.float32
BF16 = mybir.dt.bfloat16
I32 = mybir.dt.int32

B = 4
S = 512
QT = S // 128
D = 128
KC = 77
KA = B * KC
BANK = 512
ROWS = 81
LN_EPS = 1e-5
NEG = -1e9
NEG_INF = -1e30
KEEP = S // 2
BITS = 31

COLS = {}
_at = 0
for _n, _w in (("gamma_media", 1), ("beta_media", 1), ("gamma_lat", 1), ("beta_lat", 1), ("ln_gamma", 1), ("ln_beta", 1),
               ("kv_gate", 1), ("gate", 1), ("b1", 2), ("hb", 36)):
    COLS[_n] = (_at, _w)
    _at += _w
NCOLS = _at
ROWC = {}
_at = 0
for _n, _w in (("w_gate_b", 8), ("expert_bias", 8), ("gate_b", 8), ("router_b", 16), ("bo", 128), ("b_out", 128), ("bv", 128)):
    ROWC[_n] = (_at, _w)
    _at += _w
NROWC = _at
FW = {"f0": 8 + 256, "f1": 8 + 1024 + 2048, "f2": 8 + 9 * 512, "f3": 16 + 2048}
FOFF = {"f0": 0, "f1": FW["f0"], "f2": FW["f0"] + FW["f1"], "f3": FW["f0"] + FW["f1"] + FW["f2"]}
NFW = sum(FW.values())
STAGE = 1024
PW = {}
_at = 0
for _n, _w in (("wv0", 512), ("wv1", 128), ("wv2", 128), ("wv3", 1024), ("wo0", 512), ("wo1", 128), ("wo2", 128), ("wo3", 1024),
               ("w2_0", 256), ("sw3", 512), ("w3", 1024), ("w2_2", 1152)):
    PW[_n] = (_at, _w)
    _at += _w
NPW = _at


def build(nc, A, out, STAGES=8):
    with ExitStack() as ctx:
        def sb(name, shape, dt=F32):
            return ctx.enter_context(nc.sbuf_tensor(name, shape, dt))

        def sem(name):
            return ctx.enter_context(nc.semaphore(name))

        def sems(prefix, names):
            return {n: sem(prefix + n) for n in names.split()}

        x = sb("x", [128, B, QT, D])
        xn = sb("xn", [128, QT, D])
        xt = sb("xt", [128, S])
        xh = sb("xh", [128, B, S], BF16)
        xl = sb("xl", [128, B, S], BF16)
        stats = sb("stats", [128, QT, 6])
        mv = sb("mv", [128, QT, 2])
        veps = sb("veps", [128, QT])
        rstd = sb("rstd", [128, QT])
        mhalf = sb("mhalf", [128, QT])
        epst = sb("epst", [128, QT])
        tick = sb("tick", [128, 1])
        identf = sb("identf", [128, 128])
        identb = sb("identb", [128, 128], BF16)
        ones = sb("ones", [ROWS, S], BF16)
        cols = sb("cols", [128, NCOLS])
        rowc = sb("rowc", [128, NROWC])
        pw = sb("pw", [128, NPW])
        fh = sb("fh", [128, NFW], BF16)
        fl = sb("fl", [128, NFW], BF16)
        ctxT = sb("ctxT", [128, KA])
        ch = sb("ch", [128, KA], BF16)
        cl = sb("cl", [128, KA], BF16)
        Gh = sb("Gh", [128, 16, 128], BF16)
        Gl = sb("Gl", [128, 16, 128], BF16)
        Mh = sb("Mh", [128, 16, KA], BF16)
        Ml = sb("Ml", [128, 16, KA], BF16)
        sel0 = sb("sel0", [ROWS, 16, 128], BF16)
        V = sb("V", [128, 4160])
        P4 = sb("P4", [128, 4, S])
        nm = sb("nm", [128, QT, ROWS + 15], BF16)
        nmT = sb("nmT", [ROWS, S], BF16)
        mx = sb("mx", [128, QT, 16])
        mr1 = sb("mr1", [128, QT, 16])
        mr2 = sb("mr2", [128, QT, 16])
        rec = sb("rec", [128, QT, 16])
        attn = sb("attn", [128, QT, 1024])
        gw = attn[0:64, :, :].rearrange("p q d -> p (q d)").rearrange("p (k h d) -> p k h d", k=2, h=16)
        aT = sb("aT", [128, 2, S])
        work = sb("work", [128, 12 * 512])

        ps = ctx.enter_context(nc.psum_tensor("ps", [128, 8 * BANK], F32))

        def bank(i, n=BANK, rows=128, off=0):
            return ps[0:rows, i * BANK + off:i * BANK + off + n]

        def col(name, i=0):
            return cols[:, COLS[name][0] + i:COLS[name][0] + i + 1]

        def rowv(name):
            return rowc[:, ROWC[name][0]:ROWC[name][0] + ROWC[name][1]]

        def pwv(name):
            return pw[:, PW[name][0]:PW[name][0] + PW[name][1]]

        kgf = work[:, 0:512]
        kgh = work[:, 512:768].bitcast(BF16)
        kgl = work[:, 768:1024].bitcast(BF16)
        MLh = work[:, 1024:3072].bitcast(BF16).rearrange("p (h k) -> p h k", h=8)
        MLl = work[:, 3072:5120].bitcast(BF16).rearrange("p (h k) -> p h k", h=8)
        negm = work[0:KC, 0:512]
        mres = work[0:KC, 512:1024]
        mpart = [work[0:KC, 1024 + 256 * i:1280 + 256 * i].bitcast(BF16) for i in range(3)]
        bqm = work[0:ROWS, 2048:2048 + 2464].bitcast(BF16).rearrange("p (h k) -> p h k", h=16)
        bqf = work[0:16, 4608:4608 + KA]
        bqh = work[0:16, 4920:4920 + KA]
        uw = work[:, 5232:5264]
        uws = work[:, 5264:5296]
        crow = sb("crow", [KC, B, D])
        cxf = sb("cxf", [128, KA])
        negk = sb("negk", [KC, B])
        negb = sb("negb", [KC, 1])
        negr = sb("negr", [1, KA], BF16)
        mk8 = sb("mk8", [KC, B], mybir.dt.uint8)
        mr8 = sb("mr8", [1, KA], mybir.dt.uint8)
        cst = sb("cst", [KC, B, 6])
        cmv = sb("cmv", [KC, B, 2])
        cve = sb("cve", [KC, B])
        crs = sb("crs", [KC, B])
        bkq = sb("bkq", [8, 2, 16])
        delta = sb("delta", [16, 16])
        b2c = sb("b2c", [9, 128])
        b2s = sb("b2s", [32, B, 128])
        tri = sb("tri", [128, 256])
        bits = sb("bits", [32, 32], I32)
        expd = sb("expd", [32, B, 2, 128], BF16)

        in_x = sem("in_x")
        in_c = sem("in_c")
        in_w = sem("in_w")
        in_mask = sem("in_mask")
        in_pw = sem("in_pw")
        out_s = sem("out_s")
        const = sem("const")
        N = sems("n_", "st var ep rstd xn tp xt xh xl st2 var2 ep2 rstd2 xn2")
        R = sems("p_", "gld gp gh gl mp mh ml vp ve vm")
        ATT = "mxp mx sT ex pv rc on res"
        Z = sems("z_", "nmc nm nmt nmT atp at op")
        done = sem("done")
        L = [sems(f"a{i}_", ATT) for i in range(4)]
        kq = sems("kq_", "kg kgh kgl nb")
        c0 = sems("c_", "st var ep rstd xn tp xt xh xl neg")
        m1 = sems("m_", "in_ chain up us bq bqc bqe")

        block = ctx.enter_context(nc.Block())
        end_of = {}

        DIM = [64, 8, 8, 64]
        NH = [8, 16, 16, 16]
        WV = [512, 128, 128, 1024]
        GB = [sum(NH[:l]) // 4 for l in range(4)]
        HB = [sum(NH[:l]) for l in range(4)]
        CB = [sum(B * NH[k] * DIM[k] // 128 for k in range(l)) for l in range(4)]
        VB = [sum(B * ((w + 511) // 512) for w in WV[:l]) for l in range(4)]
        SC = [0.125, 8 ** -0.5, 8 ** -0.5, 0.125]

        def dve_norm(dve, s, b, double=False):
            if s["first"] == 0:
                dve.wait_ge(in_x, 16)
            else:
                dve.wait_ge(done, s["first"] - B + b + 1)
            for j in range(QT):
                last = nc.vector.bn_stats(stats[:, j, :], x[:, b, j, :])
            last.then_inc(N["st"], 1)
            dve.wait_ge(N["st"], s["first"] + b + 1)
            nc.vector.memset(tick[:], 0.0)
            for j in range(QT):
                last = nc.vector.bn_aggr(mv[:, j, :], stats[:, j, :])
            last.then_inc(N["var"], 1)
            dve.wait_ge(N["rstd"], s["first"] + b + 1)
            for j in range(QT):
                last = nc.vector.tensor_scalar(xn[:, j, :], x[:, b, j, :], mv[:, j, 0:1], rstd[:, j:j + 1],
                                               ALU.subtract, ALU.mult)
            last.then_inc(N["xn"], 1)
            if double:
                dve.wait_ge(N["xn"], s["first"] + b + 1)
                for j in range(QT):
                    last = nc.vector.bn_stats(stats[:, j, :], xn[:, j, :])
                last.then_inc(N["st2"], 1)
                dve.wait_ge(N["st2"], s["first2"] + b + 1)
                nc.vector.memset(tick[:], 0.0)
                for j in range(QT):
                    last = nc.vector.bn_aggr(mv[:, j, :], stats[:, j, :])
                last.then_inc(N["var2"], 1)
                dve.wait_ge(N["rstd2"], s["first2"] + b + 1)
                for j in range(QT):
                    last = nc.vector.tensor_scalar(xn[:, j, :], xn[:, j, :], mv[:, j, 0:1], rstd[:, j:j + 1],
                                                   ALU.subtract, ALU.mult)
                last.then_inc(N["xn2"], 1)

        def pool_norm(pool, s, b, double=False):
            for var, ep, rs, n0 in ((N["var"], N["ep"], N["rstd"], s["first"]),) + (((N["var2"], N["ep2"], N["rstd2"], s["first2"]),) if double else ()):
                pool.wait_ge(var, n0 + b + 1)
                nc.gpsimd.tensor_tensor(veps[:], mv[:, :, 1], epst[:], ALU.add).then_inc(ep, 1)
                pool.wait_ge(ep, n0 + b + 1)
                nc.gpsimd.tensor_tensor(rstd[:], veps[:], mhalf[:], ALU.pow).then_inc(rs, 1)
            pool.wait_ge(N["xh"], s["first"] + b + 1)
            nc.gpsimd.tensor_tensor(xl[:, b, :], xt[:], xh[:, b, :], ALU.subtract).then_inc(N["xl"], 1)

        def pe_norm(pe, s, b, double=False):
            pe.wait_ge(N["xn2"] if double else N["xn"], (s["first2"] if double else s["first"]) + b + 1)
            for j in range(QT):
                last = nc.tensor.transpose(bank(7, 128, off=128 * j), xn[:, j, :], identf[:])
            last.then_inc(N["tp"], 1)

        def act_norm(act, s, b, gamma=None, beta=None):
            act.wait_ge(N["tp"], s["first"] + b + 1)
            if gamma:
                nc.scalar.activation(xt[:], bank(7), ACT.Identity, bias=col(beta), scale=col(gamma)).then_inc(N["xt"], 1)
            else:
                nc.scalar.activation(xt[:], bank(7), ACT.Copy).then_inc(N["xt"], 1)
            act.wait_ge(N["xt"], s["first"] + b + 1)
            nc.scalar.activation(xh[:, b, :], xt[:], ACT.Copy).then_inc(N["xh"], 1)

        def keys_parts(l):
            return (ch, cl) if l else (cxh, cxl)

        cxh = sb("cxh", [128, KA], BF16)
        cxl = sb("cxl", [128, KA], BF16)

        def v_steps(l):
            w = NH[l] * DIM[l]
            for b in range(B):
                for c in range(0, w, 512):
                    n = min(512, w - c)
                    hh = n // DIM[l]
                    d1 = DIM[l] + 1
                    o = (b * NH[l] + c // DIM[l]) * d1
                    yield b, c, n, V[0:KC, o:o + hh * d1].rearrange("p (h d) -> p h d", d=d1)[:, :, 0:DIM[l]]

        def sp_prep(sp, l):
            if l:
                sp.wait_ge(Z["atp"], CB[l])
            sp.dma_start(gw[0:DIM[l], :, 0:NH[l], :], A[f"g{l}"]).then_inc(R["gld"], 16)

        def pe_prep(pe, l):
            kh, kl = keys_parts(l)
            pe.wait_ge(R["gld"], 16 * (l + 1))
            J = DIM[l]
            if l == 1:
                pe.wait_ge(in_c, 16 * 11)
                for i in range(2):
                    for h in range(16):
                        last = nc.tensor.matmul(bank(7, 1, off=16 * i + h), gw[0:8, 1 - i, h, :], bkq[:, i, h:h + 1],
                                                start=True, stop=True)
                last.then_inc(m1["up"], 1)
            for g in range(NH[l] // 4):
                if g >= 2:
                    pe.wait_ge(R["gh"], GB[l] + g - 1)
                    pe.wait_ge(R["gl"], GB[l] + g - 1)
                for i in range(4):
                    h = 4 * g + i
                    last = nc.tensor.matmul(bank(g % 2, 128, off=128 * i), gw[0:J, 0, h, :], gw[0:J, 1, h, :],
                                            start=True, stop=True)
                last.then_inc(R["gp"], 1)
            if l == 0:
                pe.wait_ge(c0["xl"], 1)
            for h in range(NH[l]):
                if h % 4 == 0:
                    pe.wait_ge(R["gh"], GB[l] + h // 4 + 1)
                    pe.wait_ge(R["gl"], GB[l] + h // 4 + 1)
                if h >= 2:
                    pe.wait_ge(R["mh"], HB[l] + h - 1)
                    pe.wait_ge(R["ml"], HB[l] + h - 1)
                o = bank(2 + h % 2, KA)
                nc.tensor.matmul(o, Gh[:, h, :], kh[:], start=True, stop=False)
                nc.tensor.matmul(o, Gh[:, h, :], kl[:], start=False, stop=False)
                nc.tensor.matmul(o, Gl[:, h, :], kh[:], start=False, stop=True).then_inc(R["mp"], 1)
            kf = ctxT if l else cxf
            pe.wait_ge(in_pw, 16)
            for n, (b, c, w, dst) in enumerate(v_steps(l)):
                if n >= 2:
                    pe.wait_ge(R["ve"], VB[l] + n - 1)
                wv = pwv(f"wv{l}")
                nc.tensor.matmul(bank(5 + n % 2, w, KC), kf[:, b * KC:(b + 1) * KC], wv[:, c:c + w],
                                 start=True, stop=True).then_inc(R["vp"], 1)
            if l == 1:
                pe.wait_ge(m1["us"], 2)
                nc.tensor.matmul(bank(7, KA, 16), uws[:, 16:32], ctxT[:], start=True, stop=True).then_inc(m1["bq"], 1)

        def act_prep(act, l):
            for g in range(NH[l] // 4):
                act.wait_ge(R["gp"], GB[l] + g + 1)
                nc.scalar.activation(Gh[:, 4 * g:4 * g + 4, :], bank(g % 2).rearrange("p (h d) -> p h d", h=4), ACT.Copy,
                                     scale=SC[l]).then_inc(R["gh"], 1)
            if l == 1:
                act.wait_ge(m1["us"], 1)
            for h in range(NH[l]):
                act.wait_ge(R["mp"], HB[l] + h + 1)
                if l == 1:
                    nc.scalar.activation(Mh[:, h, :], bank(2 + h % 2, KA), ACT.Identity, bias=uws[:, h:h + 1]).then_inc(R["mh"], 1)
                else:
                    nc.scalar.activation(Mh[:, h, :], bank(2 + h % 2, KA), ACT.Copy).then_inc(R["mh"], 1)
            if l != 1:
                act.wait_ge(R["vm"], l + 1)
                for n, (b, c, w, dst) in enumerate(v_steps(l)):
                    act.wait_ge(R["vp"], VB[l] + n + 1)
                    src = bank(5 + n % 2, w, KC).rearrange("p (h d) -> p h d", d=DIM[l])
                    nc.scalar.activation(dst, src, ACT.Copy).then_inc(R["ve"], 1)

        def dve_prep(dve, l):
            if l == 1:
                dve.wait_ge(m1["in_"], 16)
                n = 0
                nc.vector.tensor_scalar(negm, negm, NEG, None, ALU.mult).then_inc(m1["chain"], 1)
                src = negm
                for i in range(3):
                    n += 1
                    dve.wait_ge(m1["chain"], n)
                    nc.vector.tensor_copy(mpart[i], src).then_inc(m1["chain"], 1)
                    if i < 2:
                        n += 1
                        dve.wait_ge(m1["chain"], n)
                        nc.vector.tensor_tensor(mres, src, mpart[i], ALU.subtract).then_inc(m1["chain"], 1)
                        src = mres
                dve.wait_ge(m1["up"], 1)
                nc.vector.tensor_scalar(uws, bank(7, 32), SC[1], None, ALU.mult).then_inc(m1["us"], 1)
                nc.vector.memset(bqm, 0.0).then_inc(m1["us"], 1)
            for g in range(NH[l] // 4):
                dve.wait_ge(R["gh"], GB[l] + g + 1)
                o = Gl[:, 4 * g:4 * g + 4, :].rearrange("p h d -> p (h d)")
                nc.vector.scalar_tensor_tensor(o, bank(g % 2), SC[l], Gh[:, 4 * g:4 * g + 4, :].rearrange("p h d -> p (h d)"),
                                               ALU.mult, ALU.subtract).then_inc(R["gl"], 1)
            if l == 1:
                dve.wait_ge(m1["us"], 1)
            for h in range(NH[l]):
                dve.wait_ge(R["mh"], HB[l] + h + 1)
                if l == 1:
                    nc.vector.scalar_tensor_tensor(Ml[:, h, :], bank(2 + h % 2, KA), uws[:, h:h + 1], Mh[:, h, :],
                                                   ALU.add, ALU.subtract).then_inc(R["ml"], 1)
                else:
                    nc.vector.tensor_tensor(Ml[:, h, :], bank(2 + h % 2, KA), Mh[:, h, :], ALU.subtract).then_inc(R["ml"], 1)
            if l == 1:
                dve.wait_ge(R["vm"], l + 1)
                for n, (b, c, w, dst) in enumerate(v_steps(l)):
                    dve.wait_ge(R["vp"], VB[l] + n + 1)
                    src = bank(5 + n % 2, w, KC).rearrange("p (h d) -> p h d", d=DIM[l])
                    nc.vector.tensor_tensor(dst, src, rowv("bv")[0:KC, :].rearrange("p (h d) -> p h d", d=DIM[l]),
                                            ALU.add).then_inc(R["ve"], 1)
                dve.wait_ge(m1["bq"], 1)
                bqc = cols16
                nc.vector.tensor_tensor(cols16, bkqT[:, 0:8], bkqT[:, 8:16], ALU.mult).then_inc(m1["bqc"], 1)
                dve.wait_ge(m1["bqc"], 1)
                nc.vector.tensor_reduce(bqs, cols16, AX, ALU.add).then_inc(m1["bqc"], 1)
                dve.wait_ge(m1["bqc"], 2)
                nc.vector.tensor_scalar(bqs, bqs, SC[1], None, ALU.mult).then_inc(m1["bqc"], 1)
                dve.wait_ge(m1["bqc"], 3)
                nc.vector.tensor_scalar(bqf, bank(7, KA, 16), bqs, None, ALU.add).then_inc(m1["bqc"], 1)
                dve.wait_ge(m1["bqc"], 4)
                nc.vector.tensor_copy(bqhb, bqf).then_inc(m1["bqc"], 1)
                dve.wait_ge(m1["bqc"], 5)
                nc.vector.tensor_tensor(bqf, bqf, bqhb, ALU.subtract).then_inc(m1["bqc"], 1)
                dve.wait_ge(m1["bqc"], 6)
                for i, p in enumerate((bqhb, bqf)):
                    o = bqm[32 * i:32 * i + 16, :, :]
                    last = nc.vector.tensor_tensor(o, p.unsqueeze(1).to_broadcast([16, 16, KA]),
                                                   delta[:, :].unsqueeze(2).to_broadcast([16, 16, KA]), ALU.mult)
                last.then_inc(m1["bqe"], 1)

        bkqT = sb("bkqT", [16, 16])
        cols16 = sb("cols16", [16, 8])[:, :]
        bqs = sb("bqs", [16, 1])[:, :]
        bqhb = bqh.bitcast(BF16)[:, 0:KA]

        def pool_prep(pool, l):
            if l:
                pool.wait_ge(L[l - 1]["pv"], B * (16 if l > 1 else 8 * 5))
            nc.gpsimd.memset(V[:], 1.0).then_inc(R["vm"], 1)

        GROUPS = [(0, 6), (6, 6), (12, 4)]

        def vslice(l, b, h):
            d1 = DIM[l] + 1
            return V[0:KC, bass.ds((b * 16 + h) * d1, d1)]

        def pe_attn(pe, l, b):
            s = L[l]
            pe_norm(pe, s, b, l == 3)
            pe.wait_ge(N["xh"], s["first"] + b + 1)
            for q in range(QT):
                xq = xh[:, b, 128 * q:128 * q + 128]
                for g, (h0, n) in enumerate(GROUPS):
                    if q:
                        pe.wait_ge(s["mx"], b * 12 + 3 * (q - 1) + g + 1)
                    o = bank(g, n * KC).rearrange("p (h k) -> p h k", h=n)
                    last = nc.tensor.matmul(o, xq, Mh[:, h0:h0 + n, bass.ds(b * KC, KC)], start=True, stop=l != 1)
                    if l == 1:
                        nc.tensor.matmul(o, ones[:, 0:128], bqm[:, h0:h0 + n, bass.ds(b * KC, KC)], start=False, stop=False)
                        for i in range(3):
                            last = nc.tensor.matmul(o, mpart[i][:, 128 * q:128 * q + 128],
                                                    identb[0:KC, 0:KC].unsqueeze(1).to_broadcast([KC, n, KC]),
                                                    start=False, stop=i == 2)
                    last.then_inc(s["mxp"], 1)
            pe_shift(pe, s, b)
            pe.wait_ge(N["xl"], s["first"] + b + 1)

            def scores(h):
                if h >= 2:
                    pe.wait_ge(s["ex"], b * 16 + h - 1)
                o = bank(3 + h % 2, S, KC)
                mh, ml = Mh[:, h, bass.ds(b * KC, KC)], Ml[:, h, bass.ds(b * KC, KC)]
                nc.tensor.matmul(o, mh, xh[:, b, :], start=True, stop=False)
                nc.tensor.matmul(o, mh, xl[:, b, :], start=False, stop=False)
                nc.tensor.matmul(o, ml, xh[:, b, :], start=False, stop=False)
                if l == 1:
                    nc.tensor.matmul(o, bqm[:, h, bass.ds(b * KC, KC)], ones[:], start=False, stop=False)
                    for i in range(3):
                        nc.tensor.matmul(o, identb[0:KC, 0:KC], mpart[i], start=False, stop=False)
                nc.tensor.matmul(o, sel0[:, h, 0:KC], nmT[:], start=False, stop=True).then_inc(s["sT"], 1)

            def values(h):
                pe.wait_ge(s["ex"], b * 16 + h + 1)
                d1 = DIM[l] + 1
                for q in range(QT):
                    if l == 3:
                        if h >= 2 and q == 0:
                            pe.wait_ge(s["on"], b * 16 + h - 1)
                        o = bank(5 + h % 2, d1, off=q * d1)
                    else:
                        o = bank(5 + q // 2, d1, off=(q % 2) * 16 * d1 + h * d1)
                    last = nc.tensor.matmul(o, P4[0:KC, h % 4, 128 * q:128 * q + 128], vslice(l, b, h), start=True, stop=True)
                last.then_inc(s["pv"], 1)

            scores(0)
            for h in range(16):
                if h < 15:
                    scores(h + 1)
                values(h)
            pe_out(pe, s, b, NH[l] * DIM[l] // 128, f"wo{l}", 16 if l == 3 else 2)

        def pe_shift(pe, s, b):
            pe.wait_ge(Z["nm"], s["zb"] + b + 1)
            pe.wait_ge(N["xt"], s["first"] + b + 1)
            o7 = bank(7, 256).bitcast(BF16)
            for q in range(QT):
                last = nc.tensor.transpose(o7[0:ROWS, 128 * q:128 * q + 128], nm[:, q, 0:ROWS], identb[:])
            last.then_inc(Z["nmt"], 1)
            pe.wait_ge(Z["nmT"], s["zb"] + b + 1)

        def pe_out(pe, s, b, nchunk, wo, n_on):
            pe.wait_ge(s["on"], b * n_on + n_on)
            for c in range(nchunk):
                if c >= 2:
                    pe.wait_ge(Z["at"], s["cb"] + b * nchunk + c - 1)
                for q in range(QT):
                    last = nc.tensor.transpose(bank(c % 2, 128, off=128 * q), attn[:, q, 128 * c:128 * c + 128], identf[:])
                last.then_inc(Z["atp"], 1)
                if c:
                    pe_out_chunk(pe, s, b, c - 1, nchunk, wo)
            pe_out_chunk(pe, s, b, nchunk - 1, nchunk, wo)

        def pe_out_chunk(pe, s, b, c, nchunk, wo):
            pe.wait_ge(Z["at"], s["cb"] + b * nchunk + c + 1)
            for q in range(QT):
                last = nc.tensor.matmul(bank(7, 128, off=128 * q), aT[:, c % 2, 128 * q:128 * q + 128],
                                        pwv(wo)[:, 128 * c:128 * c + 128], start=(c == 0 and q == 0),
                                        stop=(c == nchunk - 1), skip_group_check=True)
            last.then_inc(Z["op"], 1)

        def act_out(act, s, b, nchunk):
            for c in range(nchunk):
                act.wait_ge(Z["atp"], s["cb"] + b * nchunk + c + 1)
                if c >= 2:
                    act.wait_ge(Z["op"], s["cb"] + b * nchunk + c - 1)
                nc.scalar.activation(aT[:, c % 2, :], bank(c % 2), ACT.Copy).then_inc(Z["at"], 1)

        def act_attn(act, l, b):
            s = L[l]
            act_norm(act, s, b, *(("ln_gamma", "ln_beta") if l == 3 else ()))
            act_shift(act, s, b)
            for h in range(16):
                act.wait_ge(s["sT"], b * 16 + h + 1)
                if h >= 4:
                    act.wait_ge(s["pv"], b * 16 + h - 3)
                nc.scalar.activation(P4[0:KC, h % 4, :], bank(3 + h % 2, S, KC), ACT.Exp).then_inc(s["ex"], 1)
            act_out(act, s, b, NH[l] * DIM[l] // 128)

        def act_shift(act, s, b):
            act.wait_ge(Z["nmt"], s["zb"] + b + 1)
            nc.scalar.activation(nmT[:], bank(7, 256).bitcast(BF16)[0:ROWS, :], ACT.Copy).then_inc(Z["nmT"], 1)

        def dve_shift(dve, s, b, H):
            nc.vector.tensor_copy(nm[:, :, 0:H], mx[:, :, 0:H]).then_inc(Z["nmc"], 1)
            dve.wait_ge(Z["nmc"], (s["zb"] + b) * 4 + 1)
            nc.vector.tensor_tensor(mr1[:, :, 0:H], mx[:, :, 0:H], nm[:, :, 0:H], ALU.subtract).then_inc(Z["nmc"], 1)
            dve.wait_ge(Z["nmc"], (s["zb"] + b) * 4 + 2)
            nc.vector.tensor_copy(nm[:, :, 32:32 + H], mr1[:, :, 0:H]).then_inc(Z["nmc"], 1)
            dve.wait_ge(Z["nmc"], (s["zb"] + b) * 4 + 3)
            nc.vector.tensor_tensor(mr2[:, :, 0:H], mr1[:, :, 0:H], nm[:, :, 32:32 + H], ALU.subtract).then_inc(Z["nmc"], 1)
            dve.wait_ge(Z["nmc"], (s["zb"] + b) * 4 + 4)
            nc.vector.tensor_copy(nm[:, :, 64:64 + H], mr2[:, :, 0:H]).then_inc(Z["nm"], 1)

        def dve_attn(dve, l, b):
            s = L[l]
            dve_norm(dve, s, b, l == 3)
            for q in range(QT):
                for g, (h0, n) in enumerate(GROUPS):
                    dve.wait_ge(s["mxp"], b * 12 + 3 * q + g + 1)
                    last = nc.vector.tensor_reduce(mx[:, q, h0:h0 + n], bank(g, n * KC).rearrange("p (h k) -> p h k", h=n),
                                                   AX, ALU.max).then_inc(s["mx"], 1)
            dve.wait_ge(s["mx"], b * 12 + 12)
            dve_shift(dve, s, b, 16)
            if l == 3:
                for h in range(16):
                    dve_head(dve, s, b, h, 16, 1)
            else:
                dve.wait_ge(s["pv"], b * 16 + 16)
                for i in range(2):
                    o = bank(5 + i, 288).rearrange("p (q h d) -> p q h d", q=2, d=9)
                    nc.vector.reciprocal(rec[:, 2 * i:2 * i + 2, :], o[:, :, :, 8]).then_inc(s["rc"], 1)
                    dve.wait_ge(s["rc"], b * 2 + i + 1)
                    nc.vector.tensor_tensor(attn[:, 2 * i:2 * i + 2, 0:128].rearrange("p q (h d) -> p q h d", d=8),
                                            o[:, :, :, 0:8], rec[:, 2 * i:2 * i + 2, :].unsqueeze(3).to_broadcast([128, 2, 16, 8]),
                                            ALU.mult).then_inc(s["on"], 1)
            n = NH[l] * DIM[l] // 128
            dve.wait_ge(Z["op"], s["cb"] + b * n + n)
            dve_res(dve, l, s, b)

        def dve_head(dve, s, b, h, H, nc_):
            dve.wait_ge(s["pv"], (b * H + h + 1) * nc_)
            o = bank(5 + h % 2, QT * 65).rearrange("p (q d) -> p q d", d=65)
            nc.vector.reciprocal(rec[:, :, h], o[:, :, 64]).then_inc(s["rc"], 1)
            dve.wait_ge(s["rc"], b * H + h + 1)
            nc.vector.tensor_tensor(attn[:, :, 64 * h:64 * h + 64], o[:, :, 0:64],
                                    rec[:, :, h:h + 1].to_broadcast([128, QT, 64]), ALU.mult).then_inc(s["on"], 1)

        def dve_res(dve, l, s, b):
            xb = x[:, b, :, :].rearrange("p q d -> p (q d)")
            if l == 1:
                nc.vector.tensor_tensor(xb, bank(7), xb, ALU.add).then_inc(s["res"], 1)
                dve.wait_ge(s["res"], b + 1)
                nc.vector.tensor_tensor(x[:, b, :, :], x[:, b, :, :], rowv("bo").unsqueeze(1).to_broadcast([128, QT, D]),
                                        ALU.add).then_inc(done, 1)
            elif l == 3:
                nc.vector.scalar_tensor_tensor(xb, bank(7), tg[:, 0:1], xb, ALU.mult, ALU.add).then_inc(s["res"], 1)
                dve.wait_ge(s["res"], b + 1)
                nc.vector.tensor_tensor(x[:, b, :, :], x[:, b, :, :], btg[:].unsqueeze(1).to_broadcast([128, QT, D]),
                                        ALU.add).then_inc(done, 1)
            else:
                nc.vector.tensor_tensor(xb, bank(7), xb, ALU.add).then_inc(done, 1)

        tg = sb("tg", [128, 1])
        btg = sb("btg", [128, 128])
        tgs = sem("tgs")

        VL = V[:, 2080:4160].rearrange("p (c h d) -> p c h d", c=4, d=65)
        vl = sems("v_", "p e")
        kmp = sems("k_", "mp mh ml")

        def pe_attn0(pe, b):
            s = L[0]
            pe_norm(pe, s, b, True)
            pe.wait_ge(kq["kgl"], b + 1)
            for c in range(4):
                if c >= 2:
                    pe.wait_ge(vl["e"], b * 4 + c - 1)
                nc.tensor.matmul(bank(5 + c % 2), kgf[:, 128 * c:128 * c + 128], pwv("wv0"), start=True, stop=True).then_inc(vl["p"], 1)
            pe.wait_ge(N["xh"], s["first"] + b + 1)

            def keys(h):
                if h >= 1:
                    pe.wait_ge(kmp["ml"], b * 8 + h)
                nc.tensor.matmul(bank(4), Gh[:, h, :], kgh, start=True, stop=False)
                nc.tensor.matmul(bank(4), Gh[:, h, :], kgl, start=False, stop=False)
                nc.tensor.matmul(bank(4), Gl[:, h, :], kgh, start=False, stop=True).then_inc(kmp["mp"], 1)

            keys(0)
            for h in range(8):
                pe.wait_ge(kmp["mh"], b * 8 + h + 1)
                for q in range(QT):
                    n = 4 * h + q
                    if n >= 2:
                        pe.wait_ge(s["mx"], b * 32 + n - 1)
                    xq = xh[:, b, 128 * q:128 * q + 128]
                    nc.tensor.matmul(bank(2 * (n % 2)), xq, MLh[:, h, :], start=True, stop=True)
                    o = bank(2 * (n % 2) + 1, KC)
                    nc.tensor.matmul(o, xq, Mh[:, h, bass.ds(b * KC, KC)], start=True, stop=False)
                    nc.tensor.matmul(o, ones[0:1, 0:128], negr[:, bass.ds(b * KC, KC)], start=False, stop=True).then_inc(s["mxp"], 1)
                    if q == 1 and h < 7:
                        keys(h + 1)
            pe_shift(pe, s, b)
            pe.wait_ge(N["xl"], s["first"] + b + 1)
            pe.wait_ge(kmp["ml"], b * 8 + 8)

            def scores(n):
                h, c = divmod(n, 5)
                if n >= 2:
                    pe.wait_ge(s["ex"], b * 40 + n - 1)
                if c < 4:
                    o, mh, ml, w = bank(3 + n % 2), MLh[:, h, 128 * c:128 * c + 128], MLl[:, h, 128 * c:128 * c + 128], 128
                else:
                    o, w = bank(3 + n % 2, S, KC), KC
                    mh, ml = Mh[:, h, bass.ds(b * KC, KC)], Ml[:, h, bass.ds(b * KC, KC)]
                nc.tensor.matmul(o, mh, xh[:, b, :], start=True, stop=False)
                nc.tensor.matmul(o, mh, xl[:, b, :], start=False, stop=False)
                nc.tensor.matmul(o, ml, xh[:, b, :], start=False, stop=False)
                nc.tensor.matmul(o, sel0[:, h, 0:w], nmT[:], start=False, stop=True).then_inc(s["sT"], 1)

            def values(n):
                h, c = divmod(n, 5)
                pe.wait_ge(s["ex"], b * 40 + n + 1)
                if c == 0:
                    if h >= 2:
                        pe.wait_ge(s["on"], b * 8 + h - 1)
                    elif h == 0:
                        pe.wait_ge(vl["e"], b * 4 + 4)
                w = 128 if c < 4 else KC
                for q in range(QT):
                    v = VL[:, c, h, :] if c < 4 else V[0:KC, bass.ds((b * 8 + h) * 65, 65)]
                    last = nc.tensor.matmul(bank(5 + h % 2, 65, off=65 * q), P4[0:w, n % 4, 128 * q:128 * q + 128], v,
                                            start=(c == 0 and q == 0), stop=c == 4, skip_group_check=True)
                last.then_inc(s["pv"], 1)

            scores(0)
            for n in range(40):
                if n < 39:
                    scores(n + 1)
                values(n)
            pe_out(pe, s, b, 4, "wo0", 8)

        def act_attn0(act, b):
            s = L[0]
            act_norm(act, s, b, "gamma_lat", "beta_lat")
            nc.scalar.activation(kgf, xt[:], ACT.Copy, scale=col("kv_gate")).then_inc(kq["kg"], 1)
            act.wait_ge(kq["kg"], b + 1)
            nc.scalar.activation(kgh, kgf, ACT.Copy).then_inc(kq["kgh"], 1)
            for c in range(4):
                act.wait_ge(vl["p"], b * 4 + c + 1)
                nc.scalar.activation(VL[:, c, :, 0:64], bank(5 + c % 2).rearrange("p (h d) -> p h d", d=64), ACT.Copy).then_inc(vl["e"], 1)
            nc.scalar.activation(negb[:], negk[:, bass.ds(b, 1)], ACT.Copy).then_inc(kq["nb"], 1)
            for h in range(8):
                act.wait_ge(kmp["mp"], b * 8 + h + 1)
                nc.scalar.activation(MLh[:, h, :], bank(4), ACT.Copy).then_inc(kmp["mh"], 1)
            act_shift(act, s, b)
            act.wait_ge(kq["nb"], b + 1)
            for n in range(40):
                act.wait_ge(s["sT"], b * 40 + n + 1)
                if n >= 4:
                    act.wait_ge(s["pv"], b * 40 + n - 3)
                if n % 5 < 4:
                    nc.scalar.activation(P4[:, n % 4, :], bank(3 + n % 2), ACT.Exp).then_inc(s["ex"], 1)
                else:
                    nc.scalar.activation(P4[0:KC, n % 4, :], bank(3 + n % 2, S, KC), ACT.Exp,
                                         bias=negb[:]).then_inc(s["ex"], 1)
            act_out(act, s, b, 4)

        def dve_attn0(dve, b):
            s = L[0]
            dve_norm(dve, s, b, True)
            for h in range(8):
                dve.wait_ge(kmp["mh"], b * 8 + h + 1)
                nc.vector.tensor_tensor(MLl[:, h, :], bank(4), MLh[:, h, :], ALU.subtract).then_inc(kmp["ml"], 1)
                for q in range(QT):
                    n = 4 * h + q
                    dve.wait_ge(s["mxp"], b * 32 + n + 1)
                    o = ps[:, 1024 * (n % 2):1024 * (n % 2) + 512 + KC]
                    nc.vector.tensor_reduce(mx[:, q, h:h + 1], o, AX, ALU.max).then_inc(s["mx"], 1)
            dve.wait_ge(s["mx"], b * 32 + 32)
            dve_shift(dve, s, b, 8)
            for h in range(8):
                dve_head(dve, s, b, h, 8, 5)
            dve.wait_ge(Z["op"], s["cb"] + b * 4 + 4)
            dve_res(dve, 0, s, b)

        def pool_attn0(pool, b):
            s = L[0]
            pool_norm(pool, s, b, True)
            pool.wait_ge(kq["kgh"], b + 1)
            nc.gpsimd.tensor_tensor(kgl, kgf, kgh, ALU.subtract).then_inc(kq["kgl"], 1)

        FN = "c lg sp h yo "
        F = [sems(f"f{i}_", FN + more) for i, more in enumerate(("lgs g", "gt xo aa", "lgs gt xo aa t1 t2 bb cc dd ee ff", "lgs"))]
        for i in range(4):
            L[i].update(first=2 * i * B, first2=B if i == 3 else 0, zb=i * B, cb=CB[i])
            F[i].update(first=(2 * i + 1) * B)
        fsp = sems("fs_", "ld hi lo")
        EN = [8, 8, 8, 16]
        TOP = [2, 2, 2, 6]

        lg = sb("lg", [128, QT, 16])
        rsm = sb("rsm", [128, QT, 4])
        sc_ = sb("sc_", [128, QT, 16])
        sb_ = sb("sb_", [128, QT, 16])
        tri8 = sb("tri8", [128, 64])
        T1 = P4[:, 0, :].bitcast(BF16).rearrange("p (q e) -> p q e", q=QT)
        T2 = P4[:, 1, :].bitcast(BF16).rearrange("p (q e) -> p q e", q=QT)
        rank = sb("rank", [128, QT, 16])
        gates = sb("gates", [128, QT, 16])

        def fw(f, off, n, part=fh):
            return part[:, FOFF[f"f{f}"] + off:FOFF[f"f{f}"] + off + n]

        def pe_router(pe, f, b):
            s = F[f]
            E = EN[f]
            pe_norm(pe, s, b)
            pe.wait_ge(N["xl"], s["first"] + b + 1)
            for q in range(QT):
                o = bank(7, E, off=E * q)
                a, c = xh[:, b, 128 * q:128 * q + 128], xl[:, b, 128 * q:128 * q + 128]
                nc.tensor.matmul(o, a, fw(f, 0, E), start=True, stop=False)
                nc.tensor.matmul(o, a, fw(f, 0, E, fl), start=False, stop=False)
                last = nc.tensor.matmul(o, c, fw(f, 0, E), start=False, stop=True)
            last.then_inc(s["lg"], 1)

        def chainer(eng, sem_, b, per):
            n = [0]

            def link(ins):
                n[0] += 1
                ins.then_inc(sem_, 1)
                eng.wait_ge(sem_, b * per + n[0])
            return link, n

        def dve_rank(dve, link, f, score):
            E = EN[f]
            E2 = E * E
            t1 = T1[:, :, 0:E2].rearrange("p q (i j) -> p q i j", i=E)
            t2 = T2[:, :, 0:E2].rearrange("p q (i j) -> p q i j", i=E)
            for q in range(QT):
                sj = score[:, q, :].unsqueeze(1).to_broadcast([128, E, E])
                si = score[:, q, :].unsqueeze(2).to_broadcast([128, E, E])
                nc.vector.tensor_tensor(t1[:, q], sj, si, ALU.is_gt)
                last = nc.vector.tensor_tensor(t2[:, q], sj, si, ALU.is_equal)
            link(last)
            trv = (tri[:, 0:256] if E == 16 else tri8[:]).unsqueeze(1).to_broadcast([128, QT, E2])
            link(nc.vector.tensor_tensor(T2[:, :, 0:E2], T2[:, :, 0:E2], trv, ALU.mult))
            link(nc.vector.tensor_tensor(T1[:, :, 0:E2], T1[:, :, 0:E2], T2[:, :, 0:E2], ALU.add))
            for q in range(QT):
                last = nc.vector.tensor_reduce(rank[:, q, 0:E], t1[:, q], AX, ALU.add)
            link(last)
            link(nc.vector.tensor_scalar(rank[:, :, 0:E], rank[:, :, 0:E], float(TOP[f]), None, ALU.is_lt))

        def dve_logits(dve, link, f, b, bias):
            s = F[f]
            E = EN[f]
            dve.wait_ge(s["lg"], b + 1)
            src = bank(7, QT * E).rearrange("p (q e) -> p q e", e=E)
            if bias:
                link(nc.vector.tensor_tensor(lg[:, :, 0:E], src, rowv(bias).unsqueeze(1).to_broadcast([128, QT, E]), ALU.add))
            else:
                link(nc.vector.tensor_copy(lg[:, :, 0:E], src))

        def dve_softmax(dve, link, f, b):
            s = F[f]
            E = EN[f]
            link(nc.vector.tensor_reduce(rsm[:, :, 0:1], lg[:, :, 0:E], AX, ALU.max))
            link(nc.vector.tensor_tensor(lg[:, :, 0:E], lg[:, :, 0:E], rsm[:, :, 0:1].to_broadcast([128, QT, E]), ALU.subtract))
            nc.vector.memset(rsm[:, :, 3:4], 0.0).then_inc(s["lgs"], 1)
            dve.wait_ge(s["sp"], b + 1)
            link(nc.vector.tensor_reduce(rsm[:, :, 1:2], sc_[:, :, 0:E], AX, ALU.add))
            link(nc.vector.reciprocal(rsm[:, :, 2:3], rsm[:, :, 1:2]))
            link(nc.vector.tensor_tensor(sc_[:, :, 0:E], sc_[:, :, 0:E], rsm[:, :, 2:3].to_broadcast([128, QT, E]), ALU.mult))

        def act_exp_logits(act, f, b):
            s = F[f]
            act.wait_ge(s["lgs"], b + 1)
            nc.scalar.activation(sc_[:, :, 0:EN[f]], lg[:, :, 0:EN[f]], ACT.Exp).then_inc(s["sp"], 1)

        ms = sb("ms", [128, B, QT, 8])
        route = sb("route", [128, QT, 8])
        msr = P4[:, 3, 0:128].rearrange("p (q r) -> p q r", q=QT)
        G0 = work[:, 0:4096].rearrange("p (b g s) -> p b g s", b=B, g=2)
        RT = work[0:32, 4096:4608]
        junk = work[0:32, 4608:5120]
        hs0 = work[:, 5120:6144].rearrange("p (g s) -> p g s", g=2)
        selb = P4[0:32, 2, 0:256].bitcast(BF16)
        self_ = aT[0:32, 0, :]
        th = sb("th", [32, 8])
        r0 = sems("r0_", "rt rtt sel selm den rte ch lp end")
        r0d = sems("r0d_", "sb hs o")

        def pe_f0(pe):
            s = F[0]
            pe.wait_ge(fsp["hi"], 1)
            pe.wait_ge(fsp["lo"], 1)
            with pe.Fori(0, B) as b:
                pe_router(pe, 0, b)
                for g in range(2):
                    o = bank(g)
                    wh, wl = fw(0, 8 + 128 * g, 128), fw(0, 8 + 128 * g, 128, fl)
                    nc.tensor.matmul(o, wh, xh[:, b, :], start=True, stop=False)
                    nc.tensor.matmul(o, wh, xl[:, b, :], start=False, stop=False)
                    nc.tensor.matmul(o, wl, xh[:, b, :], start=False, stop=True).then_inc(s["h"], 1)
            for q in range(QT):
                pe.wait_ge(r0["rte"], q + 1)
                last = nc.tensor.transpose(bank(2, 128, 32, off=128 * q), msr[:, q, :], identf[:])
            last.then_inc(r0["rt"], 1)
            pe.wait_ge(r0["sel"], 1)
            pe.wait_ge(s["g"], 8)
            with pe.Fori(0, B) as b:
                for g in range(2):
                    nc.tensor.matmul(bank(g), expd[:, b, g, :], selb, start=True, stop=True).then_inc(r0d["sb"], 1)
                pe.wait_ge(r0d["hs"], 2 * b + 2)
                for q in range(QT):
                    o = bank(7, 128, off=128 * q)
                    for g in range(2):
                        nc.tensor.matmul(o, hs0[:, g, 128 * q:128 * q + 128], pwv("w2_0")[:, 128 * g:128 * g + 128],
                                         start=g == 0, stop=False)
                    last = nc.tensor.matmul(o, self_[:, 128 * q:128 * q + 128], b2s[:, b, :], start=False, stop=True)
                last.then_inc(r0d["o"], 1)
                pe.wait_ge(done, s["first"] + b + 1)


        def act_f0(act):
            s = F[0]
            with act.Fori(0, B) as b:
                act_norm(act, s, b)
                act_exp_logits(act, 0, b)
                for g in range(2):
                    act.wait_ge(s["h"], 2 * b + g + 1)
                    nc.scalar.activation(G0[:, b, g, :], bank(g), ACT.Gelu, bias=col("b1", g)).then_inc(s["g"], 1)

        def dve_f0(dve):
            s = F[0]
            with dve.Fori(0, B) as b:
                PER = 12
                link, n = chainer(dve, s["c"], b, PER)
                dve_norm(dve, s, b)
                dve_logits(dve, link, 0, b, "w_gate_b")
                dve_softmax(dve, link, 0, b)
                dve_rank(dve, link, 0, sc_[:, :, 0:8])
                link(nc.vector.tensor_tensor(ms[:, b, :, :], sc_[:, :, 0:8], rank[:, :, 0:8], ALU.mult))
                assert n[0] == PER, n[0]
            k = [0]

            def lk(ins):
                k[0] += 1
                ins.then_inc(r0["ch"], 1)
                dve.wait_ge(r0["ch"], k[0])
            lk(nc.vector.tensor_tensor(route[:], ms[:, 0], ms[:, 1], ALU.add))
            lk(nc.vector.tensor_tensor(route[:], route[:], ms[:, 2], ALU.add))
            lk(nc.vector.tensor_tensor(route[:], route[:], ms[:, 3], ALU.add))
            lk(nc.vector.tensor_scalar(route[:], route[:], 1e-6, None, ALU.add))
            lk(nc.vector.reciprocal(route[:], route[:]))
            for q in range(QT):
                o = msr[:, q, :].rearrange("p (b e) -> p b e", b=B)
                last = nc.vector.tensor_tensor(o, ms[:, :, q, :], route[:, q, :].unsqueeze(1).to_broadcast([128, B, 8]), ALU.mult)
                if q < QT - 1:
                    lk(last)
                else:
                    lk(last)
                k[0] += 1
                nc.vector.tensor_scalar(o, o, float(B), None, ALU.mult).then_inc(r0["ch"], 1)
                dve.wait_ge(r0["ch"], k[0])
                nc.vector.memset(th[:, 7:8], 0.0).then_inc(r0["rte"], 1)
            dve.wait_ge(r0["rt"], 1)
            lk(nc.vector.tensor_copy(RT, bank(2, S, 32)))
            lk(nc.vector.memset(th[:], 0.0))
            thi = th[:, :].bitcast(I32)
            dve.wait_ge(in_c, 16 * 11)
            with dve.Fori(0, BITS) as i:
                nc.vector.tensor_tensor(thi[:, 1:2], thi[:, 0:1], bits[:, bass.ds(i, 1)], ALU.bitwise_or).then_inc(r0["lp"], 1)
                dve.wait_ge(r0["lp"], i * 4 + 1)
                nc.vector.tensor_scalar(junk, RT, th[:, 1:2], None, ALU.is_ge, ALU.add, accum_out=th[:, 2:3]).then_inc(r0["lp"], 1)
                dve.wait_ge(r0["lp"], i * 4 + 2)
                nc.vector.tensor_scalar(th[:, 3:4], th[:, 2:3], float(KEEP), th[:, 1:2], ALU.is_ge, ALU.mult).then_inc(r0["lp"], 1)
                dve.wait_ge(r0["lp"], i * 4 + 3)
                nc.vector.tensor_tensor(th[:, 0:1], th[:, 0:1], th[:, 3:4], ALU.max).then_inc(r0["lp"], 1)
                dve.wait_ge(r0["lp"], i * 4 + 4)
            lk(nc.vector.tensor_scalar(self_, RT, th[:, 0:1], None, ALU.is_gt, ALU.add, accum_out=th[:, 4:5]))
            lk(nc.vector.tensor_scalar(th[:, 5:6], th[:, 4:5], -1.0, float(KEEP), ALU.mult, ALU.add))
            lk(nc.vector.tensor_scalar(RT, RT, th[:, 0:1], None, ALU.is_equal))
            lk(nc.vector.tensor_tensor_scan(junk, ones[0:32, :], RT, 0.0, ALU.mult, ALU.add))
            lk(nc.vector.scalar_tensor_tensor(junk, junk, th[:, 5:6], RT, ALU.is_le, ALU.mult))
            lk(nc.vector.tensor_tensor(self_, self_, junk, ALU.add))
            nc.vector.tensor_copy(selb, self_).then_inc(r0["sel"], 1)
            dve.wait_ge(s["g"], 8)
            with dve.Fori(0, B) as b:
                for g in range(2):
                    dve.wait_ge(r0d["sb"], 2 * b + g + 1)
                    nc.vector.tensor_tensor(hs0[:, g, :], G0[:, b, g, :], bank(g), ALU.mult).then_inc(r0d["hs"], 1)
                dve.wait_ge(r0d["o"], b + 1)
                xb = x[:, b, :, :].rearrange("p q d -> p (q d)")
                nc.vector.tensor_tensor(xb, bank(7), xb, ALU.add).then_inc(done, 1)

        hb = [work[:, 512 * i:512 * i + 512] for i in range(12)]

        def pe_hidden_free(pe, s, b, U, nprod, k):
            u = (k - 4) // nprod
            if nprod == 2:
                pe.wait_ge(s["aa"], b * U + u + 1)
            elif k % 4 < 2:
                pe.wait_ge(s["gt"], (b * U + u) * 2 + k % 4 + 1)
            else:
                pe.wait_ge(s["t2"], (b * U + u) * 2 + k % 4 - 1)

        def pe_units(pe, f, b, units, nprod, wdown, whid):
            s = F[f]
            U = len(units)

            def hidden(u):
                for i in range(nprod):
                    k = nprod * u + i
                    if k >= 4:
                        pe_hidden_free(pe, s, b, U, nprod, k)
                    wh, wl = whid(u, i, fh), whid(u, i, fl)
                    o = bank(k % 4)
                    nc.tensor.matmul(o, wh, xh[:, b, :], start=True, stop=False)
                    nc.tensor.matmul(o, wh, xl[:, b, :], start=False, stop=False)
                    nc.tensor.matmul(o, wl, xh[:, b, :], start=False, stop=True).then_inc(s["h"], 1)

            def down(u):
                pe.wait_ge(s["aa"], b * U + u + 1)
                if u >= 2:
                    pe.wait_ge(s["yo"], b * U + u - 1)
                for q in range(QT):
                    last = nc.tensor.matmul(bank(5 + u % 2, 128, off=128 * q), hb[8 + u % 2][:, 128 * q:128 * q + 128],
                                            wdown(u), start=True, stop=True)
                last.then_inc(s["xo"], 1)
            hidden(0)
            for u in range(U):
                if u + 1 < U:
                    hidden(u + 1)
                down(u)

        def dve_gated_add(dve, s, b, U, u, g):
            dve.wait_ge(s["xo"], b * U + u + 1)
            if u:
                dve.wait_ge(s["yo"], b * U + u)
            for q in range(QT):
                o = bank(5 + u % 2, 128, off=128 * q)
                xq = x[:, b, q, :]
                if g is None:
                    last = nc.vector.tensor_tensor(xq, o, xq, ALU.add)
                else:
                    last = nc.vector.scalar_tensor_tensor(xq, o, g(q), xq, ALU.mult, ALU.add)
            last.then_inc(s["yo"], 1)

        U1 = [("s", c) for c in range(4)] + [("e", e) for e in range(8)]

        def whid1(u, i, part):
            kind, n = U1[u]
            off = 8 + (512 * i + 128 * n if kind == "s" else 1024 + 256 * n + 128 * i)
            return fw(1, off, 128, part)

        def wdown1(u):
            kind, n = U1[u]
            return pwv("sw3" if kind == "s" else "w3")[:, 128 * n:128 * n + 128]

        def pe_f1(pe):
            with pe.Fori(0, B) as b:
                pe_router(pe, 1, b)
                pe_units(pe, 1, b, U1, 2, wdown1, whid1)
                pe.wait_ge(done, F[1]["first"] + b + 1)

        def act_f1(act):
            s = F[1]
            U = len(U1)
            with act.Fori(0, B) as b:
                act_norm(act, s, b)
                act.wait_ge(s["lg"], b + 1)
                nc.scalar.activation(sc_[:, :, 0:8], bank(7, 32).rearrange("p (q e) -> p q e", e=8), ACT.Sigmoid).then_inc(s["sp"], 1)
                for u in range(U):
                    act.wait_ge(s["h"], (b * U + u) * 2 + 1)
                    if u >= 2:
                        act.wait_ge(s["aa"], b * U + u - 1)
                    nc.scalar.activation(hb[u % 2], bank((2 * u) % 4), ACT.Silu).then_inc(s["gt"], 1)

        def dve_f1(dve):
            s = F[1]
            U = len(U1)
            with dve.Fori(0, B) as b:
                PER = 7
                link, n = chainer(dve, s["c"], b, PER)
                dve_norm(dve, s, b)
                dve.wait_ge(s["sp"], b + 1)
                link(nc.vector.tensor_tensor(sb_[:, :, 0:8], sc_[:, :, 0:8], rowv("expert_bias").unsqueeze(1).to_broadcast([128, QT, 8]), ALU.add))
                dve_rank(dve, link, 1, sb_[:, :, 0:8])
                link(nc.vector.tensor_tensor(gates[:, :, 0:8], sc_[:, :, 0:8], rank[:, :, 0:8], ALU.mult))
                assert n[0] == PER, n[0]

                def g_of(u):
                    kind, e = U1[u]
                    return None if kind == "s" else lambda q: gates[:, q, e:e + 1]
                for u in range(U):
                    dve.wait_ge(s["gt"], b * U + u + 1)
                    dve.wait_ge(s["h"], (b * U + u) * 2 + 2)
                    if u >= 2:
                        dve.wait_ge(s["xo"], b * U + u - 1)
                    nc.vector.tensor_tensor(hb[8 + u % 2], hb[u % 2], bank((2 * u + 1) % 4), ALU.mult).then_inc(s["aa"], 1)
                    if u:
                        dve_gated_add(dve, s, b, U, u - 1, g_of(u - 1))
                dve_gated_add(dve, s, b, U, U - 1, g_of(U - 1))
                dve.wait_ge(s["yo"], b * U + U)
                nc.vector.memset(rsm[:, :, 3:4], 0.0).then_inc(done, 1)

        U2 = 9
        cwx = sb("cwx", [128, QT, 9])
        cwT = P4[0:9, 3, :]

        def whid2(u, i, part):
            return fw(2, 8 + 512 * u + 128 * i, 128, part)

        def wdown2(u):
            return pwv("w2_2")[:, 128 * u:128 * u + 128]

        def pe_f2(pe):
            s = F[2]
            with pe.Fori(0, B) as b:
                pe_router(pe, 2, b)
                pe_units(pe, 2, b, list(range(U2)), 4, wdown2, whid2)
                pe.wait_ge(s["bb"], b + 1)
                for q in range(QT):
                    last = nc.tensor.transpose(bank(7, 128, 9, off=128 * q), cwx[:, q, :], identf[:])
                last.then_inc(s["cc"], 1)
                pe.wait_ge(s["dd"], b + 1)
                for q in range(QT):
                    last = nc.tensor.matmul(bank(4, 128, off=128 * q), cwT[:, 128 * q:128 * q + 128], b2c[:], start=True, stop=True)
                last.then_inc(s["ee"], 1)
                pe.wait_ge(done, s["first"] + b + 1)

        def act_f2(act):
            s = F[2]
            with act.Fori(0, B) as b:
                act_norm(act, s, b)
                act_exp_logits(act, 2, b)
                for u in range(U2):
                    for i in range(2):
                        act.wait_ge(s["h"], (b * U2 + u) * 4 + i + 1)
                        if u >= 2:
                            act.wait_ge(s["t2"], (b * U2 + u - 1) * 2)
                        nc.scalar.activation(hb[2 * (u % 2) + i], bank(i), ACT.Identity, bias=col("hb", 4 * u + i)).then_inc(s["gt"], 1)
                    act.wait_ge(s["t1"], b * U2 + u + 1)
                    nc.scalar.activation(hb[6], hb[4], ACT.Sigmoid, scale=1.702).then_inc(s["ff"], 1)
                act.wait_ge(s["cc"], b + 1)
                nc.scalar.activation(cwT, bank(7, S, 9), ACT.Copy).then_inc(s["dd"], 1)

        def dve_f2(dve):
            s = F[2]
            with dve.Fori(0, B) as b:
                PER = 13 + 9 * 4
                link, n = chainer(dve, s["c"], b, PER)
                dve_norm(dve, s, b)
                dve_logits(dve, link, 2, b, None)
                dve_softmax(dve, link, 2, b)
                link(nc.vector.tensor_tensor(sb_[:, :, 0:8], sc_[:, :, 0:8], rowv("gate_b").unsqueeze(1).to_broadcast([128, QT, 8]), ALU.add))
                dve_rank(dve, link, 2, sb_[:, :, 0:8])
                link(nc.vector.tensor_tensor(cwx[:, :, 0:8], sc_[:, :, 0:8], rank[:, :, 0:8], ALU.mult))
                nc.vector.memset(cwx[:, :, 8:9], 1.0).then_inc(s["bb"], 1)

                def g_of(u):
                    return None if u == 8 else lambda q: cwx[:, q, u:u + 1]
                for u in range(U2):
                    dve.wait_ge(s["gt"], (b * U2 + u) * 2 + 2)
                    for i in range(2):
                        dve.wait_ge(s["h"], (b * U2 + u) * 4 + 3 + i)
                        last = nc.vector.scalar_tensor_tensor(hb[4 + i], bank(2 + i), col("hb", 4 * u + 2 + i), hb[2 * (u % 2) + i],
                                                              ALU.add, ALU.mult).then_inc(s["t2"], 1)
                    dve.wait_ge(s["t2"], (b * U2 + u) * 2 + 2)
                    nc.vector.tensor_scalar(hb[4], hb[4], 7.0, None, ALU.min).then_inc(s["t1"], 1)
                    link(nc.vector.tensor_scalar(hb[5], hb[5], 7.0, -7.0, ALU.min, ALU.max))
                    link(nc.vector.tensor_scalar(hb[5], hb[5], 1.0, None, ALU.add))
                    link(nc.vector.tensor_tensor(hb[7], hb[5], hb[4], ALU.mult))
                    dve.wait_ge(s["ff"], b * U2 + u + 1)
                    if u >= 2:
                        dve.wait_ge(s["xo"], b * U2 + u - 1)
                    nc.vector.tensor_tensor(hb[8 + u % 2], hb[7], hb[6], ALU.mult).then_inc(s["aa"], 1)
                    link(nc.vector.memset(rsm[:, :, 3:4], 0.0))
                    if u:
                        dve_gated_add(dve, s, b, U2, u - 1, g_of(u - 1))
                dve_gated_add(dve, s, b, U2, U2 - 1, g_of(U2 - 1))
                assert n[0] == PER, n[0]
                dve.wait_ge(s["yo"], b * U2 + U2)
                dve.wait_ge(s["ee"], b + 1)
                xb = x[:, b, :, :].rearrange("p q d -> p (q d)")
                nc.vector.tensor_tensor(xb, bank(4), xb, ALU.add).then_inc(done, 1)

        def pe_f3(pe):
            s = F[3]
            with pe.Fori(0, B) as b:
                pe_router(pe, 3, b)
                for q in range(QT):
                    a, c = xh[:, b, 128 * q:128 * q + 128], xl[:, b, 128 * q:128 * q + 128]
                    for g in range(4):
                        n = 4 * q + g
                        if n >= 4:
                            pe.wait_ge(s["yo"], b * 16 + n - 3)
                        o = bank(n % 4)
                        nc.tensor.matmul(o, a, fw(3, 16 + 512 * g, 512), start=True, stop=False)
                        nc.tensor.matmul(o, a, fw(3, 16 + 512 * g, 512, fl), start=False, stop=False)
                        nc.tensor.matmul(o, c, fw(3, 16 + 512 * g, 512), start=False, stop=True).then_inc(s["h"], 1)
                pe.wait_ge(done, s["first"] + b + 1)

        def act_f3(act):
            with act.Fori(0, B) as b:
                act_norm(act, F[3], b)
                act_exp_logits(act, 3, b)

        def dve_f3(dve):
            s = F[3]
            with dve.Fori(0, B) as b:
                PER = 21 + 16 * 3
                link, n = chainer(dve, s["c"], b, PER)
                dve_norm(dve, s, b)
                dve_logits(dve, link, 3, b, "router_b")
                dve_softmax(dve, link, 3, b)
                dve_rank(dve, link, 3, sc_[:])
                link(nc.vector.tensor_tensor(gates[:], sc_[:], rank[:], ALU.mult))
                sm = rsm[:, :, 0:1]
                link(nc.vector.tensor_reduce(sm, gates[:], AX, ALU.add))
                link(nc.vector.tensor_scalar(sm, sm, 1e-10, None, ALU.add))
                link(nc.vector.reciprocal(sm, sm))
                link(nc.vector.tensor_tensor(gates[:], gates[:], sm.to_broadcast([128, QT, 16]), ALU.mult))
                link(nc.vector.tensor_reduce(rsm[:, :, 1:2], gates[:], AX, ALU.add))
                link(nc.vector.tensor_scalar(rsm[:, :, 2:3], rsm[:, :, 1:2], 1e-10, None, ALU.max))
                link(nc.vector.reciprocal(rsm[:, :, 2:3], rsm[:, :, 2:3]))
                link(nc.vector.tensor_tensor(gates[:], gates[:], rsm[:, :, 2:3].to_broadcast([128, QT, 16]), ALU.mult))
                link(nc.vector.tensor_scalar(rsm[:, :, 1:2], rsm[:, :, 1:2], 1e-10, None, ALU.mult))
                for q in range(QT):
                    for g in range(4):
                        dve.wait_ge(s["h"], b * 16 + 4 * q + g + 1)
                        for i in range(4):
                            e = 4 * g + i
                            add = nc.vector.scalar_tensor_tensor(x[:, b, q, :], bank(g, 128, off=128 * i), gates[:, q, e:e + 1],
                                                                 x[:, b, q, :], ALU.mult, ALU.add)
                            if i < 3:
                                link(add)
                        add.then_inc(s["yo"], 1)
                        dve.wait_ge(s["yo"], b * 16 + 4 * q + g + 1)
                assert n[0] == PER, n[0]
                nc.vector.tensor_tensor(x[:, b, :, :], x[:, b, :, :], rsm[:, :, 1:2].to_broadcast([128, QT, D]), ALU.add).then_inc(done, 1)

        order = [("a", 0), ("f", 0), ("a", 1), ("f", 1), ("a", 2), ("f", 2), ("a", 3), ("f", 3)][:STAGES]

        stage = work[:, 5120:6144]
        NST = (NFW + STAGE - 1) // STAGE

        @block.sync
        def _(sp):
            sp.dma_start(x[:], A["x"]).then_inc(in_x, 16)
            sp.dma_start(ctxT[:], A["ctxT"]).then_inc(in_c, 16)
            sp.dma_start(crow[:], A["ctxr"]).then_inc(in_c, 16)
            sp.dma_start(cols[:], A["cols"]).then_inc(in_c, 16)
            sp.dma_start(rowc[:], A["rowc"]).then_inc(in_c, 16)
            sp.dma_start(bkq[:], A["bkq"]).then_inc(in_c, 16)
            sp.dma_start(bkqT[:], A["bkqT"]).then_inc(in_c, 16)
            sp.dma_start(b2c[:], A["b2c"]).then_inc(in_c, 16)
            sp.dma_start(b2s[:], A["b2s"]).then_inc(in_c, 16)
            sp.dma_start(tri[:], A["tri"]).then_inc(in_c, 16)
            sp.dma_start(tri8[:], A["tri8"]).then_inc(in_c, 16)
            sp.dma_start(bits[:], A["bits"]).then_inc(in_c, 16)
            sp.dma_start(mk8[:], A["mk8"]).then_inc(in_mask, 16)
            sp.dma_start(mr8[:], A["mr8"]).then_inc(in_mask, 16)
            sp.dma_start(identf[:], A["identf"]).then_inc(in_w, 16)
            sp.dma_start(identb[:], A["identb"]).then_inc(in_w, 16)
            sp.dma_start(sel0[:], A["sel0"]).then_inc(in_w, 16)
            sp.dma_start(expd[:], A["expd"]).then_inc(in_w, 16)
            sp.dma_start(delta[:], A["delta"]).then_inc(in_w, 16)
            sp_prep(sp, 0)
            sp.dma_start(pw[:], A["pw"]).then_inc(in_pw, 16)
            for n in range((NFW + STAGE - 1) // STAGE):
                w = min(STAGE, NFW - n * STAGE)
                if n:
                    sp.wait_ge(fsp["lo"], n)
                sp.dma_start(stage[:, 0:w], A["fw"][:, n * STAGE:n * STAGE + w]).then_inc(fsp["ld"], 16)
            for l in range(1, 4):
                if ("a", l) in order:
                    sp_prep(sp, l)
                    if l == 1:
                        sp.wait_ge(done, 2 * B)
                        sp.dma_start(negm, A["maskT"]).then_inc(m1["in_"], 16)
            sp.wait_ge(done, B * len(order))
            sp.dma_start(out, x[:]).then_inc(out_s, 16)
            sp.wait_ge(out_s, 16)

        @block.gpsimd
        def _(pool):
            nc.gpsimd.memset(mhalf[:], -0.5).then_inc(const, 1)
            nc.gpsimd.memset(epst[:], LN_EPS).then_inc(const, 1)
            nc.gpsimd.memset(ones[:], 1.0).then_inc(const, 1)
            nc.gpsimd.memset(nm[:], 0.0).then_inc(const, 1)
            pool.wait_ge(const, 4)
            pool.wait_ge(c0["var"], 1)
            nc.gpsimd.tensor_scalar(cve[:], cmv[:, :, 1], LN_EPS, 1.0, ALU.add, ALU.mult).then_inc(c0["ep"], 1)
            pool.wait_ge(c0["ep"], 1)
            nc.gpsimd.tensor_tensor(crs[:], cve[:], mhalf[0:KC, :], ALU.pow).then_inc(c0["rstd"], 1)
            pool.wait_ge(c0["xh"], 2)
            nc.gpsimd.tensor_tensor(cxl[:], cxf[:], cxh[:], ALU.subtract).then_inc(c0["xl"], 1)
            nc.gpsimd.tensor_tensor(cl[:], ctxT[:], ch[:], ALU.subtract).then_inc(c0["xl"], 1)
            pool_prep(pool, 0)
            for n in range(NST):
                w = min(STAGE, NFW - n * STAGE)
                pool.wait_ge(fsp["hi"], n + 1)
                nc.gpsimd.tensor_tensor(fl[:, n * STAGE:n * STAGE + w], stage[:, 0:w], fh[:, n * STAGE:n * STAGE + w],
                                        ALU.subtract).then_inc(fsp["lo"], 1)
            for k, i in order:
                if k == "a" and i:
                    pool_prep(pool, i)
                with pool.Fori(0, B) as b:
                    if k == "a" and i == 0:
                        pool_attn0(pool, b)
                    elif k == "a":
                        pool_norm(pool, L[i], b, i == 3)
                    else:
                        pool_norm(pool, F[i], b)

        @block.scalar
        def _(act):
            act.wait_ge(in_c, 16 * 11)
            act.wait_ge(c0["neg"], 1)
            nc.scalar.activation(tg[:], col("gate"), ACT.Tanh).then_inc(tgs, 1)
            nc.scalar.activation(ch[:], ctxT[:], ACT.Copy).then_inc(c0["xh"], 1)
            act.wait_ge(c0["tp"], 1)
            nc.scalar.activation(cxf[:], bank(7, KA), ACT.Identity, bias=col("beta_media"), scale=col("gamma_media")).then_inc(c0["xt"], 1)
            act.wait_ge(c0["xt"], 1)
            nc.scalar.activation(cxh[:], cxf[:], ACT.Copy).then_inc(c0["xh"], 1)
            act_prep(act, 0)
            for n in range(NST):
                w = min(STAGE, NFW - n * STAGE)
                act.wait_ge(fsp["ld"], 16 * (n + 1))
                nc.scalar.activation(fh[:, n * STAGE:n * STAGE + w], stage[:, 0:w], ACT.Copy).then_inc(fsp["hi"], 1)
            for k, i in order:
                if k == "a":
                    if i:
                        act_prep(act, i)
                    with act.Fori(0, B) as b:
                        act_attn0(act, b) if i == 0 else act_attn(act, i, b)
                else:
                    (act_f0, act_f1, act_f2, act_f3)[i](act)

        @block.vector
        def _(dve):
            dve.wait_ge(in_c, 16 * 11)
            for b in range(B):
                last = nc.vector.bn_stats(cst[:, b, :], crow[:, b, :])
            last.then_inc(c0["st"], 1)
            dve.wait_ge(c0["st"], 1)
            for b in range(B):
                last = nc.vector.bn_aggr(cmv[:, b, :], cst[:, b, :])
            last.then_inc(c0["var"], 1)
            dve.wait_ge(in_mask, 32)
            nc.vector.tensor_scalar(negk[:], mk8[:], NEG_INF, None, ALU.mult)
            nc.vector.tensor_scalar(negr[:], mr8[:], NEG_INF, None, ALU.mult).then_inc(c0["neg"], 1)
            dve.wait_ge(c0["rstd"], 1)
            for b in range(B):
                last = nc.vector.tensor_scalar(crow[:, b, :], crow[:, b, :], cmv[:, b, 0:1], crs[:, b:b + 1], ALU.subtract, ALU.mult)
            last.then_inc(c0["xn"], 1)
            dve.wait_ge(tgs, 1)
            nc.vector.tensor_scalar(btg[:], rowv("b_out"), tg[:, 0:1], None, ALU.mult).then_inc(tgs, 1)
            dve_prep(dve, 0)
            for k, i in order:
                if k == "a":
                    if i:
                        dve_prep(dve, i)
                    with dve.Fori(0, B) as b:
                        dve_attn0(dve, b) if i == 0 else dve_attn(dve, i, b)
                else:
                    (dve_f0, dve_f1, dve_f2, dve_f3)[i](dve)

        @block.tensor
        def _(pe):
            pe.wait_ge(in_w, 16 * 5)
            pe.wait_ge(const, 4)
            pe.wait_ge(c0["xn"], 1)
            for b in range(B):
                last = nc.tensor.transpose(bank(7, KC, off=KC * b), crow[:, b, :], identf[0:KC, 0:KC])
            last.then_inc(c0["tp"], 1)
            pe_prep(pe, 0)
            for k, i in order:
                if k == "a":
                    if i:
                        pe_prep(pe, i)
                    if i == 1:
                        pe.wait_ge(m1["bqe"], 1)
                    with pe.Fori(0, B) as b:
                        pe_attn0(pe, b) if i == 0 else pe_attn(pe, i, b)
                else:
                    if i == 1:
                        pe.wait_ge(fsp["lo"], NST)
                    (pe_f0, pe_f1, pe_f2, pe_f3)[i](pe)


def layout(inputs):
    import numpy as np
    bf16 = mybir.dt.np(mybir.dt.bfloat16)
    I = {k: np.asarray(v) for k, v in inputs.items()}
    f = np.float32
    t = {}
    t["x"] = I["x"].reshape(B, QT, 128, D).transpose(2, 0, 1, 3)
    c = I["ctx_1024"]
    t["ctxT"] = c.reshape(KA, D).T
    t["ctxr"] = c.transpose(1, 0, 2)
    mask = I["mask_BxS2_bk0"]
    t["mk8"] = mask.T
    t["mr8"] = mask.reshape(1, KA)
    t["maskT"] = I["mask_1x1xSxS2_fk1"].reshape(S, KC).T

    def whole(v):
        return np.broadcast_to(v.reshape(1, -1), (128, v.size))

    def hidden2(v, sv):
        w = np.concatenate([v, sv[None]], 0)
        return w[:, 0::2].T, w[:, 1::2].T
    b1e, b1o = hidden2(I["L2_ffn_b1"], I["L2_ffn_sb1"])
    b3e, b3o = hidden2(I["L2_ffn_b3"], I["L2_ffn_sb3"])
    hb = np.stack([b1e, b1o, b3e, b3o], 2).reshape(128, 36)
    t["cols"] = np.concatenate([I["L0_xattn_gamma_media"][:, None], I["L0_xattn_beta_media"][:, None],
                                I["L0_xattn_gamma_lat"][:, None], I["L0_xattn_beta_lat"][:, None],
                                I["L3_xattn_ln_gamma"][:, None], I["L3_xattn_ln_beta"][:, None],
                                whole(I["L0_xattn_kv_gate"]), whole(I["L3_xattn_gate"]),
                                I["L0_ffn_b1"].reshape(2, 128).T, hb], 1)
    t["rowc"] = np.concatenate([whole(I[n]) for n in ("L0_ffn_w_gate_b", "L1_ffn_expert_bias", "L2_ffn_gate_b", "L3_ffn_router_b",
                                                      "L1_xattn_bo", "L3_xattn_b_out", "L1_xattn_bv")], 1)
    bk, bq = I["L1_xattn_bk"].reshape(16, 8), I["L1_xattn_bq"].reshape(16, 8)
    t["bkq"] = np.stack([bk.T, bq.T], 1)
    t["bkqT"] = np.concatenate([bk, bq], 1)
    t["b2c"] = np.concatenate([I["L2_ffn_b2"], I["L2_ffn_sb2"][None]], 0)
    z = np.zeros((B, 8, B, D), f)
    for b in range(B):
        z[b, :, b, :] = I["L0_ffn_b2"]
    t["b2s"] = z.reshape(32, B, D)

    def heads(wq, wk, n):
        return np.stack([wk.reshape(D, n, -1).transpose(2, 1, 0), wq.reshape(D, n, -1).transpose(2, 1, 0)], 1)
    wk3, wv3 = I["L3_xattn_w_kv"][:, :1024], I["L3_xattn_w_kv"][:, 1024:]
    t["g0"] = heads(I["L0_xattn_Wq"], I["L0_xattn_Wk"], 8)
    t["g1"] = heads(I["L1_xattn_Wq"].T, I["L1_xattn_Wk"].T, 16)
    t["g2"] = heads(I["L2_xattn_Wq"].T, I["L2_xattn_Wk"].T, 16)
    t["g3"] = heads(I["L3_xattn_w_q"], wk3, 16)

    def chunks(w):
        return w.reshape(-1, 128, w.shape[1]).transpose(1, 0, 2).reshape(128, -1)
    w22 = np.concatenate([I["L2_ffn_w2"], I["L2_ffn_sw2"][None]], 0)
    t["pw"] = np.concatenate([I["L0_xattn_Wv"], I["L1_xattn_Wv"].T, I["L2_xattn_Wv"].T, wv3,
                              chunks(I["L0_xattn_Wout"]), I["L1_xattn_Wo"].T, I["L2_xattn_Wo"].T, chunks(I["L3_xattn_w_out"]),
                              chunks(I["L0_ffn_W2"].reshape(256, D)), chunks(I["L1_ffn_shared_w3"].T),
                              I["L1_ffn_w3"].transpose(2, 0, 1).reshape(128, -1), w22.transpose(2, 0, 1).reshape(128, -1)], 1)
    w1 = np.concatenate([I["L2_ffn_w1"], I["L2_ffn_sw1"][None]], 0)
    w3 = np.concatenate([I["L2_ffn_w3"], I["L2_ffn_sw3"][None]], 0)
    f2 = np.stack([w1[:, 0::2], w1[:, 1::2], w3[:, 0::2], w3[:, 1::2]], 1)
    t["fw"] = np.concatenate([I["L0_ffn_w_gate_w"], I["L0_ffn_W1"].transpose(1, 0, 2).reshape(D, 256),
                              I["L1_ffn_router_w"].T, I["L1_ffn_shared_w1"].T, I["L1_ffn_shared_w2"].T,
                              I["L1_ffn_w12"].transpose(2, 0, 1).reshape(D, -1),
                              I["L2_ffn_gate_w"].T, f2.transpose(3, 0, 1, 2).reshape(D, -1),
                              I["L3_ffn_router_w"].T, I["L3_ffn_expert_w"].transpose(1, 0, 2).reshape(D, -1)], 1)
    t["identf"] = np.eye(128, dtype=f)
    t["identb"] = np.eye(128, dtype=bf16)
    s0 = np.zeros((ROWS, 16, 128), bf16)
    for h in range(16):
        for p in (0, 32, 64):
            s0[p + h, h, :] = -1.0
    t["sel0"] = s0
    ex = np.zeros((B, 8, B, 2, 128), bf16)
    for b in range(B):
        for e in range(8):
            ex[b, e, b, e // 4, 32 * (e % 4):32 * (e % 4) + 32] = 1.0
    t["expd"] = ex.reshape(32, B, 2, 128)
    t["delta"] = np.eye(16, dtype=f)
    t["tri"] = np.broadcast_to(np.tril(np.ones((16, 16), f), -1).reshape(1, 256), (128, 256))
    t["tri8"] = np.broadcast_to(np.tril(np.ones((8, 8), f), -1).reshape(1, 64), (128, 64))
    bits = np.zeros((32, 32), np.int32)
    for i in range(BITS):
        bits[:, i] = 1 << (BITS - 1 - i)
    t["bits"] = bits
    return {k: np.ascontiguousarray(v) for k, v in t.items()}


def kernel(**inputs):
    import numpy as np
    import concourse.bacc as bacc
    from concourse.bass_utils import run_bass_kernel_spmd

    nc = bacc.Bacc("TRN2", target_bir_lowering=False, num_devices=1)
    arrays = layout(inputs)
    feeds, aps = {}, {}
    for name, a in arrays.items():
        feeds[f"in_{name}"] = a
        aps[name] = nc.dram_tensor(f"in_{name}", a.shape, mybir.dt.from_np(a.dtype), kind="ExternalInput").ap()
    out = nc.dram_tensor("out_x", (128, B, QT, D), F32, kind="ExternalOutput").ap()
    build(nc, aps, out)
    r = run_bass_kernel_spmd(nc, [feeds], core_ids=[0])
    return np.ascontiguousarray(r.results[0]["out_x"].transpose(1, 2, 0, 3)).reshape(B, S, D)
```

```python
from contextlib import ExitStack

import concourse.bass as bass
from concourse import mybir

ALU = mybir.AluOpType
ACT = mybir.ActivationFunctionType
AX = mybir.AxisListType.X
F32 = mybir.dt.float32
BF16 = mybir.dt.bfloat16
I32 = mybir.dt.int32

B = 4
S = 512
QT = S // 128
D = 128
KC = 77
KA = B * KC
BANK = 512
ROWS = 81
LN_EPS = 1e-5
NEG = -1e9
NEG_INF = -1e30
KEEP = S // 2
BITS = 31

COLS = {}
_at = 0
for _n, _w in (("gamma_media", 1), ("beta_media", 1), ("gamma_lat", 1), ("beta_lat", 1), ("ln_gamma", 1), ("ln_beta", 1),
               ("kv_gate", 1), ("gate", 1), ("b1", 2), ("hb", 36)):
    COLS[_n] = (_at, _w)
    _at += _w
NCOLS = _at
ROWC = {}
_at = 0
for _n, _w in (("w_gate_b", 8), ("expert_bias", 8), ("gate_b", 8), ("router_b", 16), ("bo", 128), ("b_out", 128), ("bv", 128)):
    ROWC[_n] = (_at, _w)
    _at += _w
NROWC = _at
FW = {"f0": 8 + 256, "f1": 8 + 1024 + 2048, "f2": 8 + 9 * 512, "f3": 16 + 2048}
FOFF = {"f0": 0, "f1": FW["f0"], "f2": FW["f0"] + FW["f1"], "f3": FW["f0"] + FW["f1"] + FW["f2"]}
NFW = sum(FW.values())
STAGES_PER_BATCH = 3
STAGE = -(-NFW // (B * STAGES_PER_BATCH))
PW = {}
_at = 0
for _n, _w in (("wv0", 512), ("wv1", 128), ("wv2", 128), ("wv3", 1024), ("wo0", 512), ("wo1", 128), ("wo2", 128), ("wo3", 1024),
               ("w2_0", 256), ("sw3", 512), ("w3", 1024), ("w2_2", 1152)):
    PW[_n] = (_at, _w)
    _at += _w
NPW = _at


def build(nc, A, out, STAGES=8):
    with ExitStack() as ctx:
        def sb(name, shape, dt=F32):
            return ctx.enter_context(nc.sbuf_tensor(name, shape, dt))

        def sem(name):
            return ctx.enter_context(nc.semaphore(name))

        def sems(prefix, names):
            return {n: sem(prefix + n) for n in names.split()}

        x = sb("x", [128, B, QT, D])
        xn = sb("xn", [128, QT, D])
        xt = sb("xt", [128, S])
        xh = sb("xh", [128, B, S], BF16)
        xl = sb("xl", [128, B, S], BF16)
        stats = sb("stats", [128, QT, 6])
        mv = sb("mv", [128, QT, 2])
        veps = sb("veps", [128, QT])
        rstd = sb("rstd", [128, QT])
        mhalf = sb("mhalf", [128, QT])
        epst = sb("epst", [128, QT])
        tick = sb("tick", [128, 1])
        identf = sb("identf", [128, 128])
        identb = sb("identb", [128, 128], BF16)
        ones = sb("ones", [ROWS, S], BF16)
        cols = sb("cols", [128, NCOLS])
        rowc = sb("rowc", [128, NROWC])
        pw = sb("pw", [128, NPW])
        fh = sb("fh", [128, B * STAGES_PER_BATCH * STAGE], BF16)
        fl = sb("fl", [128, B * STAGES_PER_BATCH * STAGE], BF16)
        ctxT = sb("ctxT", [128, KA])
        ch = sb("ch", [128, KA], BF16)
        cl = sb("cl", [128, KA], BF16)
        Gh = sb("Gh", [128, 16, 128], BF16)
        Gl = sb("Gl", [128, 16, 128], BF16)
        Mh = sb("Mh", [128, 16, KA], BF16)
        Ml = sb("Ml", [128, 16, KA], BF16)
        sel0 = sb("sel0", [ROWS, 16], BF16)
        Vh = sb("Vh", [128, 4160], BF16)
        Vl = sb("Vl", [128, 4160], BF16)
        P4 = sb("P4", [128, 5, S])
        Pf = [P4[:, i, :] for i in range(2)]
        Ph = [P4[:, 2, 0:256].bitcast(BF16), P4[:, 2, 256:512].bitcast(BF16), P4[:, 3, 0:256].bitcast(BF16)]
        Pl = [P4[:, 3, 256:512].bitcast(BF16), P4[:, 4, 0:256].bitcast(BF16), P4[:, 4, 256:512].bitcast(BF16)]
        nm = sb("nm", [128, QT, ROWS + 15], BF16)
        nmT = sb("nmT", [ROWS, S], BF16)
        mx = sb("mx", [128, QT, 16])
        mr1 = sb("mr1", [128, QT, 16])
        mr2 = sb("mr2", [128, QT, 16])
        rec = sb("rec", [128, QT, 16])
        attn = sb("attn", [128, QT, 1024])
        gw = attn[0:64, :, :].rearrange("p q d -> p (q d)").rearrange("p (k h d) -> p k h d", k=2, h=16)
        aT = sb("aT", [128, 2, S])
        work = sb("work", [128, 12 * 512])

        ps = ctx.enter_context(nc.psum_tensor("ps", [128, 8 * BANK], F32))

        def bank(i, n=BANK, rows=128, off=0):
            return ps[0:rows, i * BANK + off:i * BANK + off + n]

        def col(name, i=0):
            return cols[:, COLS[name][0] + i:COLS[name][0] + i + 1]

        def rowv(name):
            return rowc[:, ROWC[name][0]:ROWC[name][0] + ROWC[name][1]]

        def pwv(name):
            return pw[:, PW[name][0]:PW[name][0] + PW[name][1]]

        kgf = work[:, 0:512]
        kgh = work[:, 512:768].bitcast(BF16)
        kgl = work[:, 768:1024].bitcast(BF16)
        MLh = work[:, 1024:3072].bitcast(BF16).rearrange("p (h k) -> p h k", h=8)
        MLl = work[:, 3072:5120].bitcast(BF16).rearrange("p (h k) -> p h k", h=8)
        negm = work[0:KC, 0:512]
        mres = work[0:KC, 512:1024]
        mpart = [work[0:KC, 1024 + 256 * i:1280 + 256 * i].bitcast(BF16) for i in range(3)]
        bqm = work[0:ROWS, 2048:2048 + 2464].bitcast(BF16).rearrange("p (h k) -> p h k", h=16)
        bqf = work[0:16, 4608:4608 + KA]
        bqh = work[0:16, 4920:4920 + KA]
        uw = work[:, 5232:5264]
        uws = work[:, 5264:5296]
        crow = sb("crow", [KC, B, D])
        cxf = sb("cxf", [128, KA])
        negk = sb("negk", [KC, B])
        negb = sb("negb", [KC, 1])
        negr = sb("negr", [1, KA], BF16)
        mk8 = sb("mk8", [KC, B], mybir.dt.uint8)
        mr8 = sb("mr8", [1, KA], mybir.dt.uint8)
        cst = sb("cst", [KC, B, 6])
        cmv = sb("cmv", [KC, B, 2])
        cve = sb("cve", [KC, B])
        crs = sb("crs", [KC, B])
        bkq = sb("bkq", [8, 2, 16])
        delta = sb("delta", [16, 16])
        b2c = sb("b2c", [9, 128])
        b2s = sb("b2s", [32, B, 128])
        tri = sb("tri", [128, 256])
        bits = sb("bits", [32, 32], I32)
        expd = sb("expd", [32, B, 2, 128], BF16)

        in_x = sem("in_x")
        in_c = sem("in_c")
        in_w = sem("in_w")
        in_mask = sem("in_mask")
        in_pw = sem("in_pw")
        out_s = sem("out_s")
        const = sem("const")
        N = sems("n_", "st var ep rstd xn tp xt xh xl st2 var2 ep2 rstd2 xn2")
        R = sems("p_", "gld gp gh gl mp mh ml vp ve vh vc vm")
        ATT = "mxp mx sT ex pl pv rc on res"
        Z = sems("z_", "nmc nm nmt nmT atp at op")
        done = sem("done")
        L = [sems(f"a{i}_", ATT) for i in range(4)]
        kq = sems("kq_", "kg kgh kgl nb")
        c0 = sems("c_", "st var ep rstd xn tp xt xh xl neg")
        m1 = sems("m_", "in_ chain up us bq bqc bqe")

        block = ctx.enter_context(nc.Block())
        order = [("a", 0), ("f", 0), ("a", 1), ("f", 1), ("a", 2), ("f", 2), ("a", 3), ("f", 3)][:STAGES]

        DIM = [64, 8, 8, 64]
        NH = [8, 16, 16, 16]
        WV = [512, 128, 128, 1024]
        GB = [sum(NH[:l]) // 4 for l in range(4)]
        HB = [sum(NH[:l]) for l in range(4)]
        CB = [sum(B * NH[k] * DIM[k] // 128 for k in range(l)) for l in range(4)]
        VB = [sum(B * ((w + 511) // 512) for w in WV[:l]) for l in range(4)]
        SC = [0.125, 8 ** -0.5, 8 ** -0.5, 0.125]

        def norm_of(i, b):
            return {"n": B * i + b, "n2": (B if i == 6 else 0) + b, "b": b, "i": i, "double": i in (0, 6),
                    "gamma": {0: "gamma_lat", 6: "ln_gamma"}.get(i), "beta": {0: "beta_lat", 6: "ln_beta"}.get(i)}

        def batches(eng, i, body):
            with eng.Fori(0, B - 1) as b:
                body(b, norm_of(i, b), norm_of(i, b + 1))
            body(B - 1, norm_of(i, B - 1), None if i in (1, len(order) - 1) else norm_of(i + 1, 0))

        def dve_stats(dve, m, second=False):
            st, var, n = (N["st2"], N["var2"], m["n2"]) if second else (N["st"], N["var"], m["n"])
            if second:
                dve.wait_ge(N["xn"], m["n"] + 1)
            elif m["i"] == 0:
                dve.wait_ge(in_x, 16)
            else:
                dve.wait_ge(done, m["n"] - B + 1)
            src = xn[:, :, :] if second else x[:, m["b"], :, :]
            for j in range(QT):
                last = nc.vector.bn_stats(stats[:, j, :], src[:, j, :])
            last.then_inc(st, 1)
            dve.wait_ge(st, n + 1)
            nc.vector.memset(tick[:], 0.0)
            for j in range(QT):
                last = nc.vector.bn_aggr(mv[:, j, :], stats[:, j, :])
            last.then_inc(var, 1)

        def dve_scale(dve, m, second=False):
            rs, out_, n = (N["rstd2"], N["xn2"], m["n2"]) if second else (N["rstd"], N["xn"], m["n"])
            dve.wait_ge(rs, n + 1)
            if not second and not (isinstance(m["n"], int) and m["n"] == 0):
                dve.wait_ge(N["tp"], m["n"])
            src = xn[:, :, :] if second else x[:, m["b"], :, :]
            for j in range(QT):
                last = nc.vector.tensor_scalar(xn[:, j, :], src[:, j, :], mv[:, j, 0:1], rstd[:, j:j + 1],
                                               ALU.subtract, ALU.mult)
            last.then_inc(out_, 1)

        def dve_norm(dve, m):
            dve_stats(dve, m)
            dve_scale(dve, m)
            if m["double"]:
                dve_stats(dve, m, True)
                dve_scale(dve, m, True)

        def pool_rstd(pool, m, second=False):
            var, ep, rs, n = (N["var2"], N["ep2"], N["rstd2"], m["n2"]) if second else (N["var"], N["ep"], N["rstd"], m["n"])
            pool.wait_ge(var, n + 1)
            nc.gpsimd.tensor_tensor(veps[:], mv[:, :, 1], epst[:], ALU.add).then_inc(ep, 1)
            pool.wait_ge(ep, n + 1)
            nc.gpsimd.tensor_tensor(rstd[:], veps[:], mhalf[:], ALU.pow).then_inc(rs, 1)

        def pool_low(pool, m):
            pool.wait_ge(N["xh"], m["n"] + 1)
            nc.gpsimd.tensor_tensor(xl[:, m["b"], :], xt[:], xh[:, m["b"], :], ALU.subtract).then_inc(N["xl"], 1)

        def pool_norm(pool, m):
            pool_rstd(pool, m)
            if m["double"]:
                pool_rstd(pool, m, True)
            pool_low(pool, m)

        def pe_norm(pe, m):
            pe.wait_ge(N["xn2"] if m["double"] else N["xn"], (m["n2"] if m["double"] else m["n"]) + 1)
            for j in range(QT):
                last = nc.tensor.transpose(bank(7, 128, off=128 * j), xn[:, j, :], identf[:])
            last.then_inc(N["tp"], 1)

        def act_norm(act, m):
            act.wait_ge(N["tp"], m["n"] + 1)
            if not (isinstance(m["n"], int) and m["n"] == 0):
                act.wait_ge(N["xl"], m["n"])
            if m["gamma"]:
                nc.scalar.activation(xt[:], bank(7), ACT.Identity, bias=col(m["beta"]), scale=col(m["gamma"])).then_inc(N["xt"], 1)
            else:
                nc.scalar.activation(xt[:], bank(7), ACT.Copy).then_inc(N["xt"], 1)
            act.wait_ge(N["xt"], m["n"] + 1)
            nc.scalar.activation(xh[:, m["b"], :], xt[:], ACT.Copy).then_inc(N["xh"], 1)

        def keys_parts(l):
            return (ch, cl) if l else (cxh, cxl)

        cxh = sb("cxh", [128, KA], BF16)
        cxl = sb("cxl", [128, KA], BF16)

        def v_steps(l):
            w = NH[l] * DIM[l]
            for b in range(B):
                for c in range(0, w, 512):
                    n = min(512, w - c)
                    hh = n // DIM[l]
                    d1 = DIM[l] + 1
                    o = (b * NH[l] + c // DIM[l]) * d1
                    yield b, c, n, [v[0:KC, o:o + hh * d1].rearrange("p (h d) -> p h d", d=d1)[:, :, 0:DIM[l]] for v in (Vh, Vl)]

        def sp_prep(sp, l):
            if l:
                sp.wait_ge(Z["atp"], CB[l])
            sp.dma_start(gw[0:DIM[l], :, 0:NH[l], :], A[f"g{l}"]).then_inc(R["gld"], 16)

        def pe_prep(pe, l):
            kh, kl = keys_parts(l)
            pe.wait_ge(R["gld"], 16 * (l + 1))
            J = DIM[l]
            if l == 1:
                pe.wait_ge(in_c, 16 * 11)
                for i in range(2):
                    for h in range(16):
                        last = nc.tensor.matmul(bank(7, 1, off=16 * i + h), gw[0:8, 1 - i, h, :], bkq[:, i, h:h + 1],
                                                start=True, stop=True)
                last.then_inc(m1["up"], 1)
            for g in range(NH[l] // 4):
                if g >= 2:
                    pe.wait_ge(R["gh"], GB[l] + g - 1)
                    pe.wait_ge(R["gl"], GB[l] + g - 1)
                for i in range(4):
                    h = 4 * g + i
                    last = nc.tensor.matmul(bank(g % 2, 128, off=128 * i), gw[0:J, 0, h, :], gw[0:J, 1, h, :],
                                            start=True, stop=True)
                last.then_inc(R["gp"], 1)
            if l == 0:
                pe.wait_ge(c0["xl"], 1)
            for h in range(NH[l]):
                if h % 4 == 0:
                    pe.wait_ge(R["gh"], GB[l] + h // 4 + 1)
                    pe.wait_ge(R["gl"], GB[l] + h // 4 + 1)
                if h >= 2:
                    pe.wait_ge(R["mh"], HB[l] + h - 1)
                    pe.wait_ge(R["ml"], HB[l] + h - 1)
                o = bank(2 + h % 2, KA)
                nc.tensor.matmul(o, Gh[:, h, :], kh[:], start=True, stop=False)
                nc.tensor.matmul(o, Gh[:, h, :], kl[:], start=False, stop=False)
                nc.tensor.matmul(o, Gl[:, h, :], kh[:], start=False, stop=True).then_inc(R["mp"], 1)
            kf = ctxT if l else cxf
            pe.wait_ge(in_pw, 16)
            for n, (b, c, w, dst) in enumerate(v_steps(l)):
                if n >= 2:
                    pe.wait_ge(R["ve"], VB[l] + n - 1)
                wv = pwv(f"wv{l}")
                nc.tensor.matmul(bank(5 + n % 2, w, KC), kf[:, b * KC:(b + 1) * KC], wv[:, c:c + w],
                                 start=True, stop=True).then_inc(R["vp"], 1)
            if l == 1:
                pe.wait_ge(m1["us"], 2)
                nc.tensor.matmul(bank(7, KA, 16), uws[:, 16:32], ctxT[:], start=True, stop=True).then_inc(m1["bq"], 1)

        def act_prep(act, l):
            for g in range(NH[l] // 4):
                act.wait_ge(R["gp"], GB[l] + g + 1)
                nc.scalar.activation(Gh[:, 4 * g:4 * g + 4, :], bank(g % 2).rearrange("p (h d) -> p h d", h=4), ACT.Copy,
                                     scale=SC[l]).then_inc(R["gh"], 1)
            if l == 1:
                act.wait_ge(m1["us"], 1)
            for h in range(NH[l]):
                act.wait_ge(R["mp"], HB[l] + h + 1)
                if l == 1:
                    nc.scalar.activation(Mh[:, h, :], bank(2 + h % 2, KA), ACT.Identity, bias=uws[:, h:h + 1]).then_inc(R["mh"], 1)
                else:
                    nc.scalar.activation(Mh[:, h, :], bank(2 + h % 2, KA), ACT.Copy).then_inc(R["mh"], 1)
            if l != 1:
                act.wait_ge(R["vm"], l + 1)
                for n, (b, c, w, dst) in enumerate(v_steps(l)):
                    act.wait_ge(R["vp"], VB[l] + n + 1)
                    src = bank(5 + n % 2, w, KC).rearrange("p (h d) -> p h d", d=DIM[l])
                    nc.scalar.activation(dst[0], src, ACT.Copy).then_inc(R["vh"], 1)

        def dve_prep(dve, l):
            if l == 1:
                dve.wait_ge(m1["in_"], 16)
                n = 0
                nc.vector.tensor_scalar(negm, negm, NEG, None, ALU.mult).then_inc(m1["chain"], 1)
                src = negm
                for i in range(3):
                    n += 1
                    dve.wait_ge(m1["chain"], n)
                    nc.vector.tensor_copy(mpart[i], src).then_inc(m1["chain"], 1)
                    if i < 2:
                        n += 1
                        dve.wait_ge(m1["chain"], n)
                        nc.vector.tensor_tensor(mres, src, mpart[i], ALU.subtract).then_inc(m1["chain"], 1)
                        src = mres
                dve.wait_ge(m1["up"], 1)
                nc.vector.tensor_scalar(uws, bank(7, 32), SC[1], None, ALU.mult).then_inc(m1["us"], 1)
                nc.vector.memset(bqm, 0.0).then_inc(m1["us"], 1)
            for g in range(NH[l] // 4):
                dve.wait_ge(R["gh"], GB[l] + g + 1)
                o = Gl[:, 4 * g:4 * g + 4, :].rearrange("p h d -> p (h d)")
                nc.vector.scalar_tensor_tensor(o, bank(g % 2), SC[l], Gh[:, 4 * g:4 * g + 4, :].rearrange("p h d -> p (h d)"),
                                               ALU.mult, ALU.subtract).then_inc(R["gl"], 1)
            if l == 1:
                dve.wait_ge(m1["us"], 1)
            for h in range(NH[l]):
                dve.wait_ge(R["mh"], HB[l] + h + 1)
                if l == 1:
                    nc.vector.scalar_tensor_tensor(Ml[:, h, :], bank(2 + h % 2, KA), uws[:, h:h + 1], Mh[:, h, :],
                                                   ALU.add, ALU.subtract).then_inc(R["ml"], 1)
                else:
                    nc.vector.tensor_tensor(Ml[:, h, :], bank(2 + h % 2, KA), Mh[:, h, :], ALU.subtract).then_inc(R["ml"], 1)
            dve.wait_ge(R["vm"], l + 1)
            for n, (b, c, w, dst) in enumerate(v_steps(l)):
                src = bank(5 + n % 2, w, KC).rearrange("p (h d) -> p h d", d=DIM[l])
                if l == 1:
                    dve.wait_ge(R["vp"], VB[l] + n + 1)
                    vf = aT[0:KC, 0, 128 * b:128 * b + 128].rearrange("p (h d) -> p h d", d=DIM[l])
                    nc.vector.tensor_tensor(vf, src, rowv("bv")[0:KC, :].rearrange("p (h d) -> p h d", d=DIM[l]),
                                            ALU.add).then_inc(R["vc"], 1)
                    dve.wait_ge(R["vc"], 2 * n + 1)
                    nc.vector.tensor_copy(dst[0], vf).then_inc(R["vc"], 1)
                    dve.wait_ge(R["vc"], 2 * n + 2)
                    nc.vector.tensor_tensor(dst[1], vf, dst[0], ALU.subtract).then_inc(R["ve"], 1)
                else:
                    dve.wait_ge(R["vh"], VB[l] - (VB[1 + 1] - VB[1] if l > 1 else 0) + n + 1)
                    nc.vector.tensor_tensor(dst[1], src, dst[0], ALU.subtract).then_inc(R["ve"], 1)
            if l == 1:
                dve.wait_ge(m1["bq"], 1)
                bqc = cols16
                nc.vector.tensor_tensor(cols16, bkqT[:, 0:8], bkqT[:, 8:16], ALU.mult).then_inc(m1["bqc"], 1)
                dve.wait_ge(m1["bqc"], 1)
                nc.vector.tensor_reduce(bqs, cols16, AX, ALU.add).then_inc(m1["bqc"], 1)
                dve.wait_ge(m1["bqc"], 2)
                nc.vector.tensor_scalar(bqs, bqs, SC[1], None, ALU.mult).then_inc(m1["bqc"], 1)
                dve.wait_ge(m1["bqc"], 3)
                nc.vector.tensor_scalar(bqf, bank(7, KA, 16), bqs, None, ALU.add).then_inc(m1["bqc"], 1)
                dve.wait_ge(m1["bqc"], 4)
                nc.vector.tensor_copy(bqhb, bqf).then_inc(m1["bqc"], 1)
                dve.wait_ge(m1["bqc"], 5)
                nc.vector.tensor_tensor(bqf, bqf, bqhb, ALU.subtract).then_inc(m1["bqc"], 1)
                dve.wait_ge(m1["bqc"], 6)
                for i, p in enumerate((bqhb, bqf)):
                    o = bqm[32 * i:32 * i + 16, :, :]
                    last = nc.vector.tensor_tensor(o, p.unsqueeze(1).to_broadcast([16, 16, KA]),
                                                   delta[:, :].unsqueeze(2).to_broadcast([16, 16, KA]), ALU.mult)
                last.then_inc(m1["bqe"], 1)

        bkqT = sb("bkqT", [16, 16])
        cols16 = sb("cols16", [16, 8])[:, :]
        bqs = sb("bqs", [16, 1])[:, :]
        bqhb = bqh.bitcast(BF16)[:, 0:KA]

        def pool_prep(pool, l):
            if l:
                pool.wait_ge(L[l - 1]["pv"], B * (16 if l > 1 else 8 * 5))
            nc.gpsimd.memset(Vl[:], 0.0)
            nc.gpsimd.memset(Vh[:], 1.0).then_inc(R["vm"], 1)

        GROUPS = [(0, 6), (6, 6), (12, 4)]

        def vslice(l, b, h):
            d1 = DIM[l] + 1
            return [v[0:KC, bass.ds((b * 16 + h) * d1, d1)] for v in (Vh, Vl)]

        def pe_attn(pe, l, b, m, nx):
            s = L[l]
            pe.wait_ge(N["xh"], s["first"] + b + 1)
            for q in range(QT):
                xq = xh[:, b, 128 * q:128 * q + 128]
                for g, (h0, n) in enumerate(GROUPS):
                    if q:
                        pe.wait_ge(s["mx"], b * 12 + 3 * (q - 1) + g + 1)
                    o = bank(g, n * KC).rearrange("p (h k) -> p h k", h=n)
                    last = nc.tensor.matmul(o, xq, Mh[:, h0:h0 + n, bass.ds(b * KC, KC)], start=True, stop=l != 1)
                    if l == 1:
                        nc.tensor.matmul(o, ones[:, 0:128], bqm[:, h0:h0 + n, bass.ds(b * KC, KC)], start=False, stop=False)
                        for i in range(3):
                            last = nc.tensor.matmul(o, mpart[i][:, 128 * q:128 * q + 128],
                                                    identb[0:KC, 0:KC].unsqueeze(1).to_broadcast([KC, n, KC]),
                                                    start=False, stop=i == 2)
                    last.then_inc(s["mxp"], 1)
            pe_shift(pe, s, b)
            pe.wait_ge(N["xl"], s["first"] + b + 1)

            def scores(h):
                if h >= 2:
                    pe.wait_ge(s["ex"], b * 16 + h - 1)
                o = bank(3 + h % 2, S, KC)
                mh, ml = Mh[:, h, bass.ds(b * KC, KC)], Ml[:, h, bass.ds(b * KC, KC)]
                nc.tensor.matmul(o, mh, xh[:, b, :], start=True, stop=False)
                nc.tensor.matmul(o, mh, xl[:, b, :], start=False, stop=False)
                nc.tensor.matmul(o, ml, xh[:, b, :], start=False, stop=False)
                if l == 1:
                    nc.tensor.matmul(o, bqm[:, h, bass.ds(b * KC, KC)], ones[:], start=False, stop=False)
                    for i in range(3):
                        nc.tensor.matmul(o, identb[0:KC, 0:KC], mpart[i], start=False, stop=False)
                nc.tensor.matmul(o, sel0[:, h:h + 1].to_broadcast([ROWS, KC]), nmT[:], start=False, stop=True).then_inc(s["sT"], 1)

            def values(h):
                pe.wait_ge(s["pl"], b * 16 + h + 1)
                d1 = DIM[l] + 1
                vh, vl_ = vslice(l, b, h)
                for q in range(QT):
                    if l == 3:
                        if h >= 2 and q == 0:
                            pe.wait_ge(s["on"], b * 16 + h - 1)
                        o = bank(5 + h % 2, d1, off=q * d1)
                    else:
                        o = bank(5 + q // 2, d1, off=(q % 2) * 16 * d1 + h * d1)
                    ph, pl = Ph[h % 3][0:KC, 128 * q:128 * q + 128], Pl[h % 3][0:KC, 128 * q:128 * q + 128]
                    nc.tensor.matmul(o, ph, vh, start=True, stop=False)
                    nc.tensor.matmul(o, ph, vl_, start=False, stop=False)
                    last = nc.tensor.matmul(o, pl, vh, start=False, stop=True)
                last.then_inc(s["pv"], 1)

            scores(0)
            scores(1)
            for h in range(16):
                if h < 14:
                    scores(h + 2)
                values(h)
                if h == 5 and nx:
                    pe_norm(pe, nx)
            if nx:
                pe.wait_ge(N["xt"], nx["n"] + 1)
            pe_out(pe, s, b, NH[l] * DIM[l] // 128, f"wo{l}", 16 if l == 3 else 2)

        def pe_shift(pe, s, b):
            pe.wait_ge(Z["nm"], s["zb"] + b + 1)
            pe.wait_ge(N["xt"], s["first"] + b + 1)
            o7 = bank(7, 256).bitcast(BF16)
            for q in range(QT):
                last = nc.tensor.transpose(o7[0:ROWS, 128 * q:128 * q + 128], nm[:, q, 0:ROWS], identb[:])
            last.then_inc(Z["nmt"], 1)
            pe.wait_ge(Z["nmT"], s["zb"] + b + 1)

        def pe_out(pe, s, b, nchunk, wo, n_on):
            pe.wait_ge(s["on"], b * n_on + n_on)
            for c in range(nchunk):
                if c >= 2:
                    pe.wait_ge(Z["at"], s["cb"] + b * nchunk + c - 1)
                for q in range(QT):
                    last = nc.tensor.transpose(bank(c % 2, 128, off=128 * q), attn[:, q, 128 * c:128 * c + 128], identf[:])
                last.then_inc(Z["atp"], 1)
                if c:
                    pe_out_chunk(pe, s, b, c - 1, nchunk, wo)
            pe_out_chunk(pe, s, b, nchunk - 1, nchunk, wo)

        def pe_out_chunk(pe, s, b, c, nchunk, wo):
            pe.wait_ge(Z["at"], s["cb"] + b * nchunk + c + 1)
            for q in range(QT):
                last = nc.tensor.matmul(bank(7, 128, off=128 * q), aT[:, c % 2, 128 * q:128 * q + 128],
                                        pwv(wo)[:, 128 * c:128 * c + 128], start=(c == 0 and q == 0),
                                        stop=(c == nchunk - 1), skip_group_check=True)
            last.then_inc(Z["op"], 1)

        def act_out(act, s, b, nchunk):
            for c in range(nchunk):
                act.wait_ge(Z["atp"], s["cb"] + b * nchunk + c + 1)
                if c >= 2:
                    act.wait_ge(Z["op"], s["cb"] + b * nchunk + c - 1)
                nc.scalar.activation(aT[:, c % 2, :], bank(c % 2), ACT.Copy).then_inc(Z["at"], 1)

        def act_exp(act, s, n0, n, rows, bias=None):
            src = bank(3 + n % 2, S, rows)
            kw = {} if bias is None else {"bias": bias}
            if n >= 3:
                act.wait_ge(s["pv"], n0 + n - 2)
            nc.scalar.activation(Ph[n % 3][0:rows, :], src, ACT.Exp, **kw)
            if n >= 2:
                act.wait_ge(s["pl"], n0 + n - 1)
            nc.scalar.activation(Pf[n % 2][0:rows, :], src, ACT.Exp, **kw).then_inc(s["ex"], 1)

        def pool_attn(pool, l, b, m, nx):
            for h in range(16):
                pool_parts(pool, L[l], b * 16, h, KC)
                if h == 0 and nx:
                    pool_rstd(pool, nx)
                if h == 2 and nx and nx["double"]:
                    pool_rstd(pool, nx, True)
                if h == 10 and nx:
                    pool_low(pool, nx)

        def pool_parts(pool, s, n0, n, rows):
            pool.wait_ge(s["ex"], n0 + n + 1)
            nc.gpsimd.tensor_tensor(Pl[n % 3][0:rows, :], Pf[n % 2][0:rows, :], Ph[n % 3][0:rows, :],
                                    ALU.subtract).then_inc(s["pl"], 1)

        def act_attn(act, l, b, m, nx):
            s = L[l]
            act_shift(act, s, b)
            for h in range(16):
                act.wait_ge(s["sT"], b * 16 + h + 1)
                act_exp(act, s, b * 16, h, KC)
                if h == 7 and nx:
                    act_norm(act, nx)
            act_out(act, s, b, NH[l] * DIM[l] // 128)

        def act_shift(act, s, b):
            act.wait_ge(Z["nmt"], s["zb"] + b + 1)
            nc.scalar.activation(nmT[:], bank(7, 256).bitcast(BF16)[0:ROWS, :], ACT.Copy).then_inc(Z["nmT"], 1)

        def dve_shift(dve, s, b, H):
            nc.vector.tensor_copy(nm[:, :, 0:H], mx[:, :, 0:H]).then_inc(Z["nmc"], 1)
            dve.wait_ge(Z["nmc"], (s["zb"] + b) * 4 + 1)
            nc.vector.tensor_tensor(mr1[:, :, 0:H], mx[:, :, 0:H], nm[:, :, 0:H], ALU.subtract).then_inc(Z["nmc"], 1)
            dve.wait_ge(Z["nmc"], (s["zb"] + b) * 4 + 2)
            nc.vector.tensor_copy(nm[:, :, 32:32 + H], mr1[:, :, 0:H]).then_inc(Z["nmc"], 1)
            dve.wait_ge(Z["nmc"], (s["zb"] + b) * 4 + 3)
            nc.vector.tensor_tensor(mr2[:, :, 0:H], mr1[:, :, 0:H], nm[:, :, 32:32 + H], ALU.subtract).then_inc(Z["nmc"], 1)
            dve.wait_ge(Z["nmc"], (s["zb"] + b) * 4 + 4)
            nc.vector.tensor_copy(nm[:, :, 64:64 + H], mr2[:, :, 0:H]).then_inc(Z["nm"], 1)

        def dve_attn(dve, l, b, m, nx):
            s = L[l]
            for q in range(QT):
                for g, (h0, n) in enumerate(GROUPS):
                    dve.wait_ge(s["mxp"], b * 12 + 3 * q + g + 1)
                    last = nc.vector.tensor_reduce(mx[:, q, h0:h0 + n], bank(g, n * KC).rearrange("p (h k) -> p h k", h=n),
                                                   AX, ALU.max).then_inc(s["mx"], 1)
            dve.wait_ge(s["mx"], b * 12 + 12)
            dve_shift(dve, s, b, 16)
            if nx:
                dve_stats(dve, nx)
            if l == 3:
                for h in range(16):
                    dve_head(dve, s, b, h, 16, 1)
                    if h == 1 and nx:
                        dve_scale(dve, nx)
                        if nx["double"]:
                            dve_stats(dve, nx, True)
                    if h == 3 and nx and nx["double"]:
                        dve_scale(dve, nx, True)
            else:
                if nx:
                    dve_scale(dve, nx)
                    if nx["double"]:
                        dve_stats(dve, nx, True)
                        dve_scale(dve, nx, True)
                dve.wait_ge(s["pv"], b * 16 + 16)
                for i in range(2):
                    o = bank(5 + i, 288).rearrange("p (q h d) -> p q h d", q=2, d=9)
                    nc.vector.reciprocal(rec[:, 2 * i:2 * i + 2, :], o[:, :, :, 8]).then_inc(s["rc"], 1)
                    dve.wait_ge(s["rc"], b * 2 + i + 1)
                    nc.vector.tensor_tensor(attn[:, 2 * i:2 * i + 2, 0:128].rearrange("p q (h d) -> p q h d", d=8),
                                            o[:, :, :, 0:8], rec[:, 2 * i:2 * i + 2, :].unsqueeze(3).to_broadcast([128, 2, 16, 8]),
                                            ALU.mult).then_inc(s["on"], 1)
            n = NH[l] * DIM[l] // 128
            dve.wait_ge(Z["op"], s["cb"] + b * n + n)
            dve_res(dve, l, s, b)

        def dve_head(dve, s, b, h, H, nc_):
            dve.wait_ge(s["pv"], (b * H + h + 1) * nc_)
            o = bank(5 + h % 2, QT * 65).rearrange("p (q d) -> p q d", d=65)
            nc.vector.reciprocal(rec[:, :, h], o[:, :, 64]).then_inc(s["rc"], 1)
            dve.wait_ge(s["rc"], b * H + h + 1)
            nc.vector.tensor_tensor(attn[:, :, 64 * h:64 * h + 64], o[:, :, 0:64],
                                    rec[:, :, h:h + 1].to_broadcast([128, QT, 64]), ALU.mult).then_inc(s["on"], 1)

        def dve_res(dve, l, s, b):
            xb = x[:, b, :, :].rearrange("p q d -> p (q d)")
            if l == 1:
                nc.vector.tensor_tensor(xb, bank(7), xb, ALU.add).then_inc(s["res"], 1)
                dve.wait_ge(s["res"], b + 1)
                nc.vector.tensor_tensor(x[:, b, :, :], x[:, b, :, :], rowv("bo").unsqueeze(1).to_broadcast([128, QT, D]),
                                        ALU.add).then_inc(done, 1)
            elif l == 3:
                nc.vector.scalar_tensor_tensor(xb, bank(7), tg[:, 0:1], xb, ALU.mult, ALU.add).then_inc(s["res"], 1)
                dve.wait_ge(s["res"], b + 1)
                nc.vector.tensor_tensor(x[:, b, :, :], x[:, b, :, :], btg[:].unsqueeze(1).to_broadcast([128, QT, D]),
                                        ALU.add).then_inc(done, 1)
            else:
                nc.vector.tensor_tensor(xb, bank(7), xb, ALU.add).then_inc(done, 1)

        tg = sb("tg", [128, 1])
        btg = sb("btg", [128, 128])
        tgs = sem("tgs")

        VLh, VLl = [v[:, 2080:4160].rearrange("p (c h d) -> p c h d", c=4, d=65) for v in (Vh, Vl)]
        vl = sems("v_", "p h e")
        kmp = sems("k_", "mp mh ml")
        fsp = sems("fs_", "ld hi lo")
        stage = work[:, 5120:5120 + STAGE]

        def pe_attn0(pe, b, m, nx):
            s = L[0]
            pe.wait_ge(kq["kgl"], b + 1)
            for c in range(4):
                if c >= 2:
                    pe.wait_ge(vl["e"], b * 4 + c - 1)
                nc.tensor.matmul(bank(5 + c % 2), kgf[:, 128 * c:128 * c + 128], pwv("wv0"), start=True, stop=True).then_inc(vl["p"], 1)
            pe.wait_ge(N["xh"], s["first"] + b + 1)

            def keys(h):
                if h >= 1:
                    pe.wait_ge(kmp["ml"], b * 8 + h)
                nc.tensor.matmul(bank(4), Gh[:, h, :], kgh, start=True, stop=False)
                nc.tensor.matmul(bank(4), Gh[:, h, :], kgl, start=False, stop=False)
                nc.tensor.matmul(bank(4), Gl[:, h, :], kgh, start=False, stop=True).then_inc(kmp["mp"], 1)

            keys(0)
            for h in range(8):
                pe.wait_ge(kmp["mh"], b * 8 + h + 1)
                for q in range(QT):
                    n = 4 * h + q
                    if n >= 2:
                        pe.wait_ge(s["mx"], b * 32 + n - 1)
                    xq = xh[:, b, 128 * q:128 * q + 128]
                    nc.tensor.matmul(bank(2 * (n % 2)), xq, MLh[:, h, :], start=True, stop=True)
                    o = bank(2 * (n % 2) + 1, KC)
                    nc.tensor.matmul(o, xq, Mh[:, h, bass.ds(b * KC, KC)], start=True, stop=False)
                    nc.tensor.matmul(o, ones[0:1, 0:128], negr[:, bass.ds(b * KC, KC)], start=False, stop=True).then_inc(s["mxp"], 1)
                    if q == 1 and h < 7:
                        keys(h + 1)
            pe_shift(pe, s, b)
            pe.wait_ge(N["xl"], s["first"] + b + 1)
            pe.wait_ge(kmp["ml"], b * 8 + 8)

            def scores(n):
                h, c = divmod(n, 5)
                if n >= 2:
                    pe.wait_ge(s["ex"], b * 40 + n - 1)
                if c < 4:
                    o, mh, ml, w = bank(3 + n % 2), MLh[:, h, 128 * c:128 * c + 128], MLl[:, h, 128 * c:128 * c + 128], 128
                else:
                    o, w = bank(3 + n % 2, S, KC), KC
                    mh, ml = Mh[:, h, bass.ds(b * KC, KC)], Ml[:, h, bass.ds(b * KC, KC)]
                nc.tensor.matmul(o, mh, xh[:, b, :], start=True, stop=False)
                nc.tensor.matmul(o, mh, xl[:, b, :], start=False, stop=False)
                nc.tensor.matmul(o, ml, xh[:, b, :], start=False, stop=False)
                nc.tensor.matmul(o, sel0[:, h:h + 1].to_broadcast([ROWS, w]), nmT[:], start=False, stop=True).then_inc(s["sT"], 1)

            def values(n):
                h, c = divmod(n, 5)
                pe.wait_ge(s["pl"], b * 40 + n + 1)
                if c == 0:
                    if h >= 2:
                        pe.wait_ge(s["on"], b * 8 + h - 1)
                    elif h == 0:
                        pe.wait_ge(vl["e"], b * 4 + 4)
                w = 128 if c < 4 else KC
                for q in range(QT):
                    vh, vlo = ([v[:, c, h, :] for v in (VLh, VLl)] if c < 4 else
                               [v[0:KC, bass.ds((b * 8 + h) * 65, 65)] for v in (Vh, Vl)])
                    o = bank(5 + h % 2, 65, off=65 * q)
                    ph, pl = Ph[n % 3][0:w, 128 * q:128 * q + 128], Pl[n % 3][0:w, 128 * q:128 * q + 128]
                    nc.tensor.matmul(o, ph, vh, start=(c == 0 and q == 0), stop=False, skip_group_check=True)
                    nc.tensor.matmul(o, ph, vlo, start=False, stop=False, skip_group_check=True)
                    last = nc.tensor.matmul(o, pl, vh, start=False, stop=c == 4, skip_group_check=True)
                last.then_inc(s["pv"], 1)

            scores(0)
            scores(1)
            for n in range(40):
                if n < 38:
                    scores(n + 2)
                values(n)
                if n == 10 and nx:
                    pe_norm(pe, nx)
            if nx:
                pe.wait_ge(N["xt"], nx["n"] + 1)
            pe_out(pe, s, b, 4, "wo0", 8)

        def act_attn0(act, b, m, nx):
            s = L[0]
            act.wait_ge(N["xt"], m["n"] + 1)
            nc.scalar.activation(kgf, xt[:], ACT.Copy, scale=col("kv_gate")).then_inc(kq["kg"], 1)
            act.wait_ge(kq["kg"], b + 1)
            nc.scalar.activation(kgh, kgf, ACT.Copy).then_inc(kq["kgh"], 1)
            for c in range(4):
                act.wait_ge(vl["p"], b * 4 + c + 1)
                nc.scalar.activation(VLh[:, c, :, 0:64], bank(5 + c % 2).rearrange("p (h d) -> p h d", d=64), ACT.Copy).then_inc(vl["h"], 1)
            nc.scalar.activation(negb[:], negk[:, bass.ds(b, 1)], ACT.Copy).then_inc(kq["nb"], 1)
            for h in range(8):
                act.wait_ge(kmp["mp"], b * 8 + h + 1)
                nc.scalar.activation(MLh[:, h, :], bank(4), ACT.Copy).then_inc(kmp["mh"], 1)
            act_shift(act, s, b)
            act.wait_ge(kq["nb"], b + 1)
            for n in range(40):
                act.wait_ge(s["sT"], b * 40 + n + 1)
                act_exp(act, s, b * 40, n, 128 if n % 5 < 4 else KC, None if n % 5 < 4 else negb[:])
                if n == 14 and nx:
                    act_norm(act, nx)
            act_out(act, s, b, 4)

        def dve_attn0(dve, b, m, nx):
            s = L[0]
            for c in range(4):
                dve.wait_ge(vl["h"], b * 4 + c + 1)
                nc.vector.tensor_tensor(VLl[:, c, :, 0:64], bank(5 + c % 2).rearrange("p (h d) -> p h d", d=64),
                                        VLh[:, c, :, 0:64], ALU.subtract).then_inc(vl["e"], 1)
            for h in range(8):
                dve.wait_ge(kmp["mh"], b * 8 + h + 1)
                nc.vector.tensor_tensor(MLl[:, h, :], bank(4), MLh[:, h, :], ALU.subtract).then_inc(kmp["ml"], 1)
                for q in range(QT):
                    n = 4 * h + q
                    dve.wait_ge(s["mxp"], b * 32 + n + 1)
                    o = ps[:, 1024 * (n % 2):1024 * (n % 2) + 512 + KC]
                    nc.vector.tensor_reduce(mx[:, q, h:h + 1], o, AX, ALU.max).then_inc(s["mx"], 1)
            dve.wait_ge(s["mx"], b * 32 + 32)
            dve_shift(dve, s, b, 8)
            if nx:
                dve_norm(dve, nx)
            for h in range(8):
                dve_head(dve, s, b, h, 8, 5)
                if h % 2 and h // 2 < STAGES_PER_BATCH:
                    dve_weights(dve, b, h // 2)
            dve.wait_ge(Z["op"], s["cb"] + b * 4 + 4)
            dve_res(dve, 0, s, b)

        def dve_weights(dve, b, k):
            n = b * STAGES_PER_BATCH + k
            dve.wait_ge(fsp["ld"], n * 16 + 16)
            h, l_ = [part[:, bass.ds(n * STAGE, STAGE)] for part in (fh, fl)]
            nc.vector.tensor_copy(h, stage).then_inc(fsp["hi"], 1)
            dve.wait_ge(fsp["hi"], n + 1)
            nc.vector.tensor_tensor(l_, stage, h, ALU.subtract).then_inc(fsp["lo"], 1)

        def pool_attn0(pool, b, m, nx):
            s = L[0]
            pool.wait_ge(kq["kgh"], b + 1)
            nc.gpsimd.tensor_tensor(kgl, kgf, kgh, ALU.subtract).then_inc(kq["kgl"], 1)
            for n in range(40):
                pool_parts(pool, s, b * 40, n, 128 if n % 5 < 4 else KC)
                if n == 0 and nx:
                    pool_rstd(pool, nx)
                if n == 2 and nx and nx["double"]:
                    pool_rstd(pool, nx, True)
                if n == 16 and nx:
                    pool_low(pool, nx)

        FN = "c lg sp h yo "
        F = [sems(f"f{i}_", FN + more) for i, more in enumerate(("lgs g", "gt xo aa", "lgs gt xo aa t1 t2 bb cc dd ee ff", "lgs"))]
        for i in range(4):
            L[i].update(first=2 * i * B, first2=B if i == 3 else 0, zb=i * B, cb=CB[i])
            F[i].update(first=(2 * i + 1) * B)
        EN = [8, 8, 8, 16]
        TOP = [2, 2, 2, 6]

        lg = sb("lg", [128, QT, 16])
        rsm = sb("rsm", [128, QT, 4])
        sc_ = sb("sc_", [128, QT, 16])
        sb_ = sb("sb_", [128, QT, 16])
        tri8 = sb("tri8", [128, 64])
        T1 = P4[:, 0, :].bitcast(BF16).rearrange("p (q e) -> p q e", q=QT)
        T2 = P4[:, 1, :].bitcast(BF16).rearrange("p (q e) -> p q e", q=QT)
        rank = sb("rank", [128, QT, 16])
        gates = sb("gates", [128, QT, 16])

        def fw(f, off, n, part=fh):
            return part[:, FOFF[f"f{f}"] + off:FOFF[f"f{f}"] + off + n]

        def pe_router(pe, f, b):
            s = F[f]
            E = EN[f]
            pe.wait_ge(N["xl"], s["first"] + b + 1)
            for q in range(QT):
                o = bank(7, E, off=E * q)
                a, c = xh[:, b, 128 * q:128 * q + 128], xl[:, b, 128 * q:128 * q + 128]
                nc.tensor.matmul(o, a, fw(f, 0, E), start=True, stop=False)
                nc.tensor.matmul(o, a, fw(f, 0, E, fl), start=False, stop=False)
                last = nc.tensor.matmul(o, c, fw(f, 0, E), start=False, stop=True)
            last.then_inc(s["lg"], 1)

        def chainer(eng, sem_, b, per):
            n = [0]

            def link(ins):
                n[0] += 1
                ins.then_inc(sem_, 1)
                eng.wait_ge(sem_, b * per + n[0])
            return link, n

        def dve_rank(dve, link, f, score):
            E = EN[f]
            E2 = E * E
            t1 = T1[:, :, 0:E2].rearrange("p q (i j) -> p q i j", i=E)
            t2 = T2[:, :, 0:E2].rearrange("p q (i j) -> p q i j", i=E)
            for q in range(QT):
                sj = score[:, q, :].unsqueeze(1).to_broadcast([128, E, E])
                si = score[:, q, :].unsqueeze(2).to_broadcast([128, E, E])
                nc.vector.tensor_tensor(t1[:, q], sj, si, ALU.is_gt)
                last = nc.vector.tensor_tensor(t2[:, q], sj, si, ALU.is_equal)
            link(last)
            trv = (tri[:, 0:256] if E == 16 else tri8[:]).unsqueeze(1).to_broadcast([128, QT, E2])
            link(nc.vector.tensor_tensor(T2[:, :, 0:E2], T2[:, :, 0:E2], trv, ALU.mult))
            link(nc.vector.tensor_tensor(T1[:, :, 0:E2], T1[:, :, 0:E2], T2[:, :, 0:E2], ALU.add))
            for q in range(QT):
                last = nc.vector.tensor_reduce(rank[:, q, 0:E], t1[:, q], AX, ALU.add)
            link(last)
            link(nc.vector.tensor_scalar(rank[:, :, 0:E], rank[:, :, 0:E], float(TOP[f]), None, ALU.is_lt))

        def dve_logits(dve, link, f, b, bias):
            s = F[f]
            E = EN[f]
            dve.wait_ge(s["lg"], b + 1)
            src = bank(7, QT * E).rearrange("p (q e) -> p q e", e=E)
            if bias:
                link(nc.vector.tensor_tensor(lg[:, :, 0:E], src, rowv(bias).unsqueeze(1).to_broadcast([128, QT, E]), ALU.add))
            else:
                link(nc.vector.tensor_copy(lg[:, :, 0:E], src))

        def dve_softmax(dve, link, f, b):
            s = F[f]
            E = EN[f]
            link(nc.vector.tensor_reduce(rsm[:, :, 0:1], lg[:, :, 0:E], AX, ALU.max))
            link(nc.vector.tensor_tensor(lg[:, :, 0:E], lg[:, :, 0:E], rsm[:, :, 0:1].to_broadcast([128, QT, E]), ALU.subtract))
            nc.vector.memset(rsm[:, :, 3:4], 0.0).then_inc(s["lgs"], 1)
            dve.wait_ge(s["sp"], b + 1)
            link(nc.vector.tensor_reduce(rsm[:, :, 1:2], sc_[:, :, 0:E], AX, ALU.add))
            link(nc.vector.reciprocal(rsm[:, :, 2:3], rsm[:, :, 1:2]))
            link(nc.vector.tensor_tensor(sc_[:, :, 0:E], sc_[:, :, 0:E], rsm[:, :, 2:3].to_broadcast([128, QT, E]), ALU.mult))

        def act_exp_logits(act, f, b):
            s = F[f]
            act.wait_ge(s["lgs"], b + 1)
            nc.scalar.activation(sc_[:, :, 0:EN[f]], lg[:, :, 0:EN[f]], ACT.Exp).then_inc(s["sp"], 1)

        ms = sb("ms", [128, B, QT, 8])
        route = sb("route", [128, QT, 8])
        msr = P4[:, 3, 0:128].rearrange("p (q r) -> p q r", q=QT)
        G0 = work[:, 0:4096].rearrange("p (b g s) -> p b g s", b=B, g=2)
        RT = work[0:32, 4096:4608]
        junk = work[0:32, 4608:5120]
        hs0 = work[:, 5120:6144].rearrange("p (g s) -> p g s", g=2)
        selb = P4[0:32, 2, 0:256].bitcast(BF16)
        self_ = aT[0:32, 0, :]
        th = sb("th", [32, 8])
        r0 = sems("r0_", "rt rtt sel selm den rte ch lp end")
        r0d = sems("r0d_", "sb hs o")

        def pe_f0(pe):
            s = F[0]
            pe.wait_ge(fsp["lo"], B * STAGES_PER_BATCH + 1)
            def pe_batch(b, m, nx):
                pe_router(pe, 0, b)
                for g in range(2):
                    o = bank(g)
                    wh, wl = fw(0, 8 + 128 * g, 128), fw(0, 8 + 128 * g, 128, fl)
                    nc.tensor.matmul(o, wh, xh[:, b, :], start=True, stop=False)
                    nc.tensor.matmul(o, wh, xl[:, b, :], start=False, stop=False)
                    nc.tensor.matmul(o, wl, xh[:, b, :], start=False, stop=True).then_inc(s["h"], 1)
                if nx:
                    pe.wait_ge(s["lgs"], b + 1)
                    pe_norm(pe, nx)
            batches(pe, 1, pe_batch)
            for q in range(QT):
                pe.wait_ge(r0["rte"], q + 1)
                last = nc.tensor.transpose(bank(2, 128, 32, off=128 * q), msr[:, q, :], identf[:])
            last.then_inc(r0["rt"], 1)
            pe.wait_ge(r0["sel"], 1)
            pe.wait_ge(s["g"], 8)
            with pe.Fori(0, B) as b:
                for g in range(2):
                    nc.tensor.matmul(bank(g), expd[:, b, g, :], selb, start=True, stop=True).then_inc(r0d["sb"], 1)
                pe.wait_ge(r0d["hs"], 2 * b + 2)
                for q in range(QT):
                    o = bank(7, 128, off=128 * q)
                    for g in range(2):
                        nc.tensor.matmul(o, hs0[:, g, 128 * q:128 * q + 128], pwv("w2_0")[:, 128 * g:128 * g + 128],
                                         start=g == 0, stop=False)
                    last = nc.tensor.matmul(o, self_[:, 128 * q:128 * q + 128], b2s[:, b, :], start=False, stop=True)
                last.then_inc(r0d["o"], 1)
                pe.wait_ge(done, s["first"] + b + 1)


        def act_f0(act):
            s = F[0]
            def act_batch(b, m, nx):
                act_exp_logits(act, 0, b)
                for g in range(2):
                    act.wait_ge(s["h"], 2 * b + g + 1)
                    nc.scalar.activation(G0[:, b, g, :], bank(g), ACT.Gelu, bias=col("b1", g)).then_inc(s["g"], 1)
                if nx:
                    act_norm(act, nx)
            batches(act, 1, act_batch)

        def dve_f0(dve):
            s = F[0]
            def dve_batch(b, m, nx):
                PER = 12
                link, n = chainer(dve, s["c"], b, PER)
                dve_logits(dve, link, 0, b, "w_gate_b")
                dve_softmax(dve, link, 0, b)
                if nx:
                    dve_stats(dve, nx)
                dve_rank(dve, link, 0, sc_[:, :, 0:8])
                if nx:
                    dve_scale(dve, nx)
                link(nc.vector.tensor_tensor(ms[:, b, :, :], sc_[:, :, 0:8], rank[:, :, 0:8], ALU.mult))
                assert n[0] == PER, n[0]
            batches(dve, 1, dve_batch)
            k = [0]

            def lk(ins):
                k[0] += 1
                ins.then_inc(r0["ch"], 1)
                dve.wait_ge(r0["ch"], k[0])
            lk(nc.vector.tensor_tensor(route[:], ms[:, 0], ms[:, 1], ALU.add))
            lk(nc.vector.tensor_tensor(route[:], route[:], ms[:, 2], ALU.add))
            lk(nc.vector.tensor_tensor(route[:], route[:], ms[:, 3], ALU.add))
            lk(nc.vector.tensor_scalar(route[:], route[:], 1e-6, None, ALU.add))
            lk(nc.vector.reciprocal(route[:], route[:]))
            for q in range(QT):
                o = msr[:, q, :].rearrange("p (b e) -> p b e", b=B)
                last = nc.vector.tensor_tensor(o, ms[:, :, q, :], route[:, q, :].unsqueeze(1).to_broadcast([128, B, 8]), ALU.mult)
                if q < QT - 1:
                    lk(last)
                else:
                    lk(last)
                k[0] += 1
                nc.vector.tensor_scalar(o, o, float(B), None, ALU.mult).then_inc(r0["ch"], 1)
                dve.wait_ge(r0["ch"], k[0])
                nc.vector.memset(th[:, 7:8], 0.0).then_inc(r0["rte"], 1)
            dve.wait_ge(r0["rt"], 1)
            lk(nc.vector.tensor_copy(RT, bank(2, S, 32)))
            lk(nc.vector.memset(th[:], 0.0))
            thi = th[:, :].bitcast(I32)
            dve.wait_ge(in_c, 16 * 11)
            with dve.Fori(0, BITS) as i:
                nc.vector.tensor_tensor(thi[:, 1:2], thi[:, 0:1], bits[:, bass.ds(i, 1)], ALU.bitwise_or).then_inc(r0["lp"], 1)
                dve.wait_ge(r0["lp"], i * 4 + 1)
                nc.vector.tensor_scalar(junk, RT, th[:, 1:2], None, ALU.is_ge, ALU.add, accum_out=th[:, 2:3]).then_inc(r0["lp"], 1)
                dve.wait_ge(r0["lp"], i * 4 + 2)
                nc.vector.tensor_scalar(th[:, 3:4], th[:, 2:3], float(KEEP), th[:, 1:2], ALU.is_ge, ALU.mult).then_inc(r0["lp"], 1)
                dve.wait_ge(r0["lp"], i * 4 + 3)
                nc.vector.tensor_tensor(th[:, 0:1], th[:, 0:1], th[:, 3:4], ALU.max).then_inc(r0["lp"], 1)
                dve.wait_ge(r0["lp"], i * 4 + 4)
            lk(nc.vector.tensor_scalar(self_, RT, th[:, 0:1], None, ALU.is_gt, ALU.add, accum_out=th[:, 4:5]))
            lk(nc.vector.tensor_scalar(th[:, 5:6], th[:, 4:5], -1.0, float(KEEP), ALU.mult, ALU.add))
            lk(nc.vector.tensor_scalar(RT, RT, th[:, 0:1], None, ALU.is_equal))
            lk(nc.vector.tensor_tensor_scan(junk, ones[0:32, :], RT, 0.0, ALU.mult, ALU.add))
            lk(nc.vector.scalar_tensor_tensor(junk, junk, th[:, 5:6], RT, ALU.is_le, ALU.mult))
            lk(nc.vector.tensor_tensor(self_, self_, junk, ALU.add))
            nc.vector.tensor_copy(selb, self_).then_inc(r0["sel"], 1)
            dve.wait_ge(s["g"], 8)
            with dve.Fori(0, B) as b:
                for g in range(2):
                    dve.wait_ge(r0d["sb"], 2 * b + g + 1)
                    nc.vector.tensor_tensor(hs0[:, g, :], G0[:, b, g, :], bank(g), ALU.mult).then_inc(r0d["hs"], 1)
                dve.wait_ge(r0d["o"], b + 1)
                xb = x[:, b, :, :].rearrange("p q d -> p (q d)")
                nc.vector.tensor_tensor(xb, bank(7), xb, ALU.add).then_inc(done, 1)

        hb = [work[:, 512 * i:512 * i + 512] for i in range(12)]

        def pe_hidden_free(pe, s, b, U, nprod, k):
            u = (k - 4) // nprod
            if nprod == 2:
                pe.wait_ge(s["aa"], b * U + u + 1)
            elif k % 4 < 2:
                pe.wait_ge(s["gt"], (b * U + u) * 2 + k % 4 + 1)
            else:
                pe.wait_ge(s["t2"], (b * U + u) * 2 + k % 4 - 1)

        def pe_units(pe, f, b, units, nprod, wdown, whid, nx):
            s = F[f]
            U = len(units)

            def hidden(u):
                for i in range(nprod):
                    k = nprod * u + i
                    if k >= 4:
                        pe_hidden_free(pe, s, b, U, nprod, k)
                    wh, wl = whid(u, i, fh), whid(u, i, fl)
                    o = bank(k % 4)
                    nc.tensor.matmul(o, wh, xh[:, b, :], start=True, stop=False)
                    nc.tensor.matmul(o, wh, xl[:, b, :], start=False, stop=False)
                    nc.tensor.matmul(o, wl, xh[:, b, :], start=False, stop=True).then_inc(s["h"], 1)

            def down(u):
                pe.wait_ge(s["aa"], b * U + u + 1)
                if u >= 2:
                    pe.wait_ge(s["yo"], b * U + u - 1)
                for q in range(QT):
                    last = nc.tensor.matmul(bank(5 + u % 2, 128, off=128 * q), hb[8 + u % 2][:, 128 * q:128 * q + 128],
                                            wdown(u), start=True, stop=True)
                last.then_inc(s["xo"], 1)
            hidden(0)
            for u in range(U):
                if u + 1 < U:
                    hidden(u + 1)
                down(u)
                if u == 4 and nx:
                    pe.wait_ge(s["sp"], b + 1)
                    pe_norm(pe, nx)

        def dve_gated_add(dve, s, b, U, u, g):
            dve.wait_ge(s["xo"], b * U + u + 1)
            if u:
                dve.wait_ge(s["yo"], b * U + u)
            for q in range(QT):
                o = bank(5 + u % 2, 128, off=128 * q)
                xq = x[:, b, q, :]
                if g is None:
                    last = nc.vector.tensor_tensor(xq, o, xq, ALU.add)
                else:
                    last = nc.vector.scalar_tensor_tensor(xq, o, g(q), xq, ALU.mult, ALU.add)
            last.then_inc(s["yo"], 1)

        U1 = [("s", c) for c in range(4)] + [("e", e) for e in range(8)]

        def whid1(u, i, part):
            kind, n = U1[u]
            off = 8 + (512 * i + 128 * n if kind == "s" else 1024 + 256 * n + 128 * i)
            return fw(1, off, 128, part)

        def wdown1(u):
            kind, n = U1[u]
            return pwv("sw3" if kind == "s" else "w3")[:, 128 * n:128 * n + 128]

        def pe_f1(pe):
            def pe_batch(b, m, nx):
                pe_router(pe, 1, b)
                pe_units(pe, 1, b, U1, 2, wdown1, whid1, nx)
            batches(pe, 3, pe_batch)

        def act_f1(act):
            s = F[1]
            U = len(U1)
            def act_batch(b, m, nx):
                act.wait_ge(s["lg"], b + 1)
                nc.scalar.activation(sc_[:, :, 0:8], bank(7, 32).rearrange("p (q e) -> p q e", e=8), ACT.Sigmoid).then_inc(s["sp"], 1)
                for u in range(U):
                    act.wait_ge(s["h"], (b * U + u) * 2 + 1)
                    if u >= 2:
                        act.wait_ge(s["aa"], b * U + u - 1)
                    nc.scalar.activation(hb[u % 2], bank((2 * u) % 4), ACT.Silu).then_inc(s["gt"], 1)
                    if u == 6 and nx:
                        act_norm(act, nx)
            batches(act, 3, act_batch)

        def dve_f1(dve):
            s = F[1]
            U = len(U1)
            def dve_batch(b, m, nx):
                PER = 7
                link, n = chainer(dve, s["c"], b, PER)
                dve.wait_ge(s["sp"], b + 1)
                link(nc.vector.tensor_tensor(sb_[:, :, 0:8], sc_[:, :, 0:8], rowv("expert_bias").unsqueeze(1).to_broadcast([128, QT, 8]), ALU.add))
                dve_rank(dve, link, 1, sb_[:, :, 0:8])
                link(nc.vector.tensor_tensor(gates[:, :, 0:8], sc_[:, :, 0:8], rank[:, :, 0:8], ALU.mult))
                assert n[0] == PER, n[0]

                def g_of(u):
                    kind, e = U1[u]
                    return None if kind == "s" else lambda q: gates[:, q, e:e + 1]
                for u in range(U):
                    dve.wait_ge(s["gt"], b * U + u + 1)
                    dve.wait_ge(s["h"], (b * U + u) * 2 + 2)
                    if u >= 2:
                        dve.wait_ge(s["xo"], b * U + u - 1)
                    nc.vector.tensor_tensor(hb[8 + u % 2], hb[u % 2], bank((2 * u + 1) % 4), ALU.mult).then_inc(s["aa"], 1)
                    if u:
                        dve_gated_add(dve, s, b, U, u - 1, g_of(u - 1))
                    if u == 1 and nx:
                        dve_stats(dve, nx)
                    if u == 2 and nx:
                        dve_scale(dve, nx)
                dve_gated_add(dve, s, b, U, U - 1, g_of(U - 1))
                dve.wait_ge(s["yo"], b * U + U)
                nc.vector.memset(rsm[:, :, 3:4], 0.0).then_inc(done, 1)
            batches(dve, 3, dve_batch)

        U2 = 9
        cwx = sb("cwx", [128, QT, 9])
        cwT = P4[0:9, 3, :]

        def whid2(u, i, part):
            return fw(2, 8 + 512 * u + 128 * i, 128, part)

        def wdown2(u):
            return pwv("w2_2")[:, 128 * u:128 * u + 128]

        def pe_f2(pe):
            s = F[2]
            def pe_batch(b, m, nx):
                pe_router(pe, 2, b)
                pe_units(pe, 2, b, list(range(U2)), 4, wdown2, whid2, nx)
                if nx:
                    pe.wait_ge(N["xt"], nx["n"] + 1)
                pe.wait_ge(s["bb"], b + 1)
                for q in range(QT):
                    last = nc.tensor.transpose(bank(7, 128, 9, off=128 * q), cwx[:, q, :], identf[:])
                last.then_inc(s["cc"], 1)
                pe.wait_ge(s["dd"], b + 1)
                for q in range(QT):
                    last = nc.tensor.matmul(bank(4, 128, off=128 * q), cwT[:, 128 * q:128 * q + 128], b2c[:], start=True, stop=True)
                last.then_inc(s["ee"], 1)
            batches(pe, 5, pe_batch)

        def act_f2(act):
            s = F[2]
            def act_batch(b, m, nx):
                act_exp_logits(act, 2, b)
                for u in range(U2):
                    for i in range(2):
                        act.wait_ge(s["h"], (b * U2 + u) * 4 + i + 1)
                        if u >= 2:
                            act.wait_ge(s["t2"], (b * U2 + u - 1) * 2)
                        nc.scalar.activation(hb[2 * (u % 2) + i], bank(i), ACT.Identity, bias=col("hb", 4 * u + i)).then_inc(s["gt"], 1)
                    act.wait_ge(s["t1"], b * U2 + u + 1)
                    nc.scalar.activation(hb[6], hb[4], ACT.Sigmoid, scale=1.702).then_inc(s["ff"], 1)
                    if u == 5 and nx:
                        act_norm(act, nx)
                act.wait_ge(s["cc"], b + 1)
                nc.scalar.activation(cwT, bank(7, S, 9), ACT.Copy).then_inc(s["dd"], 1)
            batches(act, 5, act_batch)

        def dve_f2(dve):
            s = F[2]
            def dve_batch(b, m, nx):
                PER = 13 + 9 * 4
                link, n = chainer(dve, s["c"], b, PER)
                dve_logits(dve, link, 2, b, None)
                dve_softmax(dve, link, 2, b)
                link(nc.vector.tensor_tensor(sb_[:, :, 0:8], sc_[:, :, 0:8], rowv("gate_b").unsqueeze(1).to_broadcast([128, QT, 8]), ALU.add))
                dve_rank(dve, link, 2, sb_[:, :, 0:8])
                link(nc.vector.tensor_tensor(cwx[:, :, 0:8], sc_[:, :, 0:8], rank[:, :, 0:8], ALU.mult))
                nc.vector.memset(cwx[:, :, 8:9], 1.0).then_inc(s["bb"], 1)

                def g_of(u):
                    return None if u == 8 else lambda q: cwx[:, q, u:u + 1]
                for u in range(U2):
                    dve.wait_ge(s["gt"], (b * U2 + u) * 2 + 2)
                    for i in range(2):
                        dve.wait_ge(s["h"], (b * U2 + u) * 4 + 3 + i)
                        last = nc.vector.scalar_tensor_tensor(hb[4 + i], bank(2 + i), col("hb", 4 * u + 2 + i), hb[2 * (u % 2) + i],
                                                              ALU.add, ALU.mult).then_inc(s["t2"], 1)
                    dve.wait_ge(s["t2"], (b * U2 + u) * 2 + 2)
                    nc.vector.tensor_scalar(hb[4], hb[4], 7.0, None, ALU.min).then_inc(s["t1"], 1)
                    link(nc.vector.tensor_scalar(hb[5], hb[5], 7.0, -7.0, ALU.min, ALU.max))
                    link(nc.vector.tensor_scalar(hb[5], hb[5], 1.0, None, ALU.add))
                    link(nc.vector.tensor_tensor(hb[7], hb[5], hb[4], ALU.mult))
                    dve.wait_ge(s["ff"], b * U2 + u + 1)
                    if u >= 2:
                        dve.wait_ge(s["xo"], b * U2 + u - 1)
                    nc.vector.tensor_tensor(hb[8 + u % 2], hb[7], hb[6], ALU.mult).then_inc(s["aa"], 1)
                    link(nc.vector.memset(rsm[:, :, 3:4], 0.0))
                    if u:
                        dve_gated_add(dve, s, b, U2, u - 1, g_of(u - 1))
                    if u == 1 and nx:
                        dve_stats(dve, nx)
                        if not nx["double"]:
                            dve_scale(dve, nx)
                    if u == 2 and nx and nx["double"]:
                        dve_scale(dve, nx)
                        dve_stats(dve, nx, True)
                    if u == 3 and nx and nx["double"]:
                        dve_scale(dve, nx, True)
                dve_gated_add(dve, s, b, U2, U2 - 1, g_of(U2 - 1))
                assert n[0] == PER, n[0]
                dve.wait_ge(s["yo"], b * U2 + U2)
                dve.wait_ge(s["ee"], b + 1)
                xb = x[:, b, :, :].rearrange("p q d -> p (q d)")
                nc.vector.tensor_tensor(xb, bank(4), xb, ALU.add).then_inc(done, 1)
            batches(dve, 5, dve_batch)

        def pe_f3(pe):
            s = F[3]
            def pe_batch(b, m, nx):
                pe_router(pe, 3, b)
                pe.wait_ge(done, s["first"] + b)
                for q in range(QT):
                    a, c = xh[:, b, 128 * q:128 * q + 128], xl[:, b, 128 * q:128 * q + 128]
                    for g in range(4):
                        n = 4 * q + g
                        if n >= 4:
                            pe.wait_ge(s["yo"], b * 16 + n - 3)
                        o = bank(n % 4)
                        nc.tensor.matmul(o, a, fw(3, 16 + 512 * g, 512), start=True, stop=False)
                        nc.tensor.matmul(o, a, fw(3, 16 + 512 * g, 512, fl), start=False, stop=False)
                        nc.tensor.matmul(o, c, fw(3, 16 + 512 * g, 512), start=False, stop=True).then_inc(s["h"], 1)
                    if q == 1 and nx:
                        pe.wait_ge(s["lgs"], b + 1)
                        pe_norm(pe, nx)
            batches(pe, 7, pe_batch)

        def act_f3(act):
            def act_batch(b, m, nx):
                act_exp_logits(act, 3, b)
                if nx:
                    act_norm(act, nx)
            batches(act, 7, act_batch)

        def dve_f3(dve):
            s = F[3]
            def dve_batch(b, m, nx):
                PER = 21 + 16 * 3
                link, n = chainer(dve, s["c"], b, PER)
                dve_logits(dve, link, 3, b, "router_b")
                dve_softmax(dve, link, 3, b)
                dve_rank(dve, link, 3, sc_[:])
                link(nc.vector.tensor_tensor(gates[:], sc_[:], rank[:], ALU.mult))
                sm = rsm[:, :, 0:1]
                link(nc.vector.tensor_reduce(sm, gates[:], AX, ALU.add))
                link(nc.vector.tensor_scalar(sm, sm, 1e-10, None, ALU.add))
                link(nc.vector.reciprocal(sm, sm))
                link(nc.vector.tensor_tensor(gates[:], gates[:], sm.to_broadcast([128, QT, 16]), ALU.mult))
                link(nc.vector.tensor_reduce(rsm[:, :, 1:2], gates[:], AX, ALU.add))
                link(nc.vector.tensor_scalar(rsm[:, :, 2:3], rsm[:, :, 1:2], 1e-10, None, ALU.max))
                link(nc.vector.reciprocal(rsm[:, :, 2:3], rsm[:, :, 2:3]))
                link(nc.vector.tensor_tensor(gates[:], gates[:], rsm[:, :, 2:3].to_broadcast([128, QT, 16]), ALU.mult))
                link(nc.vector.tensor_scalar(rsm[:, :, 1:2], rsm[:, :, 1:2], 1e-10, None, ALU.mult))
                for q in range(QT):
                    if q == 1 and nx:
                        dve_stats(dve, nx)
                        dve_scale(dve, nx)
                    for g in range(4):
                        dve.wait_ge(s["h"], b * 16 + 4 * q + g + 1)
                        for i in range(4):
                            e = 4 * g + i
                            add = nc.vector.scalar_tensor_tensor(x[:, b, q, :], bank(g, 128, off=128 * i), gates[:, q, e:e + 1],
                                                                 x[:, b, q, :], ALU.mult, ALU.add)
                            if i < 3:
                                link(add)
                        add.then_inc(s["yo"], 1)
                        dve.wait_ge(s["yo"], b * 16 + 4 * q + g + 1)
                assert n[0] == PER, n[0]
                nc.vector.tensor_tensor(x[:, b, :, :], x[:, b, :, :], rsm[:, :, 1:2].to_broadcast([128, QT, D]), ALU.add).then_inc(done, 1)
            batches(dve, 7, dve_batch)


        @block.sync
        def _(sp):
            sp.dma_start(x[:], A["x"]).then_inc(in_x, 16)
            sp.dma_start(ctxT[:], A["ctxT"]).then_inc(in_c, 16)
            sp.dma_start(crow[:], A["ctxr"]).then_inc(in_c, 16)
            sp.dma_start(cols[:], A["cols"]).then_inc(in_c, 16)
            sp.dma_start(rowc[:], A["rowc"]).then_inc(in_c, 16)
            sp.dma_start(bkq[:], A["bkq"]).then_inc(in_c, 16)
            sp.dma_start(bkqT[:], A["bkqT"]).then_inc(in_c, 16)
            sp.dma_start(b2c[:], A["b2c"]).then_inc(in_c, 16)
            sp.dma_start(b2s[:], A["b2s"]).then_inc(in_c, 16)
            sp.dma_start(tri[:], A["tri"]).then_inc(in_c, 16)
            sp.dma_start(tri8[:], A["tri8"]).then_inc(in_c, 16)
            sp.dma_start(bits[:], A["bits"]).then_inc(in_c, 16)
            sp.dma_start(mk8[:], A["mk8"]).then_inc(in_mask, 16)
            sp.dma_start(mr8[:], A["mr8"]).then_inc(in_mask, 16)
            sp.dma_start(identf[:], A["identf"]).then_inc(in_w, 16)
            sp.dma_start(identb[:], A["identb"]).then_inc(in_w, 16)
            sp.dma_start(sel0[:], A["sel0"]).then_inc(in_w, 16)
            sp.dma_start(expd[:], A["expd"]).then_inc(in_w, 16)
            sp.dma_start(delta[:], A["delta"]).then_inc(in_w, 16)
            sp_prep(sp, 0)
            sp.dma_start(pw[:], A["pw"]).then_inc(in_pw, 16)
            with sp.Fori(0, B) as b:
                for k in range(STAGES_PER_BATCH):
                    n = b * STAGES_PER_BATCH + k
                    sp.wait_ge(fsp["lo"], n + 1)
                    sp.dma_start(stage, A["fw"][:, bass.ds(n * STAGE, STAGE)]).then_inc(fsp["ld"], 16)
            for l in range(1, 4):
                if ("a", l) in order:
                    sp_prep(sp, l)
                    if l == 1:
                        sp.wait_ge(done, 2 * B)
                        sp.dma_start(negm, A["maskT"]).then_inc(m1["in_"], 16)
            sp.wait_ge(done, B * len(order))
            sp.dma_start(out, x[:]).then_inc(out_s, 16)
            sp.wait_ge(out_s, 16)

        @block.gpsimd
        def _(pool):
            nc.gpsimd.memset(mhalf[:], -0.5).then_inc(const, 1)
            nc.gpsimd.memset(epst[:], LN_EPS).then_inc(const, 1)
            nc.gpsimd.memset(ones[:], 1.0).then_inc(const, 1)
            nc.gpsimd.memset(nm[:], 0.0).then_inc(const, 1)
            nc.gpsimd.memset(stage, 0.0).then_inc(fsp["lo"], 1)
            pool.wait_ge(const, 4)
            pool.wait_ge(c0["var"], 1)
            nc.gpsimd.tensor_scalar(cve[:], cmv[:, :, 1], LN_EPS, 1.0, ALU.add, ALU.mult).then_inc(c0["ep"], 1)
            pool.wait_ge(c0["ep"], 1)
            nc.gpsimd.tensor_tensor(crs[:], cve[:], mhalf[0:KC, :], ALU.pow).then_inc(c0["rstd"], 1)
            pool.wait_ge(c0["xh"], 2)
            nc.gpsimd.tensor_tensor(cxl[:], cxf[:], cxh[:], ALU.subtract).then_inc(c0["xl"], 1)
            nc.gpsimd.tensor_tensor(cl[:], ctxT[:], ch[:], ALU.subtract).then_inc(c0["xl"], 1)
            pool_prep(pool, 0)
            for k, i in order:
                if k == "a" and i:
                    pool_prep(pool, i)
                if k == "a" and i < 2:
                    pool_norm(pool, norm_of(2 * i, 0))
                if k == "a":
                    batches(pool, 2 * i, lambda b, m, nx: pool_attn0(pool, b, m, nx) if i == 0 else pool_attn(pool, i, b, m, nx))
                else:
                    batches(pool, 2 * i + 1, lambda b, m, nx: pool_norm(pool, nx) if nx else None)

        @block.scalar
        def _(act):
            act.wait_ge(in_c, 16 * 11)
            act.wait_ge(c0["neg"], 1)
            nc.scalar.activation(tg[:], col("gate"), ACT.Tanh).then_inc(tgs, 1)
            nc.scalar.activation(ch[:], ctxT[:], ACT.Copy).then_inc(c0["xh"], 1)
            act.wait_ge(c0["tp"], 1)
            nc.scalar.activation(cxf[:], bank(7, KA), ACT.Identity, bias=col("beta_media"), scale=col("gamma_media")).then_inc(c0["xt"], 1)
            act.wait_ge(c0["xt"], 1)
            nc.scalar.activation(cxh[:], cxf[:], ACT.Copy).then_inc(c0["xh"], 1)
            act_prep(act, 0)
            for k, i in order:
                if k == "a":
                    if i:
                        act_prep(act, i)
                    if i < 2:
                        act_norm(act, norm_of(2 * i, 0))
                    batches(act, 2 * i, lambda b, m, nx: act_attn0(act, b, m, nx) if i == 0 else act_attn(act, i, b, m, nx))
                else:
                    (act_f0, act_f1, act_f2, act_f3)[i](act)

        @block.vector
        def _(dve):
            dve.wait_ge(in_c, 16 * 11)
            for b in range(B):
                last = nc.vector.bn_stats(cst[:, b, :], crow[:, b, :])
            last.then_inc(c0["st"], 1)
            dve.wait_ge(c0["st"], 1)
            for b in range(B):
                last = nc.vector.bn_aggr(cmv[:, b, :], cst[:, b, :])
            last.then_inc(c0["var"], 1)
            dve.wait_ge(in_mask, 32)
            nc.vector.tensor_scalar(negk[:], mk8[:], NEG_INF, None, ALU.mult)
            nc.vector.tensor_scalar(negr[:], mr8[:], NEG_INF, None, ALU.mult).then_inc(c0["neg"], 1)
            dve.wait_ge(c0["rstd"], 1)
            for b in range(B):
                last = nc.vector.tensor_scalar(crow[:, b, :], crow[:, b, :], cmv[:, b, 0:1], crs[:, b:b + 1], ALU.subtract, ALU.mult)
            last.then_inc(c0["xn"], 1)
            dve.wait_ge(tgs, 1)
            nc.vector.tensor_scalar(btg[:], rowv("b_out"), tg[:, 0:1], None, ALU.mult).then_inc(tgs, 1)
            dve_prep(dve, 0)
            for k, i in order:
                if k == "a":
                    if i:
                        dve_prep(dve, i)
                    if i < 2:
                        dve_norm(dve, norm_of(2 * i, 0))
                    batches(dve, 2 * i, lambda b, m, nx: dve_attn0(dve, b, m, nx) if i == 0 else dve_attn(dve, i, b, m, nx))
                else:
                    (dve_f0, dve_f1, dve_f2, dve_f3)[i](dve)

        @block.tensor
        def _(pe):
            pe.wait_ge(in_w, 16 * 5)
            pe.wait_ge(const, 4)
            pe.wait_ge(c0["xn"], 1)
            for b in range(B):
                last = nc.tensor.transpose(bank(7, KC, off=KC * b), crow[:, b, :], identf[0:KC, 0:KC])
            last.then_inc(c0["tp"], 1)
            pe_prep(pe, 0)
            for k, i in order:
                if k == "a":
                    if i:
                        pe_prep(pe, i)
                    if i == 1:
                        pe.wait_ge(m1["bqe"], 1)
                    if i < 2:
                        pe_norm(pe, norm_of(2 * i, 0))
                    batches(pe, 2 * i, lambda b, m, nx: pe_attn0(pe, b, m, nx) if i == 0 else pe_attn(pe, i, b, m, nx))
                else:
                    pe.wait_ge(done, F[i]["first"])
                    (pe_f0, pe_f1, pe_f2, pe_f3)[i](pe)


def layout(inputs):
    import numpy as np
    bf16 = mybir.dt.np(mybir.dt.bfloat16)
    I = {k: np.asarray(v) for k, v in inputs.items()}
    f = np.float32
    t = {}
    t["x"] = I["x"].reshape(B, QT, 128, D).transpose(2, 0, 1, 3)
    c = I["ctx_1024"]
    t["ctxT"] = c.reshape(KA, D).T
    t["ctxr"] = c.transpose(1, 0, 2)
    mask = I["mask_BxS2_bk0"]
    t["mk8"] = mask.T
    t["mr8"] = mask.reshape(1, KA)
    t["maskT"] = I["mask_1x1xSxS2_fk1"].reshape(S, KC).T

    def whole(v):
        return np.broadcast_to(v.reshape(1, -1), (128, v.size))

    def hidden2(v, sv):
        w = np.concatenate([v, sv[None]], 0)
        return w[:, 0::2].T, w[:, 1::2].T
    b1e, b1o = hidden2(I["L2_ffn_b1"], I["L2_ffn_sb1"])
    b3e, b3o = hidden2(I["L2_ffn_b3"], I["L2_ffn_sb3"])
    hb = np.stack([b1e, b1o, b3e, b3o], 2).reshape(128, 36)
    t["cols"] = np.concatenate([I["L0_xattn_gamma_media"][:, None], I["L0_xattn_beta_media"][:, None],
                                I["L0_xattn_gamma_lat"][:, None], I["L0_xattn_beta_lat"][:, None],
                                I["L3_xattn_ln_gamma"][:, None], I["L3_xattn_ln_beta"][:, None],
                                whole(I["L0_xattn_kv_gate"]), whole(I["L3_xattn_gate"]),
                                I["L0_ffn_b1"].reshape(2, 128).T, hb], 1)
    t["rowc"] = np.concatenate([whole(I[n]) for n in ("L0_ffn_w_gate_b", "L1_ffn_expert_bias", "L2_ffn_gate_b", "L3_ffn_router_b",
                                                      "L1_xattn_bo", "L3_xattn_b_out", "L1_xattn_bv")], 1)
    bk, bq = I["L1_xattn_bk"].reshape(16, 8), I["L1_xattn_bq"].reshape(16, 8)
    t["bkq"] = np.stack([bk.T, bq.T], 1)
    t["bkqT"] = np.concatenate([bk, bq], 1)
    t["b2c"] = np.concatenate([I["L2_ffn_b2"], I["L2_ffn_sb2"][None]], 0)
    z = np.zeros((B, 8, B, D), f)
    for b in range(B):
        z[b, :, b, :] = I["L0_ffn_b2"]
    t["b2s"] = z.reshape(32, B, D)

    def heads(wq, wk, n):
        return np.stack([wk.reshape(D, n, -1).transpose(2, 1, 0), wq.reshape(D, n, -1).transpose(2, 1, 0)], 1)
    wk3, wv3 = I["L3_xattn_w_kv"][:, :1024], I["L3_xattn_w_kv"][:, 1024:]
    t["g0"] = heads(I["L0_xattn_Wq"], I["L0_xattn_Wk"], 8)
    t["g1"] = heads(I["L1_xattn_Wq"].T, I["L1_xattn_Wk"].T, 16)
    t["g2"] = heads(I["L2_xattn_Wq"].T, I["L2_xattn_Wk"].T, 16)
    t["g3"] = heads(I["L3_xattn_w_q"], wk3, 16)

    def chunks(w):
        return w.reshape(-1, 128, w.shape[1]).transpose(1, 0, 2).reshape(128, -1)
    w22 = np.concatenate([I["L2_ffn_w2"], I["L2_ffn_sw2"][None]], 0)
    t["pw"] = np.concatenate([I["L0_xattn_Wv"], I["L1_xattn_Wv"].T, I["L2_xattn_Wv"].T, wv3,
                              chunks(I["L0_xattn_Wout"]), I["L1_xattn_Wo"].T, I["L2_xattn_Wo"].T, chunks(I["L3_xattn_w_out"]),
                              chunks(I["L0_ffn_W2"].reshape(256, D)), chunks(I["L1_ffn_shared_w3"].T),
                              I["L1_ffn_w3"].transpose(2, 0, 1).reshape(128, -1), w22.transpose(2, 0, 1).reshape(128, -1)], 1)
    w1 = np.concatenate([I["L2_ffn_w1"], I["L2_ffn_sw1"][None]], 0)
    w3 = np.concatenate([I["L2_ffn_w3"], I["L2_ffn_sw3"][None]], 0)
    f2 = np.stack([w1[:, 0::2], w1[:, 1::2], w3[:, 0::2], w3[:, 1::2]], 1)
    t["fw"] = np.concatenate([I["L0_ffn_w_gate_w"], I["L0_ffn_W1"].transpose(1, 0, 2).reshape(D, 256),
                              I["L1_ffn_router_w"].T, I["L1_ffn_shared_w1"].T, I["L1_ffn_shared_w2"].T,
                              I["L1_ffn_w12"].transpose(2, 0, 1).reshape(D, -1),
                              I["L2_ffn_gate_w"].T, f2.transpose(3, 0, 1, 2).reshape(D, -1),
                              I["L3_ffn_router_w"].T, I["L3_ffn_expert_w"].transpose(1, 0, 2).reshape(D, -1),
                              np.zeros((D, B * STAGES_PER_BATCH * STAGE - NFW), f)], 1)
    t["identf"] = np.eye(128, dtype=f)
    t["identb"] = np.eye(128, dtype=bf16)
    s0 = np.zeros((ROWS, 16), bf16)
    for h in range(16):
        for p in (0, 32, 64):
            s0[p + h, h] = -1.0
    t["sel0"] = s0
    ex = np.zeros((B, 8, B, 2, 128), bf16)
    for b in range(B):
        for e in range(8):
            ex[b, e, b, e // 4, 32 * (e % 4):32 * (e % 4) + 32] = 1.0
    t["expd"] = ex.reshape(32, B, 2, 128)
    t["delta"] = np.eye(16, dtype=f)
    t["tri"] = np.broadcast_to(np.tril(np.ones((16, 16), f), -1).reshape(1, 256), (128, 256))
    t["tri8"] = np.broadcast_to(np.tril(np.ones((8, 8), f), -1).reshape(1, 64), (128, 64))
    bits = np.zeros((32, 32), np.int32)
    for i in range(BITS):
        bits[:, i] = 1 << (BITS - 1 - i)
    t["bits"] = bits
    return {k: np.ascontiguousarray(v) for k, v in t.items()}


def kernel(**inputs):
    import numpy as np
    import concourse.bacc as bacc
    from concourse.bass_utils import run_bass_kernel_spmd

    nc = bacc.Bacc("TRN2", target_bir_lowering=False, num_devices=1)
    arrays = layout(inputs)
    feeds, aps = {}, {}
    for name, a in arrays.items():
        feeds[f"in_{name}"] = a
        aps[name] = nc.dram_tensor(f"in_{name}", a.shape, mybir.dt.from_np(a.dtype), kind="ExternalInput").ap()
    out = nc.dram_tensor("out_x", (128, B, QT, D), F32, kind="ExternalOutput").ap()
    build(nc, aps, out)
    r = run_bass_kernel_spmd(nc, [feeds], core_ids=[0])
    return np.ascontiguousarray(r.results[0]["out_x"].transpose(1, 2, 0, 3)).reshape(B, S, D)
```

```python
from contextlib import ExitStack

import concourse.bass as bass
from concourse import mybir

ALU = mybir.AluOpType
ACT = mybir.ActivationFunctionType
AX = mybir.AxisListType.X
F32 = mybir.dt.float32
BF16 = mybir.dt.bfloat16
I32 = mybir.dt.int32

B = 4
S = 512
QT = S // 128
D = 128
KC = 77
KA = B * KC
BANK = 512
ROWS = 81
LN_EPS = 1e-5
NEG = -1e9
NEG_INF = -1e30
KEEP = S // 2
BITS = 31
UNROLL = 4

COLS = {}
_at = 0
for _n, _w in (("gamma_media", 1), ("beta_media", 1), ("gamma_lat", 1), ("beta_lat", 1), ("ln_gamma", 1), ("ln_beta", 1),
               ("kv_gate", 1), ("gate", 1), ("b1", 2), ("hb", 36)):
    COLS[_n] = (_at, _w)
    _at += _w
NCOLS = _at
ROWC = {}
_at = 0
for _n, _w in (("w_gate_b", 8), ("expert_bias", 8), ("gate_b", 8), ("router_b", 16), ("bo", 128), ("b_out", 128), ("bv", 128)):
    ROWC[_n] = (_at, _w)
    _at += _w
NROWC = _at
FW = {"f0": 8 + 256, "f1": 8 + 1024 + 2048, "f2": 8 + 9 * 512, "f3": 16 + 2048}
FOFF = {"f0": 0, "f1": FW["f0"], "f2": FW["f0"] + FW["f1"], "f3": FW["f0"] + FW["f1"] + FW["f2"]}
NFW = sum(FW.values())
STAGES_PER_BATCH = 3
STAGE = -(-NFW // (B * STAGES_PER_BATCH))
PW = {}
_at = 0
for _n, _w in (("wv0", 512), ("wv1", 128), ("wv2", 128), ("wv3", 1024), ("wo0", 512), ("wo1", 128), ("wo2", 128), ("wo3", 1024),
               ("w2_0", 256), ("sw3", 512), ("w3", 1024), ("w2_2", 1152)):
    PW[_n] = (_at, _w)
    _at += _w
NPW = _at


def build(nc, A, out):
    with ExitStack() as ctx:
        def sb(name, shape, dt=F32):
            return ctx.enter_context(nc.sbuf_tensor(name, shape, dt))

        def sem(name):
            return ctx.enter_context(nc.semaphore(name))

        def sems(prefix, names):
            return {n: sem(prefix + n) for n in names.split()}

        x = sb("x", [128, B, QT, D])
        xn = sb("xn", [128, QT, D])
        xt = sb("xt", [128, S])
        xh = sb("xh", [128, B, S], BF16)
        xl = sb("xl", [128, B, S], BF16)
        stats = sb("stats", [128, QT, 6])
        mv = sb("mv", [128, QT, 2])
        veps = sb("veps", [128, QT])
        rstd = sb("rstd", [128, QT])
        mhalf = sb("mhalf", [128, QT])
        epst = sb("epst", [128, QT])
        tick = sb("tick", [128, 1])
        identf = sb("identf", [128, 128])
        identb = sb("identb", [128, 128], BF16)
        ones = sb("ones", [ROWS, S], BF16)
        cols = sb("cols", [128, NCOLS])
        rowc = sb("rowc", [128, NROWC])
        pw = sb("pw", [128, NPW])
        fh = sb("fh", [128, B * STAGES_PER_BATCH * STAGE], BF16)
        fl = sb("fl", [128, B * STAGES_PER_BATCH * STAGE], BF16)
        ctxT = sb("ctxT", [128, KA])
        ch = sb("ch", [128, KA], BF16)
        cl = sb("cl", [128, KA], BF16)
        Gh = sb("Gh", [128, 16, 128], BF16)
        Gl = sb("Gl", [128, 16, 128], BF16)
        Mh = sb("Mh", [128, 16, KA], BF16)
        Ml = sb("Ml", [128, 16, KA], BF16)
        sel0 = sb("sel0", [128, 16], BF16)
        Vh = sb("Vh", [128, 4160], BF16)
        Vl = sb("Vl", [128, 4160], BF16)
        P4 = sb("P4", [128, 5, S])
        Pf = [P4[:, i, :] for i in range(2)]
        Ph = [P4[:, 2, 0:256].bitcast(BF16), P4[:, 2, 256:512].bitcast(BF16), P4[:, 3, 0:256].bitcast(BF16)]
        Pl = [P4[:, 3, 256:512].bitcast(BF16), P4[:, 4, 0:256].bitcast(BF16), P4[:, 4, 256:512].bitcast(BF16)]
        nm = sb("nm", [128, QT, ROWS + 15], BF16)
        nmT = sb("nmT", [128, S], BF16)
        mx = sb("mx", [128, QT, 16])
        mr1 = sb("mr1", [128, QT, 16])
        mr2 = sb("mr2", [128, QT, 16])
        rec = sb("rec", [128, QT, 16])
        attn = sb("attn", [128, QT, 1024])
        gw = attn[0:64, :, :].rearrange("p q d -> p (q d)").rearrange("p (k h d) -> p k h d", k=2, h=16)
        aT = sb("aT", [128, 2, S])
        work = sb("work", [128, 12 * 512])

        ps = ctx.enter_context(nc.psum_tensor("ps", [128, 8 * BANK], F32))

        def bank(i, n=BANK, rows=128, off=0):
            return ps[0:rows, i * BANK + off:i * BANK + off + n]

        def col(name, i=0):
            return cols[:, COLS[name][0] + i:COLS[name][0] + i + 1]

        def rowv(name):
            return rowc[:, ROWC[name][0]:ROWC[name][0] + ROWC[name][1]]

        def pwv(name):
            return pw[:, PW[name][0]:PW[name][0] + PW[name][1]]

        kgf = work[:, 0:512]
        kgh = work[:, 512:1536].bitcast(BF16).rearrange("p (b k) -> p b k", b=B)
        kgl = work[:, 1536:2560].bitcast(BF16).rearrange("p (b k) -> p b k", b=B)
        MX = work[:, 2560:3072].bitcast(BF16).rearrange("p (h k) -> p h k", h=2)
        MLh = work[:, 3072:3584].bitcast(BF16).rearrange("p (h k) -> p h k", h=2)
        MLl = work[:, 3584:4096].bitcast(BF16).rearrange("p (h k) -> p h k", h=2)
        negm = Vl[0:KC, 2080:3104].bitcast(F32)
        mres = Vl[0:KC, 3104:4128].bitcast(F32)
        mpart = [Vh[0:KC, 2080 + 512 * i:2592 + 512 * i] for i in range(3)]
        bqm = attn[0:16, :, 128:744].bitcast(BF16).rearrange("p b (h k) -> p b h k", h=16)
        masked = [work[0:KC, 512 * i:512 * i + 512] for i in range(3)]
        crow = sb("crow", [KC, B, D])
        cxf = sb("cxf", [128, KA])
        negk = sb("negk", [KC, B])
        negb = sb("negb", [KC, 1])
        negr = sb("negr", [1, KA], BF16)
        mk8 = sb("mk8", [KC, B], mybir.dt.uint8)
        mr8 = sb("mr8", [1, KA], mybir.dt.uint8)
        cst = sb("cst", [KC, B, 6])
        cmv = sb("cmv", [KC, B, 2])
        cve = sb("cve", [KC, B])
        crs = sb("crs", [KC, B])
        bkq = sb("bkq", [8, 2, 16])
        delta = sb("delta", [16, 16])
        b2c = sb("b2c", [9, 128])
        b2s = sb("b2s", [32, B, 128])
        tri = sb("tri", [128, 256])
        bits = sb("bits", [32, 32], I32)
        expd = sb("expd", [32, B, 2, 128], BF16)

        in_x = sem("in_x")
        in_c = sem("in_c")
        in_w = sem("in_w")
        in_mask = sem("in_mask")
        in_pw = sem("in_pw")
        out_s = sem("out_s")
        const = sem("const")
        N = sems("n_", "st var ep rstd xn tp xt xh xl st2 var2 ep2 rstd2 xn2")
        R = sems("p_", "gld gp gh gl mp mh ml vp ve vh vc vm")
        ATT = "mxp mx sT ex pl pv rc on"
        Z = sems("z_", "nmc nm nmt nmT atp at op")
        done = sem("done")
        L = [sems(f"a{i}_", ATT + (" res" if i % 2 else "")) for i in range(4)]
        kq = sems("kq_", "kg kgh kgl nb")
        c0 = sems("c_", "st var ep rstd xn tp xt xh xl neg")
        m1 = sems("m_", "in_ chain up us pr bq bqf bqb sm")

        block = ctx.enter_context(nc.Block())
        order = [("a", 0), ("f", 0), ("a", 1), ("f", 1), ("a", 2), ("f", 2), ("a", 3), ("f", 3)]

        DIM = [64, 8, 8, 64]
        NH = [8, 16, 16, 16]
        WV = [512, 128, 128, 1024]
        GB = [sum(NH[:l]) // 4 for l in range(4)]
        HB = [sum(NH[:l]) for l in range(4)]
        CB = [sum(B * NH[k] * DIM[k] // 128 for k in range(l)) for l in range(4)]
        VB = [sum(B * ((w + 511) // 512) for w in WV[:l]) for l in range(4)]
        SC = [0.125, 8 ** -0.5, 8 ** -0.5, 0.125]

        def norm_of(i, b, first=False):
            return {"first": first, "n": B * i + b, "n2": (B if i == 6 else 0) + b, "b": b, "i": i, "double": i in (0, 6),
                    "gamma": {0: "gamma_lat", 6: "ln_gamma"}.get(i), "beta": {0: "beta_lat", 6: "ln_beta"}.get(i)}

        def batches(eng, i, body):
            with eng.Fori(0, B - 1) as b:
                body(b, norm_of(i, b), norm_of(i, b + 1))
            body(B - 1, norm_of(i, B - 1), None if i in (1, len(order) - 1) else norm_of(i + 1, 0))

        def dve_stats(dve, m, second=False):
            st, var, n = (N["st2"], N["var2"], m["n2"]) if second else (N["st"], N["var"], m["n"])
            if second:
                dve.wait_ge(N["xn"], m["n"] + 1)
            elif m["i"] == 0:
                dve.wait_ge(in_x, 16)
            else:
                dve.wait_ge(done, m["n"] - B + 1)
            src = xn[:, :, :] if second else x[:, m["b"], :, :]
            for j in range(QT):
                last = nc.vector.bn_stats(stats[:, j, :], src[:, j, :])
            last.then_inc(st, 1)
            dve.wait_ge(st, n + 1)
            nc.vector.memset(tick[:], 0.0)
            for j in range(QT):
                last = nc.vector.bn_aggr(mv[:, j, :], stats[:, j, :])
            last.then_inc(var, 1)

        def dve_scale(dve, m, second=False):
            rs, out_, n = (N["rstd2"], N["xn2"], m["n2"]) if second else (N["rstd"], N["xn"], m["n"])
            dve.wait_ge(rs, n + 1)
            if not second and not m["first"]:
                dve.wait_ge(N["tp"], m["n"])
            src = xn[:, :, :] if second else x[:, m["b"], :, :]
            for j in range(QT):
                last = nc.vector.tensor_scalar(xn[:, j, :], src[:, j, :], mv[:, j, 0:1], rstd[:, j:j + 1],
                                               ALU.subtract, ALU.mult)
            last.then_inc(out_, 1)

        def dve_norm(dve, m):
            dve_stats(dve, m)
            dve_scale(dve, m)
            if m["double"]:
                dve_stats(dve, m, True)
                dve_scale(dve, m, True)

        def pool_rstd(pool, m, second=False):
            var, ep, rs, n = (N["var2"], N["ep2"], N["rstd2"], m["n2"]) if second else (N["var"], N["ep"], N["rstd"], m["n"])
            pool.wait_ge(var, n + 1)
            nc.gpsimd.tensor_tensor(veps[:], mv[:, :, 1], epst[:], ALU.add).then_inc(ep, 1)
            pool.wait_ge(ep, n + 1)
            nc.gpsimd.tensor_tensor(rstd[:], veps[:], mhalf[:], ALU.pow).then_inc(rs, 1)

        def pool_low(pool, m):
            pool.wait_ge(N["xh"], m["n"] + 1)
            nc.gpsimd.tensor_tensor(xl[:, m["b"], :], xt[:], xh[:, m["b"], :], ALU.subtract).then_inc(N["xl"], 1)

        def pool_norm(pool, m):
            pool_rstd(pool, m)
            if m["double"]:
                pool_rstd(pool, m, True)
            pool_low(pool, m)

        def pe_norm(pe, m):
            pe.wait_ge(N["xn2"] if m["double"] else N["xn"], (m["n2"] if m["double"] else m["n"]) + 1)
            for j in range(QT):
                last = nc.tensor.transpose(bank(7, 128, off=128 * j), xn[:, j, :], identf[:])
            last.then_inc(N["tp"], 1)

        def act_norm(act, m):
            act.wait_ge(N["tp"], m["n"] + 1)
            if not m["first"]:
                act.wait_ge(N["xl"], m["n"])
            if m["gamma"]:
                nc.scalar.activation(xt[:], bank(7), ACT.Identity, bias=col(m["beta"]), scale=col(m["gamma"])).then_inc(N["xt"], 1)
            else:
                nc.scalar.activation(xt[:], bank(7), ACT.Copy).then_inc(N["xt"], 1)
            act.wait_ge(N["xt"], m["n"] + 1)
            nc.scalar.activation(xh[:, m["b"], :], xt[:], ACT.Copy).then_inc(N["xh"], 1)

        def keys_parts(l):
            return (ch, cl) if l else (cxh, cxl)

        cxh = sb("cxh", [128, KA], BF16)
        cxl = sb("cxl", [128, KA], BF16)

        def v_steps(l):
            w = NH[l] * DIM[l]
            for b in range(B):
                for c in range(0, w, 512):
                    n = min(512, w - c)
                    hh = n // DIM[l]
                    d1 = DIM[l] + 1
                    o = (b * NH[l] + c // DIM[l]) * d1
                    yield b, c, n, [v[0:KC, o:o + hh * d1].rearrange("p (h d) -> p h d", d=d1)[:, :, 0:DIM[l]] for v in (Vh, Vl)]

        def sp_prep(sp, l):
            if l:
                sp.wait_ge(Z["atp"], CB[l])
            sp.dma_start(gw[0:DIM[l], :, 0:NH[l], :], A[f"g{l}"]).then_inc(R["gld"], 16)

        def pe_prep(pe, l):
            kh, kl = keys_parts(l)
            pe.wait_ge(R["gld"], 16 * (l + 1))
            J = DIM[l]
            if l == 1:
                for i in range(2):
                    for h in range(16):
                        last = nc.tensor.matmul(bank(7, 1, off=16 * i + h), gw[0:8, 1 - i, h, :], bkq[:, i, h:h + 1],
                                                start=True, stop=True)
                last.then_inc(m1["up"], 1)
            for g in range(NH[l] // 4):
                if g >= 2:
                    pe.wait_ge(R["gh"], GB[l] + g - 1)
                    pe.wait_ge(R["gl"], GB[l] + g - 1)
                for i in range(4):
                    h = 4 * g + i
                    last = nc.tensor.matmul(bank(g % 2, 128, off=128 * i), gw[0:J, 0, h, :], gw[0:J, 1, h, :],
                                            start=True, stop=True)
                last.then_inc(R["gp"], 1)
            if l == 0:
                pe.wait_ge(c0["xl"], 1)
            for h in range(NH[l]):
                if h % 4 == 0:
                    pe.wait_ge(R["gh"], GB[l] + h // 4 + 1)
                    pe.wait_ge(R["gl"], GB[l] + h // 4 + 1)
                if h >= 2:
                    pe.wait_ge(R["mh"], HB[l] + h - 1)
                    pe.wait_ge(R["ml"], HB[l] + h - 1)
                o = bank(2 + h % 2, KA)
                nc.tensor.matmul(o, Gh[:, h, :], kh[:], start=True, stop=False)
                nc.tensor.matmul(o, Gh[:, h, :], kl[:], start=False, stop=False)
                nc.tensor.matmul(o, Gl[:, h, :], kh[:], start=False, stop=True).then_inc(R["mp"], 1)
            kf = ctxT if l else cxf
            pe.wait_ge(in_pw, 16)
            for n, (b, c, w, dst) in enumerate(v_steps(l)):
                if n >= 2 and l != 1:
                    pe.wait_ge(R["ve"], VB[l] + n - 1)
                wv = pwv(f"wv{l}")
                nc.tensor.matmul(bank(5, w, KC, off=w * n) if l == 1 else bank(5 + n % 2, w, KC), kf[:, b * KC:(b + 1) * KC], wv[:, c:c + w],
                                 start=True, stop=True).then_inc(R["vp"], 1)
            if l == 1:
                pe.wait_ge(m1["us"], 1)
                pe.wait_ge(m1["pr"], 3)
                nc.tensor.matmul(bank(7, KA, 16), uws[:, 16:32], ctxT[:], start=True, stop=False)
                nc.tensor.matmul(bank(7, KA, 16), prod, ones8, start=False, stop=True).then_inc(m1["bq"], 1)
                for b in range(B):
                    o = bank(6, 16, KC, off=16 * b)
                    nc.tensor.matmul(o, ctxT[:, b * KC:(b + 1) * KC], uws[:, 16:32], start=True, stop=False)
                    last = nc.tensor.matmul(o, ones8[:, 0:KC], prod, start=False, stop=True)
                last.then_inc(m1["bq"], 1)

        full = [aT[:, 1, :], P4[:, 4, :]]
        uws = cxh[:, 0:64].bitcast(F32)
        prod = cxl[0:8, 0:32].bitcast(F32)
        bqT = cxl[0:KC, 96:224].bitcast(F32).rearrange("p (b h) -> p b h", b=B)
        ones8 = cxf[0:8, :]
        bqf = cxf[0:16, :]
        bqb = crow[:, 0, 0:16]

        def act_prep(act, l):
            if l == 1:
                act.wait_ge(m1["up"], 1)
                nc.scalar.activation(uws, bank(7, 32), ACT.Copy, scale=SC[1]).then_inc(m1["us"], 1)
            for g in range(NH[l] // 4):
                act.wait_ge(R["gp"], GB[l] + g + 1)
                o = bank(g % 2)
                hi = nc.scalar.activation(Gh[:, 4 * g:4 * g + 4, :], o.rearrange("p (h d) -> p h d", h=4), ACT.Copy, scale=SC[l])
                if l == 1:
                    if g >= 2:
                        act.wait_ge(R["gl"], GB[l] + g - 1)
                    hi = nc.scalar.activation(full[g % 2], o, ACT.Copy, scale=SC[l])
                hi.then_inc(R["gh"], 1)
            if l == 1:
                act.wait_ge(m1["us"], 1)
            for h in range(NH[l]):
                act.wait_ge(R["mp"], HB[l] + h + 1)
                o = bank(2 + h % 2, KA)
                if l == 1:
                    nc.scalar.activation(Mh[:, h, :], o, ACT.Identity, bias=uws[:, h:h + 1])
                    if h < 2:
                        act.wait_ge(R["gl"], GB[l] + 4)
                    else:
                        act.wait_ge(R["ml"], HB[l] + h - 1)
                    nc.scalar.activation(full[h % 2][:, 0:KA], o, ACT.Identity, bias=uws[:, h:h + 1]).then_inc(R["mh"], 1)
                else:
                    nc.scalar.activation(Mh[:, h, :], o, ACT.Copy).then_inc(R["mh"], 1)
            if l == 1:
                act.wait_ge(R["vp"], VB[l] + B)
                act.wait_ge(R["ml"], HB[l] + 16)
                nc.scalar.activation(full[0][0:KC, :], bank(5, S, KC), ACT.Copy).then_inc(R["vc"], 1)
                act.wait_ge(m1["bq"], 2)
                nc.scalar.activation(bqT, bank(6, B * 16, KC).rearrange("p (b h) -> p b h", b=B), ACT.Copy)
                nc.scalar.activation(bqf, bank(7, KA, 16), ACT.Copy).then_inc(m1["bqf"], 1)
            if l != 1:
                act.wait_ge(R["vm"], l + 1)
                for n, (b, c, w, dst) in enumerate(v_steps(l)):
                    act.wait_ge(R["vp"], VB[l] + n + 1)
                    src = bank(5 + n % 2, w, KC).rearrange("p (h d) -> p h d", d=DIM[l])
                    nc.scalar.activation(dst[0], src, ACT.Copy).then_inc(R["vh"], 1)

        def dve_prep(dve, l):
            for g in range(NH[l] // 4):
                dve.wait_ge(R["gh"], GB[l] + g + 1)
                o = Gl[:, 4 * g:4 * g + 4, :].rearrange("p h d -> p (h d)")
                nc.vector.scalar_tensor_tensor(o, bank(g % 2), SC[l], Gh[:, 4 * g:4 * g + 4, :].rearrange("p h d -> p (h d)"),
                                               ALU.mult, ALU.subtract).then_inc(R["gl"], 1)
            for h in range(NH[l]):
                dve.wait_ge(R["mh"], HB[l] + h + 1)
                nc.vector.tensor_tensor(Ml[:, h, :], bank(2 + h % 2, KA), Mh[:, h, :], ALU.subtract).then_inc(R["ml"], 1)
            dve.wait_ge(R["vm"], l + 1)
            for n, (b, c, w, dst) in enumerate(v_steps(l)):
                src = bank(5 + n % 2, w, KC).rearrange("p (h d) -> p h d", d=DIM[l])
                dve.wait_ge(R["vh"], VB[l] - (VB[2] - VB[1] if l > 1 else 0) + n + 1)
                nc.vector.tensor_tensor(dst[1], src, dst[0], ALU.subtract).then_inc(R["ve"], 1)

        def pool_prep(pool, l):
            if l:
                pool.wait_ge(L[l - 1]["pv"], B * (16 if l > 1 else 8 * 5))
            nc.gpsimd.memset(Vl[:], 0.0)
            nc.gpsimd.memset(Vh[:], 1.0).then_inc(R["vm"], 1)

        def pool_prep1(pool):
            l = 1
            nc.gpsimd.memset(ones8, 1.0).then_inc(m1["pr"], 1)
            nc.gpsimd.tensor_tensor(prod, bkq[:, 0, :], bkq[:, 1, :], ALU.mult).then_inc(m1["pr"], 1)
            pool.wait_ge(m1["pr"], 2)
            nc.gpsimd.tensor_scalar(prod, prod, SC[1], 1.0, ALU.mult, ALU.mult).then_inc(m1["pr"], 1)
            for g in range(4):
                pool.wait_ge(R["gh"], GB[l] + g + 1)
                nc.gpsimd.tensor_tensor(Gl[:, 4 * g:4 * g + 4, :].rearrange("p h d -> p (h d)"), full[g % 2],
                                        Gh[:, 4 * g:4 * g + 4, :].rearrange("p h d -> p (h d)"), ALU.subtract).then_inc(R["gl"], 1)
            for h in range(16):
                pool.wait_ge(R["mh"], HB[l] + h + 1)
                nc.gpsimd.tensor_tensor(Ml[:, h, :], full[h % 2][:, 0:KA], Mh[:, h, :], ALU.subtract).then_inc(R["ml"], 1)
            pool.wait_ge(R["vc"], 1)
            vf = full[0][0:KC, :].rearrange("p (b d) -> p b d", b=B)
            nc.gpsimd.tensor_tensor(vf, vf, rowv("bv")[0:KC, :].unsqueeze(1).to_broadcast([KC, B, 128]), ALU.add).then_inc(R["vc"], 1)
            pool.wait_ge(R["vc"], 2)
            vf = full[0][0:KC, :].rearrange("p (h d) -> p h d", d=8)
            vh, vl_ = [v[0:KC, 0:B * 16 * 9].rearrange("p (h d) -> p h d", d=9)[:, :, 0:8] for v in (Vh, Vl)]
            nc.gpsimd.tensor_copy(vh, vf).then_inc(R["vc"], 1)
            pool.wait_ge(R["vc"], 3)
            nc.gpsimd.tensor_tensor(vl_, vf, vh, ALU.subtract).then_inc(R["ve"], B)
            pool.wait_ge(m1["bqf"], 1)
            for b in range(B):
                last = nc.gpsimd.tensor_tensor(bqm[:, b, :, :], bqf[:, b * KC:(b + 1) * KC].unsqueeze(1).to_broadcast([16, 16, KC]),
                                               delta[:, :].unsqueeze(2).to_broadcast([16, 16, KC]), ALU.mult)
            last.then_inc(m1["chain"], 1)
            pool.wait_ge(m1["in_"], 16)
            n = 1
            nc.gpsimd.tensor_scalar(negm, negm, NEG, 1.0, ALU.mult, ALU.mult).then_inc(m1["chain"], 1)
            src = negm
            for i in range(3):
                n += 1
                pool.wait_ge(m1["chain"], n)
                nc.gpsimd.tensor_copy(mpart[i], src).then_inc(m1["chain"], 1)
                if i < 2:
                    n += 1
                    pool.wait_ge(m1["chain"], n)
                    nc.gpsimd.tensor_tensor(mres, src, mpart[i], ALU.subtract).then_inc(m1["chain"], 1)
                    src = mres

        GROUPS = [(0, 6), (6, 6), (12, 4)]

        def vslice(l, b, h):
            d1 = DIM[l] + 1
            return [v[0:KC, bass.ds((b * 16 + h) * d1, d1)] for v in (Vh, Vl)]

        MAX_STEPS = {8: (0, 1), 9: (2, 3), 10: (4, 5), 11: (6, 7), 12: (8,), 13: (9,), 14: (10,), 15: (11,)}

        def pe_max(pe, l, b, j):
            s = L[l]
            q, g = divmod(j, 3)
            h0, n = GROUPS[g]
            if j == 0:
                pe.wait_ge(N["xh"], s["first"] + b + 1)
            if j >= 2:
                pe.wait_ge(s["mx"], b * 12 + j - 1)
            xq = xh[:, b, 128 * q:128 * q + 128]
            o = bank(j % 2, n * KC).rearrange("p (h k) -> p h k", h=n)
            last = nc.tensor.matmul(o, xq, Mh[:, h0:h0 + n, bass.ds(b * KC, KC)], start=True, stop=l != 1)
            if l == 1:
                nc.tensor.matmul(o, ones[0:16, 0:128], bqm[:, b, h0:h0 + n, :], start=False, stop=False)
                for i in range(3):
                    last = nc.tensor.matmul(o, mpart[i][:, 128 * q:128 * q + 128],
                                            identb[0:KC, 0:KC].unsqueeze(1).to_broadcast([KC, n, KC]),
                                            start=False, stop=i == 2)
            last.then_inc(s["mxp"], 1)

        def dve_max(dve, l, b, j):
            s = L[l]
            q, g = divmod(j, 3)
            h0, n = GROUPS[g]
            dve.wait_ge(s["mxp"], b * 12 + j + 1)
            nc.vector.tensor_reduce(mx[:, q, h0:h0 + n], bank(j % 2, n * KC).rearrange("p (h k) -> p h k", h=n),
                                    AX, ALU.max).then_inc(s["mx"], 1)

        def ahead(m, nx):
            return nx is not None and nx["i"] == m["i"]

        def pe_attn(pe, l, b, m, nx):
            s = L[l]
            pe_shift(pe, s, b)
            pe.wait_ge(Z["nmT"], s["zb"] + b + 1)
            pe.wait_ge(N["xl"], s["first"] + b + 1)

            def scores(h):
                if h >= 3:
                    pe.wait_ge(m1["sm"] if l == 1 else s["ex"], b * 16 + h - 2)
                o = bank(2 + h % 3, S, KC)
                mh, ml = Mh[:, h, bass.ds(b * KC, KC)], Ml[:, h, bass.ds(b * KC, KC)]
                nc.tensor.matmul(o, mh, xh[:, b, :], start=True, stop=False)
                nc.tensor.matmul(o, mh, xl[:, b, :], start=False, stop=False)
                nc.tensor.matmul(o, ml, xh[:, b, :], start=False, stop=False)
                nc.tensor.matmul(o, sel0[:, h:h + 1].to_broadcast([128, KC]), nmT[:], start=False, stop=True).then_inc(s["sT"], 1)

            def values(h):
                pe.wait_ge(s["pl"], b * 16 + h + 1)
                d1 = DIM[l] + 1
                vh, vl_ = vslice(l, b, h)
                for q in range(QT):
                    if l == 3:
                        if h >= 2 and q == 0:
                            pe.wait_ge(s["on"], b * 16 + h - 1)
                        o = bank(5 + h % 2, d1, off=q * d1)
                    else:
                        o = bank(5 + q // 2, d1, off=(q % 2) * 16 * d1 + h * d1)
                    ph, pl = Ph[h % 3][0:KC, 128 * q:128 * q + 128], Pl[h % 3][0:KC, 128 * q:128 * q + 128]
                    nc.tensor.matmul(o, ph, vh, start=True, stop=False)
                    nc.tensor.matmul(o, ph, vl_, start=False, stop=False)
                    last = nc.tensor.matmul(o, pl, vh, start=False, stop=True)
                last.then_inc(s["pv"], 1)

            for h in range(3):
                scores(h)
            for h in range(16):
                if h < 13:
                    scores(h + 3)
                if ahead(m, nx):
                    for j in MAX_STEPS.get(h, ()):
                        pe_max(pe, l, nx["b"], j)
                values(h)
                if h == 5 and nx:
                    pe_norm(pe, nx)
            if nx:
                pe.wait_ge(N["xt"], nx["n"] + 1)
            pe_out(pe, s, b, NH[l] * DIM[l] // 128, f"wo{l}", 16 if l == 3 else 2)

        def pe_shift(pe, s, b):
            pe.wait_ge(Z["nm"], s["zb"] + b + 1)
            o = bank(0, 256).bitcast(BF16)
            for q in range(QT):
                last = nc.tensor.transpose(o[0:ROWS, 128 * q:128 * q + 128], nm[:, q, 0:ROWS], identb[:])
            last.then_inc(Z["nmt"], 1)

        def pe_out(pe, s, b, nchunk, wo, n_on):
            pe.wait_ge(s["on"], b * n_on + n_on)
            for c in range(nchunk):
                if c >= 2:
                    pe.wait_ge(Z["at"], s["cb"] + b * nchunk + c - 1)
                for q in range(QT):
                    last = nc.tensor.transpose(bank(c % 2, 128, off=128 * q), attn[:, q, 128 * c:128 * c + 128], identf[:])
                last.then_inc(Z["atp"], 1)
                if c:
                    pe_out_chunk(pe, s, b, c - 1, nchunk, wo)
            pe_out_chunk(pe, s, b, nchunk - 1, nchunk, wo)

        def pe_out_chunk(pe, s, b, c, nchunk, wo):
            pe.wait_ge(Z["at"], s["cb"] + b * nchunk + c + 1)
            for q in range(QT):
                last = nc.tensor.matmul(bank(7, 128, off=128 * q), aT[:, c % 2, 128 * q:128 * q + 128],
                                        pwv(wo)[:, 128 * c:128 * c + 128], start=(c == 0 and q == 0),
                                        stop=(c == nchunk - 1), skip_group_check=True)
            last.then_inc(Z["op"], 1)

        def act_out(act, s, b, nchunk):
            for c in range(nchunk):
                act.wait_ge(Z["atp"], s["cb"] + b * nchunk + c + 1)
                if c >= 2:
                    act.wait_ge(Z["op"], s["cb"] + b * nchunk + c - 1)
                nc.scalar.activation(aT[:, c % 2, :], bank(c % 2), ACT.Copy).then_inc(Z["at"], 1)

        def act_exp(act, s, n0, n, rows, bias=None, src=None):
            src = bank(3 + n % 2, S, rows) if src is None else src
            kw = {} if bias is None else {"bias": bias}
            if n >= 3:
                act.wait_ge(s["pv"], n0 + n - 2)
            nc.scalar.activation(Ph[n % 3][0:rows, :], src, ACT.Exp, **kw)
            if n >= 2:
                act.wait_ge(s["pl"], n0 + n - 1)
            nc.scalar.activation(Pf[n % 2][0:rows, :], src, ACT.Exp, **kw).then_inc(s["ex"], 1)

        def pool_attn(pool, l, b, m, nx):
            for h in range(16):
                pool_parts(pool, L[l], b * 16, h, KC)
                if h == 0 and nx:
                    pool_rstd(pool, nx)
                if h == 2 and nx and nx["double"]:
                    pool_rstd(pool, nx, True)
                if h == 10 and nx:
                    pool_low(pool, nx)

        def pool_parts(pool, s, n0, n, rows):
            pool.wait_ge(s["ex"], n0 + n + 1)
            nc.gpsimd.tensor_tensor(Pl[n % 3][0:rows, :], Pf[n % 2][0:rows, :], Ph[n % 3][0:rows, :],
                                    ALU.subtract).then_inc(s["pl"], 1)

        def act_attn(act, l, b, m, nx):
            s = L[l]
            if l == 1:
                nc.scalar.activation(bqb, bqT[:, b, :], ACT.Copy).then_inc(m1["bqb"], 1)
            act_shift(act, s, b)
            for h in range(16):
                if l == 1:
                    act.wait_ge(m1["sm"], b * 16 + h + 1)
                    act_exp(act, s, b * 16, h, KC, src=masked[h % 3])
                else:
                    act.wait_ge(s["sT"], b * 16 + h + 1)
                    act_exp(act, s, b * 16, h, KC, src=bank(2 + h % 3, S, KC))
                if h == 7 and nx:
                    act_norm(act, nx)
            act_out(act, s, b, NH[l] * DIM[l] // 128)

        def act_shift(act, s, b):
            act.wait_ge(Z["nmt"], s["zb"] + b + 1)
            nc.scalar.activation(nmT[0:ROWS, :], bank(0, 256).bitcast(BF16)[0:ROWS, :], ACT.Copy).then_inc(Z["nmT"], 1)

        def dve_shift(dve, s, b, H, steps):
            dve.wait_ge(s["mx"], b * steps + steps)
            nc.vector.tensor_copy(nm[:, :, 0:H], mx[:, :, 0:H]).then_inc(Z["nmc"], 1)
            dve.wait_ge(Z["nmc"], (s["zb"] + b) * 4 + 1)
            nc.vector.tensor_tensor(mr1[:, :, 0:H], mx[:, :, 0:H], nm[:, :, 0:H], ALU.subtract).then_inc(Z["nmc"], 1)
            dve.wait_ge(Z["nmc"], (s["zb"] + b) * 4 + 2)
            nc.vector.tensor_copy(nm[:, :, 32:32 + H], mr1[:, :, 0:H]).then_inc(Z["nmc"], 1)
            dve.wait_ge(Z["nmc"], (s["zb"] + b) * 4 + 3)
            nc.vector.tensor_tensor(mr2[:, :, 0:H], mr1[:, :, 0:H], nm[:, :, 32:32 + H], ALU.subtract).then_inc(Z["nmc"], 1)
            dve.wait_ge(Z["nmc"], (s["zb"] + b) * 4 + 4)
            nc.vector.tensor_copy(nm[:, :, 64:64 + H], mr2[:, :, 0:H]).then_inc(Z["nm"], 1)

        def dve_attn(dve, l, b, m, nx):
            s = L[l]
            if nx:
                dve_stats(dve, nx)
            if l == 3:
                for h in range(16):
                    if ahead(m, nx):
                        for j in MAX_STEPS.get(h, ()):
                            dve_max(dve, l, nx["b"], j)
                    dve_head(dve, s, b, h, 16, 1)
                    if h == 1 and nx:
                        dve_scale(dve, nx)
                        if nx["double"]:
                            dve_stats(dve, nx, True)
                    if h == 3 and nx and nx["double"]:
                        dve_scale(dve, nx, True)
            elif l == 1:
                def add_mask(h):
                    dve.wait_ge(s["sT"], b * 16 + h + 1)
                    if h >= 3:
                        dve.wait_ge(s["ex"], b * 16 + h - 2)
                    nc.vector.scalar_tensor_tensor(masked[h % 3], bank(2 + h % 3, S, KC), bqb[:, h:h + 1], negm,
                                                   ALU.add, ALU.add).then_inc(m1["sm"], 1)
                dve.wait_ge(m1["bqb"], b + 1)
                add_mask(0)
                add_mask(1)
                for h in range(16):
                    if h < 14:
                        add_mask(h + 2)
                    if h == 2 and nx:
                        dve_scale(dve, nx)
                    if ahead(m, nx):
                        for j in MAX_STEPS.get(h, ()):
                            dve_max(dve, l, nx["b"], j)
            else:
                if nx:
                    dve_scale(dve, nx)
                    if nx["double"]:
                        dve_stats(dve, nx, True)
                        dve_scale(dve, nx, True)
                if ahead(m, nx):
                    for j in range(3 * QT):
                        dve_max(dve, l, nx["b"], j)
            if l != 3:
                dve.wait_ge(s["pv"], b * 16 + 16)
                for i in range(2):
                    o = bank(5 + i, 288).rearrange("p (q h d) -> p q h d", q=2, d=9)
                    nc.vector.reciprocal(rec[:, 2 * i:2 * i + 2, :], o[:, :, :, 8]).then_inc(s["rc"], 1)
                    dve.wait_ge(s["rc"], b * 2 + i + 1)
                    nc.vector.tensor_tensor(attn[:, 2 * i:2 * i + 2, 0:128].rearrange("p q (h d) -> p q h d", d=8),
                                            o[:, :, :, 0:8], rec[:, 2 * i:2 * i + 2, :].unsqueeze(3).to_broadcast([128, 2, 16, 8]),
                                            ALU.mult).then_inc(s["on"], 1)
            if ahead(m, nx):
                dve_shift(dve, s, nx["b"], 16, 12)
            n = NH[l] * DIM[l] // 128
            dve.wait_ge(Z["op"], s["cb"] + b * n + n)
            dve_res(dve, l, s, b)

        def dve_head(dve, s, b, h, H, units):
            dve.wait_ge(s["pv"], (b * H + h + 1) * units)
            o = bank(5 + h % 2, QT * 65).rearrange("p (q d) -> p q d", d=65)
            nc.vector.reciprocal(rec[:, :, h], o[:, :, 64]).then_inc(s["rc"], 1)
            dve.wait_ge(s["rc"], b * H + h + 1)
            nc.vector.tensor_tensor(attn[:, :, 64 * h:64 * h + 64], o[:, :, 0:64],
                                    rec[:, :, h:h + 1].to_broadcast([128, QT, 64]), ALU.mult).then_inc(s["on"], 1)

        def dve_res(dve, l, s, b):
            xb = x[:, b, :, :].rearrange("p q d -> p (q d)")
            if l == 1:
                nc.vector.tensor_tensor(xb, bank(7), xb, ALU.add).then_inc(s["res"], 1)
                dve.wait_ge(s["res"], b + 1)
                nc.vector.tensor_tensor(x[:, b, :, :], x[:, b, :, :], rowv("bo").unsqueeze(1).to_broadcast([128, QT, D]),
                                        ALU.add).then_inc(done, 1)
            elif l == 3:
                nc.vector.scalar_tensor_tensor(xb, bank(7), tg[:, 0:1], xb, ALU.mult, ALU.add).then_inc(s["res"], 1)
                dve.wait_ge(s["res"], b + 1)
                nc.vector.tensor_tensor(x[:, b, :, :], x[:, b, :, :], btg[:].unsqueeze(1).to_broadcast([128, QT, D]),
                                        ALU.add).then_inc(done, 1)
            else:
                nc.vector.tensor_tensor(xb, bank(7), xb, ALU.add).then_inc(done, 1)

        tg = sb("tg", [128, 1])
        btg = sb("btg", [128, 128])
        tgs = sem("tgs")

        VLh, VLl = [v[:, 2080:4160].rearrange("p (c h d) -> p c h d", c=4, d=65) for v in (Vh, Vl)]
        vl = sems("v_", "p h e")
        kmp = sems("k_", "mp mh ml xp xh")
        fsp = sems("fs_", "ld hi lo")
        stage = work[:, 5120:5120 + STAGE]

        UNITS0 = 40
        STEPS0 = 32
        MAX0 = {}
        for _n in range(12, UNITS0):
            MAX0[_n] = [sum(map(len, MAX0.values()))]
            if _n % 7 == 1:
                MAX0[_n].append(MAX0[_n][0] + 1)
        assert sum(map(len, MAX0.values())) == STEPS0

        def keys0_at(n):
            return ([0] if n == 11 else []) + [j // 4 + 1 for j in MAX0.get(n, ()) if j % 4 == 1 and j < STEPS0 - 4]

        def pe_keys_max(pe, b, h):
            if h == 0:
                pe.wait_ge(kq["kgh"], b + 1)
            else:
                pe.wait_ge(kmp["xh"], b * 8 + h)
            nc.tensor.matmul(bank(7), Gh[:, h, :], kgh[:, b, :], start=True, stop=True).then_inc(kmp["xp"], 1)

        def act_keys_max(act, b, h):
            act.wait_ge(kmp["xp"], b * 8 + h + 1)
            nc.scalar.activation(MX[:, h % 2, :], bank(7), ACT.Copy).then_inc(kmp["xh"], 1)

        def pe_max0(pe, b, j):
            h, q = divmod(j, 4)
            if q == 0:
                pe.wait_ge(kmp["xh"], b * 8 + h + 1)
            xq = xh[:, b, 128 * q:128 * q + 128]
            nc.tensor.matmul(bank(0), xq, MX[:, h % 2, :], start=True, stop=True)
            o = bank(1, KC)
            nc.tensor.matmul(o, xq, Mh[:, h, bass.ds(b * KC, KC)], start=True, stop=False)
            nc.tensor.matmul(o, ones[0:1, 0:128], negr[:, bass.ds(b * KC, KC)], start=False, stop=True).then_inc(L[0]["mxp"], 1)

        def dve_max0(dve, b, j):
            h, q = divmod(j, 4)
            dve.wait_ge(L[0]["mxp"], b * STEPS0 + j + 1)
            nc.vector.tensor_reduce(mx[:, q, h:h + 1], ps[:, 0:512 + KC], AX, ALU.max).then_inc(L[0]["mx"], 1)

        def pe_first0(pe):
            pe.wait_ge(N["xh"], 1)
            pe_keys_max(pe, 0, 0)
            for j in range(STEPS0):
                if j:
                    pe.wait_ge(L[0]["mx"], j)
                pe_max0(pe, 0, j)
                if j % 4 == 1 and j < STEPS0 - 4:
                    pe_keys_max(pe, 0, j // 4 + 1)

        def pe_attn0(pe, b, m, nx):
            s = L[0]

            def keys(h):
                if h:
                    pe.wait_ge(kmp["ml"], b * 8 + h)
                nc.tensor.matmul(bank(2), Gh[:, h, :], kgh[:, b, :], start=True, stop=False)
                nc.tensor.matmul(bank(2), Gh[:, h, :], kgl[:, b, :], start=False, stop=False)
                nc.tensor.matmul(bank(2), Gl[:, h, :], kgh[:, b, :], start=False, stop=True).then_inc(kmp["mp"], 1)

            def latent_values(c):
                if c >= 2:
                    pe.wait_ge(vl["e"], b * 4 + c - 1)
                nc.tensor.matmul(bank(5 + c % 2), kgf[:, 128 * c:128 * c + 128], pwv("wv0"), start=True, stop=True).then_inc(vl["p"], 1)

            pe.wait_ge(kq["kgl"], b + 1)
            latent_values(0)
            latent_values(1)
            keys(0)
            pe_shift(pe, s, b)
            latent_values(2)
            latent_values(3)
            pe.wait_ge(Z["nmT"], s["zb"] + b + 1)
            pe.wait_ge(N["xl"], s["first"] + b + 1)

            def scores(n):
                h, c = divmod(n, 5)
                if n >= 2:
                    pe.wait_ge(s["ex"], b * 40 + n - 1)
                if c == 0:
                    pe.wait_ge(kmp["ml"], b * 8 + h + 1)
                if c < 4:
                    o, w = bank(3 + n % 2), 128
                    mh, ml = MLh[:, h % 2, 128 * c:128 * c + 128], MLl[:, h % 2, 128 * c:128 * c + 128]
                else:
                    o, w = bank(3 + n % 2, S, KC), KC
                    mh, ml = Mh[:, h, bass.ds(b * KC, KC)], Ml[:, h, bass.ds(b * KC, KC)]
                nc.tensor.matmul(o, mh, xh[:, b, :], start=True, stop=False)
                nc.tensor.matmul(o, mh, xl[:, b, :], start=False, stop=False)
                nc.tensor.matmul(o, ml, xh[:, b, :], start=False, stop=False)
                nc.tensor.matmul(o, sel0[:, h:h + 1].to_broadcast([128, w]), nmT[:], start=False, stop=True).then_inc(s["sT"], 1)

            def values(n):
                h, c = divmod(n, 5)
                pe.wait_ge(s["pl"], b * 40 + n + 1)
                if c == 0:
                    if h >= 2:
                        pe.wait_ge(s["on"], b * 8 + h - 1)
                    elif h == 0:
                        pe.wait_ge(vl["e"], b * 4 + 4)
                w = 128 if c < 4 else KC
                for q in range(QT):
                    vh, vlo = ([v[:, c, h, :] for v in (VLh, VLl)] if c < 4 else
                               [v[0:KC, bass.ds((b * 8 + h) * 65, 65)] for v in (Vh, Vl)])
                    o = bank(5 + h % 2, 65, off=65 * q)
                    ph, pl = Ph[n % 3][0:w, 128 * q:128 * q + 128], Pl[n % 3][0:w, 128 * q:128 * q + 128]
                    nc.tensor.matmul(o, ph, vh, start=(c == 0 and q == 0), stop=False, skip_group_check=True)
                    nc.tensor.matmul(o, ph, vlo, start=False, stop=False, skip_group_check=True)
                    last = nc.tensor.matmul(o, pl, vh, start=False, stop=c == 4, skip_group_check=True)
                last.then_inc(s["pv"], 1)

            scores(0)
            scores(1)
            for n in range(UNITS0):
                if n % 5 == 0 and n < 35:
                    keys(n // 5 + 1)
                if n < 38:
                    scores(n + 2)
                if n == 7 and nx:
                    pe_norm(pe, nx)
                if ahead(m, nx):
                    if n == 11:
                        pe_keys_max(pe, nx["b"], 0)
                    for j in MAX0.get(n, ()):
                        if j == 0:
                            pe.wait_ge(N["xh"], nx["n"] + 1)
                        pe.wait_ge(s["mx"], nx["b"] * STEPS0 + j)
                        pe_max0(pe, nx["b"], j)
                        if j % 4 == 1 and j < STEPS0 - 4:
                            pe_keys_max(pe, nx["b"], j // 4 + 1)
                values(n)
            if nx:
                pe.wait_ge(N["xt"], nx["n"] + 1)
            pe_out(pe, s, b, 4, "wo0", 8)

        def act_gate_keys(act, m):
            act.wait_ge(N["xt"], m["n"] + 1)
            nc.scalar.activation(kgf, xt[:], ACT.Copy, scale=col("kv_gate")).then_inc(kq["kg"], 1)
            act.wait_ge(kq["kg"], m["b"] + 1)
            nc.scalar.activation(kgh[:, m["b"], :], kgf, ACT.Copy).then_inc(kq["kgh"], 1)

        def act_first0(act):
            act_gate_keys(act, norm_of(0, 0))
            for h in range(8):
                act_keys_max(act, 0, h)

        def act_attn0(act, b, m, nx):
            s = L[0]

            def keys(h):
                act.wait_ge(kmp["mp"], b * 8 + h + 1)
                nc.scalar.activation(MLh[:, h % 2, :], bank(2), ACT.Copy).then_inc(kmp["mh"], 1)

            def latent_values(c):
                act.wait_ge(vl["p"], b * 4 + c + 1)
                nc.scalar.activation(VLh[:, c, :, 0:64], bank(5 + c % 2).rearrange("p (h d) -> p h d", d=64), ACT.Copy).then_inc(vl["h"], 1)

            nc.scalar.activation(negb[:], negk[:, bass.ds(b, 1)], ACT.Copy).then_inc(kq["nb"], 1)
            latent_values(0)
            latent_values(1)
            keys(0)
            act_shift(act, s, b)
            latent_values(2)
            latent_values(3)
            act.wait_ge(kq["nb"], b + 1)
            for n in range(UNITS0):
                act.wait_ge(s["sT"], b * 40 + n + 1)
                act_exp(act, s, b * 40, n, 128 if n % 5 < 4 else KC, None if n % 5 < 4 else negb[:])
                if n % 5 == 1 and n < 35:
                    keys(n // 5 + 1)
                if n == 8 and nx:
                    act_norm(act, nx)
                    if ahead(m, nx):
                        act_gate_keys(act, nx)
                if ahead(m, nx):
                    for h in keys0_at(n - 1):
                        act_keys_max(act, nx["b"], h)
            act_out(act, s, b, 4)

        def dve_attn0(dve, b, m, nx):
            s = L[0]

            def keys(h):
                dve.wait_ge(kmp["mh"], b * 8 + h + 1)
                nc.vector.tensor_tensor(MLl[:, h % 2, :], bank(2), MLh[:, h % 2, :], ALU.subtract).then_inc(kmp["ml"], 1)

            def latent_values(c):
                dve.wait_ge(vl["h"], b * 4 + c + 1)
                nc.vector.tensor_tensor(VLl[:, c, :, 0:64], bank(5 + c % 2).rearrange("p (h d) -> p h d", d=64),
                                        VLh[:, c, :, 0:64], ALU.subtract).then_inc(vl["e"], 1)
            if nx:
                dve_stats(dve, nx)
            latent_values(0)
            latent_values(1)
            keys(0)
            latent_values(2)
            latent_values(3)
            for n in range(UNITS0):
                if n == 1 and nx:
                    dve_scale(dve, nx)
                    if nx["double"]:
                        dve_stats(dve, nx, True)
                if n == 4 and nx and nx["double"]:
                    dve_scale(dve, nx, True)
                if ahead(m, nx):
                    for j in MAX0.get(n, ()):
                        dve_max0(dve, nx["b"], j)
                if n % 5 == 1 and n < 35:
                    keys(n // 5 + 1)
                if n % 5 == 1 and n > 5:
                    dve_head(dve, s, b, n // 5 - 1, 8, 5)
                if n in (9, 19, 29):
                    dve_weights(dve, b, n // 10)
            dve_head(dve, s, b, 7, 8, 5)
            if ahead(m, nx):
                dve_shift(dve, s, nx["b"], 8, STEPS0)
            dve.wait_ge(Z["op"], s["cb"] + b * 4 + 4)
            dve_res(dve, 0, s, b)

        def dve_weights(dve, b, k):
            n = b * STAGES_PER_BATCH + k
            dve.wait_ge(fsp["ld"], n * 16 + 16)
            h, l_ = [part[:, bass.ds(n * STAGE, STAGE)] for part in (fh, fl)]
            nc.vector.tensor_copy(h, stage).then_inc(fsp["hi"], 1)
            dve.wait_ge(fsp["hi"], n + 1)
            nc.vector.tensor_tensor(l_, stage, h, ALU.subtract).then_inc(fsp["lo"], 1)

        def pool_attn0(pool, b, m, nx):
            s = L[0]
            for n in range(UNITS0):
                pool_parts(pool, s, b * 40, n, 128 if n % 5 < 4 else KC)
                if n == 0 and nx:
                    pool_rstd(pool, nx)
                if n == 3 and nx and nx["double"]:
                    pool_rstd(pool, nx, True)
                if n == 10 and nx:
                    pool_low(pool, nx)
                    if ahead(m, nx):
                        pool_gate_keys(pool, nx)

        def pool_gate_keys(pool, m):
            pool.wait_ge(kq["kgh"], m["b"] + 1)
            nc.gpsimd.tensor_tensor(kgl[:, m["b"], :], kgf, kgh[:, m["b"], :], ALU.subtract).then_inc(kq["kgl"], 1)

        FN = "c lg sp h "
        F = [sems(f"f{i}_", FN + more) for i, more in enumerate(("lgs g", "yo gt xo aa", "lgs yo gt xo aa t1 t2 bb cc dd ee ff ys m7", "lgs"))]
        for i in range(4):
            L[i].update(first=2 * i * B, first2=B if i == 3 else 0, zb=i * B, cb=CB[i])
            F[i].update(first=(2 * i + 1) * B)
        EN = [8, 8, 8, 16]
        TOP = [2, 2, 2, 6]

        lg = sb("lg", [128, QT, 16])
        rsm = sb("rsm", [128, QT, 4])
        sc_ = sb("sc_", [128, QT, 16])
        sb_ = sb("sb_", [128, QT, 16])
        tri8 = sb("tri8", [128, 64])
        T1 = P4[:, 0, :].bitcast(BF16).rearrange("p (q e) -> p q e", q=QT)
        T2 = P4[:, 1, :].bitcast(BF16).rearrange("p (q e) -> p q e", q=QT)
        rank = sb("rank", [128, QT, 16])
        gates = sb("gates", [128, QT, 16])

        def fw(f, off, n, part=fh):
            return part[:, FOFF[f"f{f}"] + off:FOFF[f"f{f}"] + off + n]

        def pe_router(pe, f, b):
            s = F[f]
            E = EN[f]
            pe.wait_ge(N["xl"], s["first"] + b + 1)
            for q in range(QT):
                o = bank(7, E, off=E * q)
                a, c = xh[:, b, 128 * q:128 * q + 128], xl[:, b, 128 * q:128 * q + 128]
                nc.tensor.matmul(o, a, fw(f, 0, E), start=True, stop=False)
                nc.tensor.matmul(o, a, fw(f, 0, E, fl), start=False, stop=False)
                last = nc.tensor.matmul(o, c, fw(f, 0, E), start=False, stop=True)
            last.then_inc(s["lg"], 1)

        def chainer(eng, sem_, b, per):
            n = [0]

            def link(ins):
                n[0] += 1
                ins.then_inc(sem_, 1)
                eng.wait_ge(sem_, b * per + n[0])
            return link, n

        def dve_rank(dve, link, f, score):
            E = EN[f]
            E2 = E * E
            t1 = T1[:, :, 0:E2].rearrange("p q (i j) -> p q i j", i=E)
            t2 = T2[:, :, 0:E2].rearrange("p q (i j) -> p q i j", i=E)
            for q in range(QT):
                sj = score[:, q, :].unsqueeze(1).to_broadcast([128, E, E])
                si = score[:, q, :].unsqueeze(2).to_broadcast([128, E, E])
                nc.vector.tensor_tensor(t1[:, q], sj, si, ALU.is_gt)
                last = nc.vector.tensor_tensor(t2[:, q], sj, si, ALU.is_equal)
            link(last)
            trv = (tri[:, 0:256] if E == 16 else tri8[:]).unsqueeze(1).to_broadcast([128, QT, E2])
            link(nc.vector.tensor_tensor(T2[:, :, 0:E2], T2[:, :, 0:E2], trv, ALU.mult))
            link(nc.vector.tensor_tensor(T1[:, :, 0:E2], T1[:, :, 0:E2], T2[:, :, 0:E2], ALU.add))
            for q in range(QT):
                last = nc.vector.tensor_reduce(rank[:, q, 0:E], t1[:, q], AX, ALU.add)
            link(last)
            link(nc.vector.tensor_scalar(rank[:, :, 0:E], rank[:, :, 0:E], float(TOP[f]), None, ALU.is_lt))

        def dve_logits(dve, link, f, b, bias):
            s = F[f]
            E = EN[f]
            dve.wait_ge(s["lg"], b + 1)
            src = bank(7, QT * E).rearrange("p (q e) -> p q e", e=E)
            if bias:
                link(nc.vector.tensor_tensor(lg[:, :, 0:E], src, rowv(bias).unsqueeze(1).to_broadcast([128, QT, E]), ALU.add))
            else:
                link(nc.vector.tensor_copy(lg[:, :, 0:E], src))

        def dve_softmax(dve, link, f, b):
            s = F[f]
            E = EN[f]
            link(nc.vector.tensor_reduce(rsm[:, :, 0:1], lg[:, :, 0:E], AX, ALU.max))
            link(nc.vector.tensor_tensor(lg[:, :, 0:E], lg[:, :, 0:E], rsm[:, :, 0:1].to_broadcast([128, QT, E]), ALU.subtract))
            nc.vector.memset(rsm[:, :, 3:4], 0.0).then_inc(s["lgs"], 1)
            dve.wait_ge(s["sp"], b + 1)
            link(nc.vector.tensor_reduce(rsm[:, :, 1:2], sc_[:, :, 0:E], AX, ALU.add))
            link(nc.vector.reciprocal(rsm[:, :, 2:3], rsm[:, :, 1:2]))
            link(nc.vector.tensor_tensor(sc_[:, :, 0:E], sc_[:, :, 0:E], rsm[:, :, 2:3].to_broadcast([128, QT, E]), ALU.mult))

        def act_exp_logits(act, f, b):
            s = F[f]
            act.wait_ge(s["lgs"], b + 1)
            nc.scalar.activation(sc_[:, :, 0:EN[f]], lg[:, :, 0:EN[f]], ACT.Exp).then_inc(s["sp"], 1)

        ms = sb("ms", [128, B, QT, 8])
        route = sb("route", [128, QT, 8])
        msr = P4[:, 3, 0:128].rearrange("p (q r) -> p q r", q=QT)
        G0 = work[:, 0:4096].rearrange("p (b g s) -> p b g s", b=B, g=2)
        RT = work[0:32, 4096:4608]
        junk = work[0:32, 4608:5120]
        hs0 = work[:, 5120:6144].rearrange("p (g s) -> p g s", g=2)
        selb = P4[0:32, 2, 0:256].bitcast(BF16)
        self_ = aT[0:32, 0, :]
        th = sb("th", [32, 8])
        r0 = sems("r0_", "rt sel rte ch lp")
        r0d = sems("r0d_", "sb hs o")

        def pe_f0(pe):
            s = F[0]
            pe.wait_ge(fsp["lo"], B * STAGES_PER_BATCH + 1)
            def pe_batch(b, m, nx):
                pe_router(pe, 0, b)
                for g in range(2):
                    o = bank(g)
                    wh, wl = fw(0, 8 + 128 * g, 128), fw(0, 8 + 128 * g, 128, fl)
                    nc.tensor.matmul(o, wh, xh[:, b, :], start=True, stop=False)
                    nc.tensor.matmul(o, wh, xl[:, b, :], start=False, stop=False)
                    nc.tensor.matmul(o, wl, xh[:, b, :], start=False, stop=True).then_inc(s["h"], 1)
                if nx:
                    pe.wait_ge(s["lgs"], b + 1)
                    pe_norm(pe, nx)
            batches(pe, 1, pe_batch)
            for q in range(QT):
                pe.wait_ge(r0["rte"], q + 1)
                last = nc.tensor.transpose(bank(4, 128, 32, off=128 * q), msr[:, q, :], identf[:])
            last.then_inc(r0["rt"], 1)
            pe.wait_ge(s["g"], 8)
            pe_prep(pe, 1)
            pe.wait_ge(r0["sel"], 1)
            pe.wait_ge(m1["bqf"], 1)
            with pe.Fori(0, B) as b:
                for g in range(2):
                    nc.tensor.matmul(bank(g), expd[:, b, g, :], selb, start=True, stop=True).then_inc(r0d["sb"], 1)
                pe.wait_ge(r0d["hs"], 2 * b + 2)
                for q in range(QT):
                    o = bank(7, 128, off=128 * q)
                    for g in range(2):
                        nc.tensor.matmul(o, hs0[:, g, 128 * q:128 * q + 128], pwv("w2_0")[:, 128 * g:128 * g + 128],
                                         start=g == 0, stop=False)
                    last = nc.tensor.matmul(o, self_[:, 128 * q:128 * q + 128], b2s[:, b, :], start=False, stop=True)
                last.then_inc(r0d["o"], 1)
                pe.wait_ge(done, s["first"] + b + 1)


        def act_f0(act):
            s = F[0]
            def act_batch(b, m, nx):
                act_exp_logits(act, 0, b)
                for g in range(2):
                    act.wait_ge(s["h"], 2 * b + g + 1)
                    nc.scalar.activation(G0[:, b, g, :], bank(g), ACT.Gelu, bias=col("b1", g)).then_inc(s["g"], 1)
                if nx:
                    act_norm(act, nx)
            batches(act, 1, act_batch)
            act_prep(act, 1)

        def dve_f0(dve):
            s = F[0]
            def dve_batch(b, m, nx):
                PER = 12
                link, n = chainer(dve, s["c"], b, PER)
                if nx:
                    dve_stats(dve, nx)
                dve_logits(dve, link, 0, b, "w_gate_b")
                dve_softmax(dve, link, 0, b)
                if nx:
                    dve_scale(dve, nx)
                dve_rank(dve, link, 0, sc_[:, :, 0:8])
                link(nc.vector.tensor_tensor(ms[:, b, :, :], sc_[:, :, 0:8], rank[:, :, 0:8], ALU.mult))
                assert n[0] == PER, n[0]
            batches(dve, 1, dve_batch)
            k = [0]

            def lk(ins):
                k[0] += 1
                ins.then_inc(r0["ch"], 1)
                dve.wait_ge(r0["ch"], k[0])
            lk(nc.vector.tensor_tensor(route[:], ms[:, 0], ms[:, 1], ALU.add))
            lk(nc.vector.tensor_tensor(route[:], route[:], ms[:, 2], ALU.add))
            lk(nc.vector.tensor_tensor(route[:], route[:], ms[:, 3], ALU.add))
            lk(nc.vector.tensor_scalar(route[:], route[:], 1e-6, None, ALU.add))
            lk(nc.vector.reciprocal(route[:], route[:]))
            for q in range(QT):
                o = msr[:, q, :].rearrange("p (b e) -> p b e", b=B)
                last = nc.vector.tensor_tensor(o, ms[:, :, q, :], route[:, q, :].unsqueeze(1).to_broadcast([128, B, 8]), ALU.mult)
                lk(last)
                k[0] += 1
                nc.vector.tensor_scalar(o, o, float(B), None, ALU.mult).then_inc(r0["ch"], 1)
                dve.wait_ge(r0["ch"], k[0])
                nc.vector.memset(th[:, 7:8], 0.0).then_inc(r0["rte"], 1)
            dve.wait_ge(r0["rt"], 1)
            lk(nc.vector.tensor_copy(RT, bank(4, S, 32)))
            lk(nc.vector.memset(th[:], 0.0))
            thi = th[:, :].bitcast(I32)
            dve.wait_ge(in_c, 16 * 10)
            with dve.Fori(0, 32 // UNROLL) as i:
                for j in range(UNROLL):
                    n = (i * UNROLL + j) * 4
                    nc.vector.tensor_tensor(thi[:, 1:2], thi[:, 0:1], bits[:, bass.ds(i * UNROLL + j, 1)], ALU.bitwise_or).then_inc(r0["lp"], 1)
                    dve.wait_ge(r0["lp"], n + 1)
                    nc.vector.tensor_scalar(junk, RT, th[:, 1:2], None, ALU.is_ge, ALU.add, accum_out=th[:, 2:3]).then_inc(r0["lp"], 1)
                    dve.wait_ge(r0["lp"], n + 2)
                    nc.vector.tensor_scalar(th[:, 3:4], th[:, 2:3], float(KEEP), th[:, 1:2], ALU.is_ge, ALU.mult).then_inc(r0["lp"], 1)
                    dve.wait_ge(r0["lp"], n + 3)
                    nc.vector.tensor_tensor(th[:, 0:1], th[:, 0:1], th[:, 3:4], ALU.max).then_inc(r0["lp"], 1)
                    dve.wait_ge(r0["lp"], n + 4)
            lk(nc.vector.tensor_scalar(self_, RT, th[:, 0:1], None, ALU.is_gt, ALU.add, accum_out=th[:, 4:5]))
            lk(nc.vector.tensor_scalar(th[:, 5:6], th[:, 4:5], -1.0, float(KEEP), ALU.mult, ALU.add))
            lk(nc.vector.tensor_scalar(RT, RT, th[:, 0:1], None, ALU.is_equal))
            lk(nc.vector.tensor_tensor_scan(junk, ones[0:32, :], RT, 0.0, ALU.mult, ALU.add))
            lk(nc.vector.scalar_tensor_tensor(junk, junk, th[:, 5:6], RT, ALU.is_le, ALU.mult))
            lk(nc.vector.tensor_tensor(self_, self_, junk, ALU.add))
            nc.vector.tensor_copy(selb, self_).then_inc(r0["sel"], 1)
            dve.wait_ge(s["g"], 8)
            with dve.Fori(0, B) as b:
                for g in range(2):
                    dve.wait_ge(r0d["sb"], 2 * b + g + 1)
                    nc.vector.tensor_tensor(hs0[:, g, :], G0[:, b, g, :], bank(g), ALU.mult).then_inc(r0d["hs"], 1)
                dve.wait_ge(r0d["o"], b + 1)
                xb = x[:, b, :, :].rearrange("p q d -> p (q d)")
                nc.vector.tensor_tensor(xb, bank(7), xb, ALU.add).then_inc(done, 1)

        hb = [work[:, 512 * i:512 * i + 512] for i in range(12)]

        def pe_hidden_free(pe, s, b, U, nprod, k):
            u = (k - 4) // nprod
            if nprod == 2:
                pe.wait_ge(s["aa"], b * U + u + 1)
            elif k % 4 < 2:
                pe.wait_ge(s["gt"], (b * U + u) * 2 + k % 4 + 1)
            else:
                pe.wait_ge(s["t2"], (b * U + u) * 2 + k % 4 - 1)

        def pe_units(pe, f, b, units, nprod, wdown, whid, nx):
            s = F[f]
            U = len(units)

            def hidden(u):
                for i in range(nprod):
                    k = nprod * u + i
                    if k >= 4:
                        pe_hidden_free(pe, s, b, U, nprod, k)
                    wh, wl = whid(u, i, fh), whid(u, i, fl)
                    o = bank(k % 4)
                    nc.tensor.matmul(o, wh, xh[:, b, :], start=True, stop=False)
                    nc.tensor.matmul(o, wh, xl[:, b, :], start=False, stop=False)
                    nc.tensor.matmul(o, wl, xh[:, b, :], start=False, stop=True).then_inc(s["h"], 1)

            def down(u):
                pe.wait_ge(s["aa"], b * U + u + 1)
                if u >= 2:
                    pe.wait_ge(s["ys" if f == 2 else "yo"], b * U + u - 1)
                for q in range(QT):
                    last = nc.tensor.matmul(bank(5 + u % 2, 128, off=128 * q), hb[8 + u % 2][:, 128 * q:128 * q + 128],
                                            wdown(u), start=True, stop=True)
                last.then_inc(s["xo"], 1)
            hidden(0)
            for u in range(U):
                if u + 1 < U:
                    hidden(u + 1)
                down(u)
                if u == (5 if f == 2 else 4) and nx:
                    pe.wait_ge(s["sp"], b + 1)
                    pe_norm(pe, nx)

        def dve_gated_add(dve, s, b, U, u, g):
            dve.wait_ge(s["xo"], b * U + u + 1)
            if u:
                dve.wait_ge(s["yo"], b * U + u)
            for q in range(QT):
                o = bank(5 + u % 2, 128, off=128 * q)
                xq = x[:, b, q, :]
                if g is None:
                    last = nc.vector.tensor_tensor(xq, o, xq, ALU.add)
                else:
                    last = nc.vector.scalar_tensor_tensor(xq, o, g(q), xq, ALU.mult, ALU.add)
            last.then_inc(s["yo"], 1)

        U1 = [("s", c) for c in range(4)] + [("e", e) for e in range(8)]

        def whid1(u, i, part):
            kind, n = U1[u]
            off = 8 + (512 * i + 128 * n if kind == "s" else 1024 + 256 * n + 128 * i)
            return fw(1, off, 128, part)

        def wdown1(u):
            kind, n = U1[u]
            return pwv("sw3" if kind == "s" else "w3")[:, 128 * n:128 * n + 128]

        def pe_f1(pe):
            def pe_batch(b, m, nx):
                pe_router(pe, 1, b)
                pe_units(pe, 1, b, U1, 2, wdown1, whid1, nx)
            batches(pe, 3, pe_batch)

        def act_f1(act):
            s = F[1]
            U = len(U1)
            def act_batch(b, m, nx):
                act.wait_ge(s["lg"], b + 1)
                nc.scalar.activation(sc_[:, :, 0:8], bank(7, 32).rearrange("p (q e) -> p q e", e=8), ACT.Sigmoid).then_inc(s["sp"], 1)
                for u in range(U):
                    act.wait_ge(s["h"], (b * U + u) * 2 + 1)
                    if u >= 2:
                        act.wait_ge(s["aa"], b * U + u - 1)
                    nc.scalar.activation(hb[u % 2], bank((2 * u) % 4), ACT.Silu).then_inc(s["gt"], 1)
                    if u == 6 and nx:
                        act_norm(act, nx)
            batches(act, 3, act_batch)

        def dve_f1(dve):
            s = F[1]
            U = len(U1)
            def dve_batch(b, m, nx):
                PER = 7
                link, n = chainer(dve, s["c"], b, PER)
                dve.wait_ge(s["sp"], b + 1)
                link(nc.vector.tensor_tensor(sb_[:, :, 0:8], sc_[:, :, 0:8], rowv("expert_bias").unsqueeze(1).to_broadcast([128, QT, 8]), ALU.add))
                dve_rank(dve, link, 1, sb_[:, :, 0:8])
                link(nc.vector.tensor_tensor(gates[:, :, 0:8], sc_[:, :, 0:8], rank[:, :, 0:8], ALU.mult))
                assert n[0] == PER, n[0]

                def g_of(u):
                    kind, e = U1[u]
                    return None if kind == "s" else lambda q: gates[:, q, e:e + 1]
                for u in range(U):
                    dve.wait_ge(s["gt"], b * U + u + 1)
                    dve.wait_ge(s["h"], (b * U + u) * 2 + 2)
                    if u >= 2:
                        dve.wait_ge(s["xo"], b * U + u - 1)
                    nc.vector.tensor_tensor(hb[8 + u % 2], hb[u % 2], bank((2 * u + 1) % 4), ALU.mult).then_inc(s["aa"], 1)
                    if u:
                        dve_gated_add(dve, s, b, U, u - 1, g_of(u - 1))
                    if u == 1 and nx:
                        dve_stats(dve, nx)
                    if u == 2 and nx:
                        dve_scale(dve, nx)
                dve_gated_add(dve, s, b, U, U - 1, g_of(U - 1))
                dve.wait_ge(s["yo"], b * U + U)
                nc.vector.memset(rsm[:, :, 3:4], 0.0).then_inc(done, 1)
            batches(dve, 3, dve_batch)

        U2 = 9
        cwx = sb("cwx", [128, QT, 9])
        cwT = P4[0:9, 3, :]
        sig = [hb[6], hb[11]]
        both = [hb[7], hb[10]]
        scaled = [P4[:, 2, :], P4[:, 4, :]]

        def whid2(u, i, part):
            return fw(2, 8 + 512 * u + 128 * i, 128, part)

        def wdown2(u):
            return pwv("w2_2")[:, 128 * u:128 * u + 128]

        def pe_f2(pe):
            s = F[2]
            def pe_batch(b, m, nx):
                pe_router(pe, 2, b)
                pe_units(pe, 2, b, list(range(U2)), 4, wdown2, whid2, nx)
                if nx:
                    pe.wait_ge(N["xt"], nx["n"] + 1)
                pe.wait_ge(s["bb"], b + 1)
                for q in range(QT):
                    last = nc.tensor.transpose(bank(7, 128, 9, off=128 * q), cwx[:, q, :], identf[:])
                last.then_inc(s["cc"], 1)
                pe.wait_ge(s["dd"], b + 1)
                for q in range(QT):
                    last = nc.tensor.matmul(bank(4, 128, off=128 * q), cwT[:, 128 * q:128 * q + 128], b2c[:], start=True, stop=True)
                last.then_inc(s["ee"], 1)
            batches(pe, 5, pe_batch)

        def act_f2(act):
            s = F[2]
            def act_batch(b, m, nx):
                act_exp_logits(act, 2, b)

                def scale_output(u):
                    act.wait_ge(s["xo"], b * U2 + u + 1)
                    if u >= 2:
                        act.wait_ge(s["yo"], b * U2 + u - 1)
                    for q in range(QT):
                        last = nc.scalar.activation(scaled[u % 2][:, 128 * q:128 * q + 128], bank(5 + u % 2, 128, off=128 * q),
                                                    ACT.Copy, scale=cwx[:, q, u:u + 1])
                    last.then_inc(s["ys"], 1)
                for u in range(U2):
                    for i in range(2):
                        act.wait_ge(s["h"], (b * U2 + u) * 4 + i + 1)
                        if u >= 2:
                            act.wait_ge(s["t2"], (b * U2 + u - 1) * 2)
                        nc.scalar.activation(hb[2 * (u % 2) + i], bank(i), ACT.Identity, bias=col("hb", 4 * u + i)).then_inc(s["gt"], 1)
                    if u == 1:
                        act.wait_ge(s["bb"], b + 1)
                    if u:
                        scale_output(u - 1)
                    act.wait_ge(s["t1"], b * U2 + u + 1)
                    if u >= 2:
                        act.wait_ge(s["aa"], b * U2 + u - 1)
                    nc.scalar.activation(sig[u % 2], hb[4], ACT.Sigmoid, scale=1.702).then_inc(s["ff"], 1)
                    if u == 6 and nx:
                        act_norm(act, nx)
                scale_output(U2 - 1)
                act.wait_ge(s["cc"], b + 1)
                nc.scalar.activation(cwT, bank(7, S, 9), ACT.Copy).then_inc(s["dd"], 1)
            batches(act, 5, act_batch)

        def dve_f2(dve):
            s = F[2]
            def dve_batch(b, m, nx):
                PER = 13 + 9
                link, n = chainer(dve, s["c"], b, PER)
                dve_logits(dve, link, 2, b, None)
                dve_softmax(dve, link, 2, b)
                link(nc.vector.tensor_tensor(sb_[:, :, 0:8], sc_[:, :, 0:8], rowv("gate_b").unsqueeze(1).to_broadcast([128, QT, 8]), ALU.add))
                dve_rank(dve, link, 2, sb_[:, :, 0:8])
                link(nc.vector.tensor_tensor(cwx[:, :, 0:8], sc_[:, :, 0:8], rank[:, :, 0:8], ALU.mult))
                nc.vector.memset(cwx[:, :, 8:9], 1.0).then_inc(s["bb"], 1)

                for u in range(U2):
                    dve.wait_ge(s["gt"], (b * U2 + u) * 2 + 2)
                    if u:
                        dve.wait_ge(s["m7"], b * U2 + u)
                    for i in range(2):
                        dve.wait_ge(s["h"], (b * U2 + u) * 4 + 3 + i)
                        last = nc.vector.scalar_tensor_tensor(hb[4 + i], bank(2 + i), col("hb", 4 * u + 2 + i), hb[2 * (u % 2) + i],
                                                              ALU.add, ALU.mult).then_inc(s["t2"], 1)
                    dve.wait_ge(s["t2"], (b * U2 + u) * 2 + 2)
                    nc.vector.tensor_scalar(hb[4], hb[4], 7.0, None, ALU.min).then_inc(s["t1"], 1)
                    link(nc.vector.tensor_scalar(hb[5], hb[5], 7.0, -7.0, ALU.min, ALU.max))
                    if u >= 2:
                        dve.wait_ge(s["aa"], b * U2 + u - 1)
                    nc.vector.scalar_tensor_tensor(both[u % 2], hb[5], 1.0, hb[4], ALU.add, ALU.mult).then_inc(s["m7"], 1)
                    dve.wait_ge(s["ff"], b * U2 + u + 1)
                    if u == 1 and nx:
                        dve_stats(dve, nx)
                    if u == 2 and nx:
                        dve_scale(dve, nx)
                        if nx["double"]:
                            dve_stats(dve, nx, True)
                    if u == 4 and nx and nx["double"]:
                        dve_scale(dve, nx, True)
                assert n[0] == PER, n[0]
                dve.wait_ge(s["yo"], b * U2 + U2 - 1)
                dve.wait_ge(s["ys"], b * U2 + U2)
                xb = x[:, b, :, :].rearrange("p q d -> p (q d)")
                nc.vector.tensor_tensor(xb, scaled[(U2 - 1) % 2], xb, ALU.add).then_inc(s["yo"], 1)
                dve.wait_ge(s["yo"], b * U2 + U2)
                dve.wait_ge(s["ee"], b + 1)
                nc.vector.tensor_tensor(xb, bank(4), xb, ALU.add).then_inc(done, 1)
            batches(dve, 5, dve_batch)

        def pool_f2(pool, b, m, nx):
            s = F[2]

            def add_output(u):
                xb = x[:, b, :, :].rearrange("p q d -> p (q d)")
                nc.gpsimd.tensor_tensor(xb, scaled[u % 2], xb, ALU.add).then_inc(s["yo"], 1)
            for u in range(U2):
                pool.wait_ge(s["m7"], b * U2 + u + 1)
                pool.wait_ge(s["ff"], b * U2 + u + 1)
                if u >= 2:
                    pool.wait_ge(s["xo"], b * U2 + u - 1)
                    pool.wait_ge(s["yo"], b * U2 + u - 1)
                nc.gpsimd.tensor_tensor(hb[8 + u % 2], both[u % 2], sig[u % 2], ALU.mult).then_inc(s["aa"], 1)
                if u:
                    add_output(u - 1)
                if u == 1 and nx:
                    pool_rstd(pool, nx)
                if u == 3 and nx and nx["double"]:
                    pool_rstd(pool, nx, True)
                if u == 7 and nx:
                    pool_low(pool, nx)

        CHAIN3 = 21
        PER3 = CHAIN3 + 64

        def STEP3(n):
            return 2 * (n // 8) + n % 2, n % 8 // 2

        def pe_f3(pe):
            s = F[3]
            def pe_batch(b, m, nx):
                pe_router(pe, 3, b)
                pe.wait_ge(done, s["first"] + b)
                for n in range(16):
                    q, g = STEP3(n)
                    a, c = xh[:, b, 128 * q:128 * q + 128], xl[:, b, 128 * q:128 * q + 128]
                    if n >= 4:
                        pe.wait_ge(s["c"], b * PER3 + CHAIN3 + 8 * ((n - 4) // 2 + 1))
                    o = bank(n % 4)
                    nc.tensor.matmul(o, a, fw(3, 16 + 512 * g, 512), start=True, stop=False)
                    nc.tensor.matmul(o, a, fw(3, 16 + 512 * g, 512, fl), start=False, stop=False)
                    nc.tensor.matmul(o, c, fw(3, 16 + 512 * g, 512), start=False, stop=True).then_inc(s["h"], 1)
                    if n == 9 and nx:
                        pe.wait_ge(s["lgs"], b + 1)
                        pe_norm(pe, nx)
            batches(pe, 7, pe_batch)

        def act_f3(act):
            def act_batch(b, m, nx):
                act_exp_logits(act, 3, b)
                if nx:
                    act_norm(act, nx)
            batches(act, 7, act_batch)

        def dve_f3(dve):
            s = F[3]
            def dve_batch(b, m, nx):
                link, n = chainer(dve, s["c"], b, PER3)
                dve_logits(dve, link, 3, b, "router_b")
                dve_softmax(dve, link, 3, b)
                dve_rank(dve, link, 3, sc_[:])
                link(nc.vector.tensor_tensor(gates[:], sc_[:], rank[:], ALU.mult))
                sm = rsm[:, :, 0:1]
                link(nc.vector.tensor_reduce(sm, gates[:], AX, ALU.add))
                link(nc.vector.tensor_scalar(sm, sm, 1e-10, None, ALU.add))
                link(nc.vector.reciprocal(sm, sm))
                link(nc.vector.tensor_tensor(gates[:], gates[:], sm.to_broadcast([128, QT, 16]), ALU.mult))
                link(nc.vector.tensor_reduce(rsm[:, :, 1:2], gates[:], AX, ALU.add))
                link(nc.vector.tensor_scalar(rsm[:, :, 2:3], rsm[:, :, 1:2], 1e-10, None, ALU.max))
                link(nc.vector.reciprocal(rsm[:, :, 2:3], rsm[:, :, 2:3]))
                link(nc.vector.tensor_tensor(gates[:], gates[:], rsm[:, :, 2:3].to_broadcast([128, QT, 16]), ALU.mult))
                link(nc.vector.tensor_scalar(rsm[:, :, 1:2], rsm[:, :, 1:2], 1e-10, None, ALU.mult))
                assert n[0] == CHAIN3, n[0]
                k = 0
                for p in range(8):
                    if p == 4 and nx:
                        dve_stats(dve, nx)
                        dve_scale(dve, nx)
                    for i in range(4):
                        for j in (2 * p, 2 * p + 1):
                            q, g = STEP3(j)
                            e = 4 * g + i
                            if i == 0:
                                dve.wait_ge(s["h"], b * 16 + j + 1)
                            if k >= 2:
                                dve.wait_ge(s["c"], b * PER3 + CHAIN3 + k - 1)
                            nc.vector.scalar_tensor_tensor(x[:, b, q, :], bank(j % 4, 128, off=128 * i), gates[:, q, e:e + 1],
                                                           x[:, b, q, :], ALU.mult, ALU.add).then_inc(s["c"], 1)
                            k += 1
                dve.wait_ge(s["c"], b * PER3 + PER3)
                nc.vector.tensor_tensor(x[:, b, :, :], x[:, b, :, :], rsm[:, :, 1:2].to_broadcast([128, QT, D]), ALU.add).then_inc(done, 1)
            batches(dve, 7, dve_batch)


        @block.sync
        def _(sp):
            sp.dma_start(x[:], A["x"]).then_inc(in_x, 16)
            sp.dma_start(ctxT[:], A["ctxT"]).then_inc(in_c, 16)
            sp.dma_start(crow[:], A["ctxr"]).then_inc(in_c, 16)
            sp.dma_start(cols[:], A["cols"]).then_inc(in_c, 16)
            sp.dma_start(rowc[:], A["rowc"]).then_inc(in_c, 16)
            sp.dma_start(bkq[:], A["bkq"]).then_inc(in_c, 16)
            sp.dma_start(b2c[:], A["b2c"]).then_inc(in_c, 16)
            sp.dma_start(b2s[:], A["b2s"]).then_inc(in_c, 16)
            sp.dma_start(tri[:], A["tri"]).then_inc(in_c, 16)
            sp.dma_start(tri8[:], A["tri8"]).then_inc(in_c, 16)
            sp.dma_start(bits[:], A["bits"]).then_inc(in_c, 16)
            sp.dma_start(mk8[:], A["mk8"]).then_inc(in_mask, 16)
            sp.dma_start(mr8[:], A["mr8"]).then_inc(in_mask, 16)
            sp.dma_start(identf[:], A["identf"]).then_inc(in_w, 16)
            sp.dma_start(identb[:], A["identb"]).then_inc(in_w, 16)
            sp.dma_start(sel0[:], A["sel0"]).then_inc(in_w, 16)
            sp.dma_start(expd[:], A["expd"]).then_inc(in_w, 16)
            sp.dma_start(delta[:], A["delta"]).then_inc(in_w, 16)
            sp_prep(sp, 0)
            sp.dma_start(pw[:], A["pw"]).then_inc(in_pw, 16)
            with sp.Fori(0, B) as b:
                for k in range(STAGES_PER_BATCH):
                    n = b * STAGES_PER_BATCH + k
                    sp.wait_ge(fsp["lo"], n + 1)
                    sp.dma_start(stage, A["fw"][:, bass.ds(n * STAGE, STAGE)]).then_inc(fsp["ld"], 16)
            for l in range(1, 4):
                sp_prep(sp, l)
                if l == 1:
                    sp.wait_ge(R["vm"], 2)
                    sp.dma_start(negm, A["maskT"]).then_inc(m1["in_"], 16)
            sp.wait_ge(done, B * len(order))
            sp.dma_start(out, x[:]).then_inc(out_s, 16)
            sp.wait_ge(out_s, 16)

        @block.gpsimd
        def _(pool):
            nc.gpsimd.memset(mhalf[:], -0.5).then_inc(const, 1)
            nc.gpsimd.memset(epst[:], LN_EPS).then_inc(const, 1)
            nc.gpsimd.memset(ones[:], 1.0).then_inc(const, 1)
            nc.gpsimd.memset(nm[:], 0.0).then_inc(const, 1)
            nc.gpsimd.memset(nmT[:], 0.0).then_inc(const, 1)
            nc.gpsimd.memset(stage, 0.0).then_inc(fsp["lo"], 1)
            pool.wait_ge(const, 5)
            pool.wait_ge(c0["var"], 1)
            nc.gpsimd.tensor_scalar(cve[:], cmv[:, :, 1], LN_EPS, 1.0, ALU.add, ALU.mult).then_inc(c0["ep"], 1)
            pool.wait_ge(c0["ep"], 1)
            nc.gpsimd.tensor_tensor(crs[:], cve[:], mhalf[0:KC, :], ALU.pow).then_inc(c0["rstd"], 1)
            pool.wait_ge(c0["xh"], 2)
            nc.gpsimd.tensor_tensor(cxl[:], cxf[:], cxh[:], ALU.subtract).then_inc(c0["xl"], 1)
            nc.gpsimd.tensor_tensor(cl[:], ctxT[:], ch[:], ALU.subtract).then_inc(c0["xl"], 1)
            pool_prep(pool, 0)
            for k, i in order:
                if k == "a" and i > 1:
                    pool_prep(pool, i)
                if k == "a" and i < 2:
                    pool_norm(pool, norm_of(2 * i, 0, first=i == 0))
                if k == "a" and i == 0:
                    pool_gate_keys(pool, norm_of(0, 0))
                if k == "a":
                    batches(pool, 2 * i, lambda b, m, nx: pool_attn0(pool, b, m, nx) if i == 0 else pool_attn(pool, i, b, m, nx))
                else:
                    batches(pool, 2 * i + 1, lambda b, m, nx: pool_f2(pool, b, m, nx) if i == 2 else pool_norm(pool, nx) if nx else None)
                    if i == 0:
                        pool_prep(pool, 1)
                        pool_prep1(pool)

        @block.scalar
        def _(act):
            act.wait_ge(in_c, 16 * 10)
            act.wait_ge(c0["neg"], 1)
            nc.scalar.activation(tg[:], col("gate"), ACT.Tanh).then_inc(tgs, 1)
            nc.scalar.activation(ch[:], ctxT[:], ACT.Copy).then_inc(c0["xh"], 1)
            act.wait_ge(c0["tp"], 1)
            nc.scalar.activation(cxf[:], bank(7, KA), ACT.Identity, bias=col("beta_media"), scale=col("gamma_media")).then_inc(c0["xt"], 1)
            act.wait_ge(c0["xt"], 1)
            nc.scalar.activation(cxh[:], cxf[:], ACT.Copy).then_inc(c0["xh"], 1)
            act_prep(act, 0)
            for k, i in order:
                if k == "a":
                    if i > 1:
                        act_prep(act, i)
                    if i < 2:
                        act_norm(act, norm_of(2 * i, 0, first=i == 0))
                    if i == 0:
                        act_first0(act)
                    batches(act, 2 * i, lambda b, m, nx: act_attn0(act, b, m, nx) if i == 0 else act_attn(act, i, b, m, nx))
                else:
                    (act_f0, act_f1, act_f2, act_f3)[i](act)

        @block.vector
        def _(dve):
            dve.wait_ge(in_c, 16 * 10)
            for b in range(B):
                last = nc.vector.bn_stats(cst[:, b, :], crow[:, b, :])
            last.then_inc(c0["st"], 1)
            dve.wait_ge(c0["st"], 1)
            for b in range(B):
                last = nc.vector.bn_aggr(cmv[:, b, :], cst[:, b, :])
            last.then_inc(c0["var"], 1)
            dve.wait_ge(in_mask, 32)
            nc.vector.tensor_scalar(negk[:], mk8[:], NEG_INF, None, ALU.mult)
            nc.vector.tensor_scalar(negr[:], mr8[:], NEG_INF, None, ALU.mult).then_inc(c0["neg"], 1)
            dve.wait_ge(c0["rstd"], 1)
            for b in range(B):
                last = nc.vector.tensor_scalar(crow[:, b, :], crow[:, b, :], cmv[:, b, 0:1], crs[:, b:b + 1], ALU.subtract, ALU.mult)
            last.then_inc(c0["xn"], 1)
            dve.wait_ge(tgs, 1)
            nc.vector.tensor_scalar(btg[:], rowv("b_out"), tg[:, 0:1], None, ALU.mult).then_inc(tgs, 1)
            dve_prep(dve, 0)
            for k, i in order:
                if k == "a":
                    if i > 1:
                        dve_prep(dve, i)
                    if i < 2:
                        dve_norm(dve, norm_of(2 * i, 0, first=i == 0))
                    for j in range(12 if i else STEPS0):
                        dve_max(dve, i, 0, j) if i else dve_max0(dve, 0, j)
                    dve_shift(dve, L[i], 0, NH[i], 12 if i else STEPS0)
                    batches(dve, 2 * i, lambda b, m, nx: dve_attn0(dve, b, m, nx) if i == 0 else dve_attn(dve, i, b, m, nx))
                else:
                    (dve_f0, dve_f1, dve_f2, dve_f3)[i](dve)

        @block.tensor
        def _(pe):
            pe.wait_ge(in_w, 16 * 5)
            pe.wait_ge(const, 5)
            pe.wait_ge(c0["xn"], 1)
            for b in range(B):
                last = nc.tensor.transpose(bank(7, KC, off=KC * b), crow[:, b, :], identf[0:KC, 0:KC])
            last.then_inc(c0["tp"], 1)
            pe_prep(pe, 0)
            for k, i in order:
                if k == "a":
                    if i > 1:
                        pe_prep(pe, i)
                    if i == 1:
                        pe.wait_ge(m1["chain"], 7)
                    if i < 2:
                        pe_norm(pe, norm_of(2 * i, 0, first=i == 0))
                    pe.wait_ge(R["ml"], HB[i] + NH[i])
                    if i == 0:
                        pe_first0(pe)
                    else:
                        for j in range(12):
                            pe_max(pe, i, 0, j)
                    batches(pe, 2 * i, lambda b, m, nx: pe_attn0(pe, b, m, nx) if i == 0 else pe_attn(pe, i, b, m, nx))
                else:
                    pe.wait_ge(done, F[i]["first"])
                    (pe_f0, pe_f1, pe_f2, pe_f3)[i](pe)


def layout(inputs):
    import numpy as np
    bf16 = mybir.dt.np(mybir.dt.bfloat16)
    I = {k: np.asarray(v) for k, v in inputs.items()}
    f = np.float32
    t = {}
    t["x"] = I["x"].reshape(B, QT, 128, D).transpose(2, 0, 1, 3)
    c = I["ctx_1024"]
    t["ctxT"] = c.reshape(KA, D).T
    t["ctxr"] = c.transpose(1, 0, 2)
    mask = I["mask_BxS2_bk0"]
    t["mk8"] = mask.T
    t["mr8"] = mask.reshape(1, KA)
    t["maskT"] = I["mask_1x1xSxS2_fk1"].reshape(S, KC).T

    def whole(v):
        return np.broadcast_to(v.reshape(1, -1), (128, v.size))

    def hidden2(v, sv):
        w = np.concatenate([v, sv[None]], 0)
        return w[:, 0::2].T, w[:, 1::2].T
    b1e, b1o = hidden2(I["L2_ffn_b1"], I["L2_ffn_sb1"])
    b3e, b3o = hidden2(I["L2_ffn_b3"], I["L2_ffn_sb3"])
    hb = np.stack([b1e, b1o, b3e, b3o], 2).reshape(128, 36)
    t["cols"] = np.concatenate([I["L0_xattn_gamma_media"][:, None], I["L0_xattn_beta_media"][:, None],
                                I["L0_xattn_gamma_lat"][:, None], I["L0_xattn_beta_lat"][:, None],
                                I["L3_xattn_ln_gamma"][:, None], I["L3_xattn_ln_beta"][:, None],
                                whole(I["L0_xattn_kv_gate"]), whole(I["L3_xattn_gate"]),
                                I["L0_ffn_b1"].reshape(2, 128).T, hb], 1)
    t["rowc"] = np.concatenate([whole(I[n]) for n in ("L0_ffn_w_gate_b", "L1_ffn_expert_bias", "L2_ffn_gate_b", "L3_ffn_router_b",
                                                      "L1_xattn_bo", "L3_xattn_b_out", "L1_xattn_bv")], 1)
    bk, bq = I["L1_xattn_bk"].reshape(16, 8), I["L1_xattn_bq"].reshape(16, 8)
    t["bkq"] = np.stack([bk.T, bq.T], 1)
    t["b2c"] = np.concatenate([I["L2_ffn_b2"], I["L2_ffn_sb2"][None]], 0)
    z = np.zeros((B, 8, B, D), f)
    for b in range(B):
        z[b, :, b, :] = I["L0_ffn_b2"]
    t["b2s"] = z.reshape(32, B, D)

    def heads(wq, wk, n):
        return np.stack([wk.reshape(D, n, -1).transpose(2, 1, 0), wq.reshape(D, n, -1).transpose(2, 1, 0)], 1)
    wk3, wv3 = I["L3_xattn_w_kv"][:, :1024], I["L3_xattn_w_kv"][:, 1024:]
    t["g0"] = heads(I["L0_xattn_Wq"], I["L0_xattn_Wk"], 8)
    t["g1"] = heads(I["L1_xattn_Wq"].T, I["L1_xattn_Wk"].T, 16)
    t["g2"] = heads(I["L2_xattn_Wq"].T, I["L2_xattn_Wk"].T, 16)
    t["g3"] = heads(I["L3_xattn_w_q"], wk3, 16)

    def chunks(w):
        return w.reshape(-1, 128, w.shape[1]).transpose(1, 0, 2).reshape(128, -1)
    w22 = np.concatenate([I["L2_ffn_w2"], I["L2_ffn_sw2"][None]], 0)
    t["pw"] = np.concatenate([I["L0_xattn_Wv"], I["L1_xattn_Wv"].T, I["L2_xattn_Wv"].T, wv3,
                              chunks(I["L0_xattn_Wout"]), I["L1_xattn_Wo"].T, I["L2_xattn_Wo"].T, chunks(I["L3_xattn_w_out"]),
                              chunks(I["L0_ffn_W2"].reshape(256, D)), chunks(I["L1_ffn_shared_w3"].T),
                              I["L1_ffn_w3"].transpose(2, 0, 1).reshape(128, -1), w22.transpose(2, 0, 1).reshape(128, -1)], 1)
    w1 = np.concatenate([I["L2_ffn_w1"], I["L2_ffn_sw1"][None]], 0)
    w3 = np.concatenate([I["L2_ffn_w3"], I["L2_ffn_sw3"][None]], 0)
    f2 = np.stack([w1[:, 0::2], w1[:, 1::2], w3[:, 0::2], w3[:, 1::2]], 1)
    t["fw"] = np.concatenate([I["L0_ffn_w_gate_w"], I["L0_ffn_W1"].transpose(1, 0, 2).reshape(D, 256),
                              I["L1_ffn_router_w"].T, I["L1_ffn_shared_w1"].T, I["L1_ffn_shared_w2"].T,
                              I["L1_ffn_w12"].transpose(2, 0, 1).reshape(D, -1),
                              I["L2_ffn_gate_w"].T, f2.transpose(3, 0, 1, 2).reshape(D, -1),
                              I["L3_ffn_router_w"].T, I["L3_ffn_expert_w"].transpose(1, 0, 2).reshape(D, -1),
                              np.zeros((D, B * STAGES_PER_BATCH * STAGE - NFW), f)], 1)
    t["identf"] = np.eye(128, dtype=f)
    t["identb"] = np.eye(128, dtype=bf16)
    s0 = np.zeros((128, 16), bf16)
    for h in range(16):
        for p in (0, 32, 64):
            s0[p + h, h] = -1.0
    t["sel0"] = s0
    ex = np.zeros((B, 8, B, 2, 128), bf16)
    for b in range(B):
        for e in range(8):
            ex[b, e, b, e // 4, 32 * (e % 4):32 * (e % 4) + 32] = 1.0
    t["expd"] = ex.reshape(32, B, 2, 128)
    t["delta"] = np.eye(16, dtype=f)
    t["tri"] = np.broadcast_to(np.tril(np.ones((16, 16), f), -1).reshape(1, 256), (128, 256))
    t["tri8"] = np.broadcast_to(np.tril(np.ones((8, 8), f), -1).reshape(1, 64), (128, 64))
    bits = np.zeros((32, 32), np.int32)
    for i in range(BITS):
        bits[:, i] = 1 << (BITS - 1 - i)
    t["bits"] = bits
    return {k: np.ascontiguousarray(v) for k, v in t.items()}


def kernel(**inputs):
    import numpy as np
    import concourse.bacc as bacc
    from concourse.bass_utils import run_bass_kernel_spmd

    nc = bacc.Bacc("TRN2", target_bir_lowering=False, num_devices=1)
    arrays = layout(inputs)
    feeds, aps = {}, {}
    for name, a in arrays.items():
        feeds[f"in_{name}"] = a
        aps[name] = nc.dram_tensor(f"in_{name}", a.shape, mybir.dt.from_np(a.dtype), kind="ExternalInput").ap()
    out = nc.dram_tensor("out_x", (128, B, QT, D), F32, kind="ExternalOutput").ap()
    build(nc, aps, out)
    r = run_bass_kernel_spmd(nc, [feeds], core_ids=[0])
    return np.ascontiguousarray(r.results[0]["out_x"].transpose(1, 2, 0, 3)).reshape(B, S, D)
```
